# Optimizing a Trainium2 kernel written in Bass

```python
import numpy as np
import jax
import jax.numpy as jnp

def _softmax(x, axis=-1):
    return jax.nn.softmax(x, axis=axis)

def _gelu(x):
    return jax.nn.gelu(x, approximate=True)

def _silu(x):
    return jax.nn.silu(x)

def _sigmoid(x):
    return jax.nn.sigmoid(x)

def _layernorm(x, axis=-1, eps=1e-05):
    m = jnp.mean(x, axis=axis, keepdims=True)
    v = jnp.var(x, axis=axis, keepdims=True)
    return (x - m) / jnp.sqrt(v + eps)

def _scatter_add(tgt, idx, src, axis=0):
    return tgt.at[idx].add(src)

def _segment_sum(src, seg, n):
    return jax.ops.segment_sum(src, seg, n)
kernel_name = 'mk_gps_d1_gnn_r32_633457'

def setup_inputs(seed: int=0):
    np.random.seed(seed)
    _w = jnp.asarray

    def _rec_inputs():
        import jax
        import jax.numpy as jnp
        _gk = jax.random.key(seed)
        x = -0.0003713 + 1 * jax.random.normal(jax.random.fold_in(_gk, 1), (3125, 256), jnp.float32)
        src = jax.random.randint(jax.random.fold_in(_gk, 2), (50000,), 0, 3125, jnp.int32)
        dst = jnp.minimum((3125 * jax.random.uniform(jax.random.fold_in(_gk, 3), (50000,)) ** 2.0).astype(jnp.int32), 99999)
        _o = jnp.argsort(dst, stable=True)
        src = src[_o]
        dst = dst[_o]
        return (x, src, dst)
    x, src, dst = _rec_inputs()

    def _L0_gnn_setup():
        import jax, jax.numpy as jnp
        import numpy as np
        N_NODES = 50000
        N_EDGES = 25000
        IN_DIM = 256
        HEADS = 4
        HEAD_DIM = 64
        NEG_SLOPE = 0.2
        key = jax.random.key(seed)
        k1, k2, k3, k4, k5 = jax.random.split(key, 5)
        x = jax.random.normal(k1, (N_NODES, IN_DIM), dtype=jnp.float32)
        edge_index = jax.random.randint(k2, (2, N_EDGES), 0, N_NODES, dtype=jnp.int64)
        W = jax.random.normal(k3, (IN_DIM, HEADS * HEAD_DIM), dtype=jnp.float32) * (1.0 / np.sqrt(IN_DIM))
        att_src = jax.random.normal(k4, (HEADS, HEAD_DIM), dtype=jnp.float32) * (1.0 / np.sqrt(HEAD_DIM))
        att_dst = jax.random.normal(k5, (HEADS, HEAD_DIM), dtype=jnp.float32) * (1.0 / np.sqrt(HEAD_DIM))
        bias = jnp.zeros((HEADS * HEAD_DIM,), dtype=jnp.float32)
        return {'x': x, 'edge_index': edge_index, 'W': W, 'att_src': att_src, 'att_dst': att_dst, 'bias': bias}
    _L0_gnn_all = _L0_gnn_setup()
    _L0_gnn_in = {k: v for k, v in _L0_gnn_all.items() if k in ('W', 'att_src', 'att_dst', 'bias')}
    del _L0_gnn_all

    def _L0_mix_setup():
        import jax, jax.numpy as jnp
        import numpy as np
        A, Bc, Cc = (0.5, 1.0, 1.0)
        H = 8
        EPS = 1e-12

        def _normalize(t):
            n = jnp.linalg.norm(t, axis=-1, keepdims=True)
            return t / jnp.maximum(n, EPS)
        key = jax.random.key(seed)
        ks = jax.random.split(key, 5)
        B, N, C = (8, 64, 256)
        D = C // H
        x = jax.random.normal(ks[0], (B, N, C), dtype=jnp.float32)
        Wqkv = jax.random.normal(ks[1], (3 * H * D, C), dtype=jnp.float32) * 0.02
        bqkv = jnp.zeros((3 * H * D,), dtype=jnp.float32)
        Wproj = jax.random.normal(ks[2], (C, H * D), dtype=jnp.float32) * 0.02
        bproj = jnp.zeros((C,), dtype=jnp.float32)
        temperature = jnp.ones((1, H, 1, 1), dtype=jnp.float32)
        return {'x': x, 'Wqkv': Wqkv, 'bqkv': bqkv, 'Wproj': Wproj, 'bproj': bproj, 'temperature': temperature}
    _L0_mix_all = _L0_mix_setup()
    _L0_mix_in = {k: v for k, v in _L0_mix_all.items() if k in ('Wqkv', 'bqkv', 'Wproj', 'bproj', 'temperature')}
    del _L0_mix_all

    def _L0_ffn_setup():
        import jax, jax.numpy as jnp
        import numpy as np
        B, S, D, H, E, K = (8, 256, 256, 1024, 8, 2)
        key = jax.random.key(seed)
        ks = jax.random.split(key, 7)
        s_in = 1.0 / np.sqrt(D)
        s_hid = 1.0 / np.sqrt(H)
        return {'x': jax.random.normal(ks[0], (B, S, D), dtype=jnp.float32), 'Wg': jax.random.uniform(ks[1], (E, D), jnp.float32, -s_in, s_in), 'bg': jax.random.uniform(ks[2], (E,), jnp.float32, -s_in, s_in), 'W1': jax.random.uniform(ks[3], (E, H, D), jnp.float32, -s_in, s_in), 'b1': jax.random.uniform(ks[4], (E, H), jnp.float32, -s_in, s_in), 'W2': jax.random.uniform(ks[5], (E, D, H), jnp.float32, -s_hid, s_hid), 'b2': jax.random.uniform(ks[6], (E, D), jnp.float32, -s_hid, s_hid)}
    _L0_ffn_all = _L0_ffn_setup()
    _L0_ffn_in = {k: v for k, v in _L0_ffn_all.items() if k in ('Wg', 'bg', 'W1', 'b1', 'W2', 'b2')}
    del _L0_ffn_all
    return {'x': x, 'src': src, 'dst': dst, 'L0_gnn_W': _L0_gnn_in['W'], 'L0_gnn_att_src': _L0_gnn_in['att_src'], 'L0_gnn_att_dst': _L0_gnn_in['att_dst'], 'L0_gnn_bias': _L0_gnn_in['bias'], 'L0_mix_Wqkv': _L0_mix_in['Wqkv'], 'L0_mix_bqkv': _L0_mix_in['bqkv'], 'L0_mix_Wproj': _L0_mix_in['Wproj'], 'L0_mix_bproj': _L0_mix_in['bproj'], 'L0_mix_temperature': _L0_mix_in['temperature'], 'L0_ffn_Wg': _L0_ffn_in['Wg'], 'L0_ffn_bg': _L0_ffn_in['bg'], 'L0_ffn_W1': _L0_ffn_in['W1'], 'L0_ffn_b1': _L0_ffn_in['b1'], 'L0_ffn_W2': _L0_ffn_in['W2'], 'L0_ffn_b2': _L0_ffn_in['b2']}

def reference(x, src, dst, L0_gnn_W, L0_gnn_att_src, L0_gnn_att_dst, L0_gnn_bias, L0_mix_Wqkv, L0_mix_bqkv, L0_mix_Wproj, L0_mix_bproj, L0_mix_temperature, L0_ffn_Wg, L0_ffn_bg, L0_ffn_W1, L0_ffn_b1, L0_ffn_W2, L0_ffn_b2):
    import jax
    import jax.numpy as jnp

    def _L0_gnn_ref(x, edge_index, W, att_src, att_dst, bias):
        import jax, jax.numpy as jnp
        import numpy as np
        N_NODES = 50000
        N_EDGES = 25000
        IN_DIM = 256
        HEADS = 4
        HEAD_DIM = 64
        NEG_SLOPE = 0.2
        N = x.shape[0]
        loops = jnp.arange(N, dtype=edge_index.dtype)
        src = jnp.concatenate([edge_index[0], loops])
        dst = jnp.concatenate([edge_index[1], loops])
        h = (x @ W).reshape(N, HEADS, HEAD_DIM)
        a_src = jnp.einsum('nhd,hd->nh', h, att_src)
        a_dst = jnp.einsum('nhd,hd->nh', h, att_dst)
        e = a_src[src] + a_dst[dst]
        e = jax.nn.leaky_relu(e, NEG_SLOPE)
        m = jax.ops.segment_max(e, dst, num_segments=N)
        e = jnp.exp(e - m[dst])
        denom = jax.ops.segment_sum(e, dst, num_segments=N)
        alpha = e / denom[dst]
        msg = alpha[:, :, None] * h[src]
        out = jax.ops.segment_sum(msg, dst, num_segments=N)
        return out.reshape(N, HEADS * HEAD_DIM) + bias

    def _L0_mix_ref(x, Wqkv, bqkv, Wproj, bproj, temperature):
        import jax, jax.numpy as jnp
        import numpy as np
        A, Bc, Cc = (0.5, 1.0, 1.0)
        H = 8
        EPS = 1e-12

        def _normalize(t):
            n = jnp.linalg.norm(t, axis=-1, keepdims=True)
            return t / jnp.maximum(n, EPS)
        B, N, C = x.shape
        D = C // H
        scale = float(D) ** 0.25
        qkv = (x @ Wqkv.T + bqkv).reshape(B, N, 3, H, D)
        qkv = jnp.transpose(qkv, (2, 0, 3, 1, 4))
        q, k, v = (qkv[0], qkv[1], qkv[2])
        q = q * scale
        v1 = jnp.concatenate([jnp.ones((B, H, N, 1), dtype=v.dtype), v], axis=-1)
        qn = _normalize(q) * (scale * temperature)
        kn = _normalize(k) * scale
        vN = v1 / N
        kv_mod = jnp.einsum('bhni,bhnj,bhne->bhije', kn, kn, vN)
        kv = jnp.einsum('bhnd,bhne->bhde', kn, vN)
        vsum = jnp.sum(vN, axis=-2)[:, :, None, :]
        y = A * jnp.einsum('bhni,bhnj,bhije->bhne', qn, qn, kv_mod) + scale ** 2 * Bc * jnp.einsum('bhnd,bhde->bhne', qn, kv) + scale ** 4 * Cc * vsum
        y_norm, y = (y[..., :1], y[..., 1:])
        y = y / y_norm
        out = jnp.transpose(y, (0, 2, 1, 3)).reshape(B, N, H * D)
        return out @ Wproj.T + bproj

    def _L0_ffn_ref(x, Wg, bg, W1, b1, W2, b2):
        import jax, jax.numpy as jnp
        import numpy as np
        B, S, D, H, E, K = (8, 256, 256, 1024, 8, 2)
        gate_scores = jnp.einsum('bsd,ed->bse', x, Wg) + bg
        topk_scores, topk_idx = jax.lax.top_k(gate_scores, K)
        topk_probs = jax.nn.softmax(topk_scores, axis=-1)
        combine = jnp.sum(topk_probs[..., None] * jax.nn.one_hot(topk_idx, E, dtype=x.dtype), axis=-2)
        out = jnp.zeros_like(x)
        for e in range(E):
            h = jax.nn.relu(jnp.einsum('bsd,hd->bsh', x, W1[e]) + b1[e])
            y = jnp.einsum('bsh,dh->bsd', h, W2[e]) + b2[e]
            out = out + combine[..., e:e + 1] * y
        return out
    edge_index = jnp.stack([src, dst])
    xn = _layernorm(x, axis=-1)
    x = x + _L0_gnn_ref(xn, edge_index, L0_gnn_W, L0_gnn_att_src, L0_gnn_att_dst, L0_gnn_bias) + _L0_mix_ref(xn[None], L0_mix_Wqkv, L0_mix_bqkv, L0_mix_Wproj, L0_mix_bproj, L0_mix_temperature)[0]
    x = x + _L0_ffn_ref(_layernorm(x, axis=-1)[None], L0_ffn_Wg, L0_ffn_bg, L0_ffn_W1, L0_ffn_b1, L0_ffn_W2, L0_ffn_b2)[0]
    return x

_drawn_inputs = setup_inputs


def setup_inputs(seed=0):
    import zlib

    import numpy as np

    out = dict(_drawn_inputs(seed))
    spreads = {'L0_gnn_bias': (0.0, 0.1),
     'L0_mix_bqkv': (0.0, 0.1),
     'L0_mix_bproj': (0.0, 0.1),
     'L0_mix_temperature': (1.0, 0.6)}
    factors = {'L0_mix_Wqkv': 8.0, 'L0_ffn_b1': 5.914, 'L0_ffn_b2': 4.648}
    for name, (base, spread) in spreads.items():
        noise = np.random.default_rng([zlib.crc32(name.encode()), seed]).standard_normal(out[name].shape)
        drawn = base * np.exp(spread * noise) if base else spread * noise
        out[name] = jnp.asarray(drawn.astype(out[name].dtype))
    for name, factor in factors.items():
        out[name] = (out[name] * factor).astype(out[name].dtype)
    return out
```

```python
from contextlib import ExitStack, contextmanager

import concourse.bass as bass
from concourse import mybir

F32 = mybir.dt.float32
I32 = mybir.dt.int32
U32 = mybir.dt.uint32
BF16 = mybir.dt.bfloat16
ALU = mybir.AluOpType
ACT = mybir.ActivationFunctionType
X = mybir.AxisListType.X
ds = bass.ds

P = 128
N = 3125
D = 256
E = 50000
GH, GD = 4, 64
MH, MD = 8, 32
NE, HID = 8, 1024
NT = -(-N // P)
TAIL = N - (NT - 1) * P
NP = NT * P
KD = D // P
HC = HID // P
AH = 2 * GH
HROW = D + GH
SQ = MD // 2
QC = P // MD
NQC = SQ // QC
NB = 8
BW = NP // NB
EP = 392
EPAD = EP * P
GE = 256
NG = EPAD // GE
NS = NG + NT - 1
TE = GE // P
NSP = 2 * P
SB = 2
NBT = NS // SB
assert NS % (2 * SB) == 0 and NG * GE == EPAD and BW * NB == NP
TW = 7
ACOL = D + 2 * GH
PAD_DST = 4096
BIG = 1e30
TOPK = 2
NJ = (TOPK * N + NE * (P - 1)) // P
NJ += NJ % 2
EPS_LN = 1e-5
EPS_N = 1e-12
QSCALE = float(MD) ** 0.25
assert NE == MH


class Steps:

    def __init__(self, eng, sem):
        self.eng, self.sem, self.n, self.i, self.per, self.k = eng, sem, 0, None, 0, 0

    def __call__(self, ins):
        ins.then_inc(self.sem, 1)
        if self.i is None:
            self.n += 1
            self.eng.wait_ge(self.sem, self.n)
        else:
            self.k += 1
            self.eng.wait_ge(self.sem, self.i * self.per + (self.n + self.k))

    @contextmanager
    def loop(self, trips, per):
        with self.eng.Fori(0, trips) as i:
            self.i, self.per, self.k = i, per, 0
            yield i
            assert self.k == per, (self.k, per)
        self.i = None
        self.n += trips * per


def gps_layer(nc, x, src, dst, wcat, wgt, att_src, att_dst, gbias, bqkv, wpt, bproj, temp,
              wg, bg, w1, b1, w2, b2, out):
    ctx = ExitStack()

    def sb(name, shape, dt=F32):
        return ctx.enter_context(nc.sbuf_tensor(name, shape, dt))

    def sem(name):
        return ctx.enter_context(nc.semaphore(name))

    def dram(name, shape, dt=F32):
        return nc.dram_tensor(name, shape, dt, kind="Internal").ap()

    def ap(t, off, pairs):
        return bass.AP(t.tensor, t.offset + off, pairs)

    def rows(t, n, w, off=0):
        return ap(t, off, [[0, n], [1, w]])

    with ctx:
        h_d = dram("h_d", [NP, HROW])
        as_d = dram("as_d", [NP, GH])
        src_d = dram("src_d", [NG, GE], I32)
        dst_d = dram("dst_d", [NG, GE], I32)
        max_d = dram("max_d", [NG, GE * (GH + 1)])
        dl_d = dram("dl_d", [NSP, GE], BF16)
        tab_d = dram("tab_d", [P, NSP * TE, TW])
        xs_d = dram("xs_d", [NJ * P, D])
        ys_d = dram("ys_d", [NJ * P, D])

        AW = 32000
        GW = 4000
        arena = sb("arena", [P, AW + GW])
        res = sb("res", [P, NT, D])
        acc = sb("acc", [P, NT * ACOL])
        identf = sb("identf", [P, P])
        identb = sb("identb", [P, P], BF16)
        onesf = sb("onesf", [P, P])
        lower = sb("lower", [P, P])
        blocks = sb("blocks", [P, P])
        iota_f = sb("iota_f", [P, P])
        iota_p = sb("iota_p", [P, 1])
        nas = sb("nas", [P, NT, AH])
        d3 = sb("d3", [P, NT * GH * 3], BF16)
        small = sb("small", [P, 700])

        A = arena[:, :]
        G = arena[:, AW:AW + GW]
        C = acc[:, :]
        S = small[:, :]

        def view(base, off, words, pat=None, **kw):
            v = base[:, off:off + words]
            return v.rearrange(pat, **kw) if pat else v

        kh = view(A, 0, NT * D, "p (t c) -> p t c", t=NT)
        vv = view(A, NT * D, NT * D, "p (t c) -> p t c", t=NT)
        qT = view(A, 2 * NT * D, KD * NP, "p (g n) -> p g n", g=KD)
        STK = 2 * NT * D + KD * NP
        stack = view(A, STK, MH * NP // 2).bitcast(BF16).rearrange("p (h n) -> p h n", h=MH)
        xn = [view(A, STK + u * D, D) for u in range(2)]
        qn = view(A, STK + NT * D, NT * D, "p (t c) -> p t c", t=NT)
        FW = SQ * MD
        kx = [view(A, STK + u * MH * 48, MH * 48) for u in range(2)]
        phi = [view(A, STK + 2 * MH * 48 + u * MH * FW, MH * FW, "p (h f) -> p h f", h=MH) for u in range(2)]
        f16, kb, vb = ([view(A, STK + 2 * MH * 48 + 2 * MH * FW + (2 * q + u) * D, D) for u in range(2)]
                       for q in range(3))
        split = [view(A, s * NP, NP).bitcast(BF16).rearrange("p (g n) -> p g n", g=KD) for s in range(3)]
        SPW = 800
        rem = view(A, 3 * NP, SPW)
        yT = view(A, 0, KD * NP, "p (g n) -> p g n", g=KD)
        ZB = 4
        zsq = [view(A, KD * NP + b * BW, BW) for b in range(ZB)]
        tq = [view(A, KD * NP + (ZB + b) * BW, BW) for b in range(2)]
        rden = [view(A, KD * NP + (ZB + 2 + b) * BW, BW) for b in range(2)]
        z16 = view(A, KD * NP + (ZB + 4) * BW, BW)
        MW = KD * NP + (ZB + 5) * BW
        wpt_s = view(A, MW, KD * D, "p (g c) -> p g c", g=KD)
        MW += KD * D

        def square():
            nonlocal MW
            MW += P
            return view(A, MW - P, P)

        coef = [[square() for g in range(KD)] for c in range(NQC)]
        cf16 = [square() for g in range(KD)]
        lin = [square() for g in range(KD)]
        gram = [square() for g in range(KD)]
        assert MW <= 2 * NT * D
        sk = [sb(f"sk{g}", [P, 1]) for g in range(KD)]
        sv = [sb(f"sv{g}", [P, 1]) for g in range(KD)]
        pairb = sb("pairb", [3 * MD, NQC, P], BF16)
        pair16 = sb("pair16", [3 * MD, MD], BF16)
        w1_s = view(A, 0, NE * KD * HID, "p (e k n) -> p e k n", e=NE, k=KD)
        w2_s = view(A, NE * KD * HID, NE * HC * D, "p (e c n) -> p e c n", e=NE, c=HC)

        wa_off = 0
        wcat_s = view(C, 0, KD * 1024, "p (k n) -> p k n", k=KD)
        wacc_s = view(C, 2048, KD * AH, "p (k n) -> p k n", k=KD)
        bqk_s = view(C, 2064, 2 * D)
        bv_s = view(C, 2576, D)
        bres_s = view(C, 2832, D)
        xT = [view(C, 3088 + u * D, KD * P, "p (k n) -> p k n", k=KD) for u in range(2)]
        hrow = [view(C, 3600 + u * 264, 264) for u in range(2)]
        qk = [view(C, 4128 + u * 512, 512, "p (h c) -> p h c", c=MD) for u in range(2)]
        qksq = [view(C, 5152 + u * 512, 512, "p (h c) -> p h c", c=MD) for u in range(2)]
        wgt_s = view(G, 0, KD * D, "p (k n) -> p k n", k=KD)
        att_s = view(G, 512, KD * AH, "p (k n) -> p k n", k=KD)
        stats = view(G, 600, NT * 6, "p (t s) -> p t s", s=6)
        mv = view(G, 760, NT * 2, "p (t s) -> p t s", s=2)
        rstd = view(G, 820, NT)
        ssq = [view(G, 860 + u * 16, 16) for u in range(2)]
        rn = [view(G, 900 + u * 16, 16) for u in range(2)]
        tempb = view(G, 940, MH)
        ssmin = view(G, 950, 2 * MH)
        dsc_i = view(C, 0, EP).bitcast(I32)
        src_i = view(C, EP, EP).bitcast(I32)
        dsc = view(C, 2 * EP, EP)
        fadd = view(C, 3 * EP, EP)
        badd = view(C, 4 * EP, EP)
        sco = view(C, 5 * EP, EP * GH, "p (e h) -> p e h", h=GH)
        mx5 = view(C, 5 * EP, EP * (GH + 1), "p (e h) -> p e h", h=GH + 1)
        fwd = view(C, 10 * EP, EP * GH, "p (e h) -> p e h", h=GH)
        rowv = view(C, 14 * EP, 8 * P, "p (q n) -> p q n", n=P)
        sl_src = view(C, 0, 2 * GE, "p (u w) -> p u w", u=2).bitcast(I32)
        sl_dst = view(C, 2 * GE, 2 * GE, "p (u w) -> p u w", u=2).bitcast(I32)
        sl_max = view(C, 4 * GE, 2 * GE * (GH + 1), "p (u w c) -> p u w c", u=2, c=GH + 1)
        tb = [view(G, 0, P * TE * TW, "p (s k w) -> p s k w", k=TE, w=TW),
              view(C, 14 * GE, P * TE * TW, "p (s k w) -> p s k w", k=TE, w=TW)]
        fsrc = view(G, P * TE * TW, 2 * GE, "p (u w) -> p u w", u=2)
        fdl = view(G, P * TE * TW + 2 * GE, 2 * GE, "p (u w) -> p u w", u=2)
        fdlb = view(G, P * TE * TW + 4 * GE, GE).bitcast(BF16).rearrange("p (u w) -> p u w", u=2)

        NBUF = 2
        gb = [view(G, u * SB * TE * ACOL, SB * TE * ACOL, "p (k c) -> p k c", c=ACOL) for u in range(NBUF)]
        o = NBUF * SB * TE * ACOL
        oh = view(G, o, SB * TE * P, "p (k v) -> p k v", v=P)
        o += SB * TE * P
        oht = [view(G, o + u * 256, 256).bitcast(BF16) for u in range(2)]
        o += 512
        dlb = [view(G, o + u * 256, 256).bitcast(BF16) for u in range(2)]
        o += 512
        tab = [view(G, o + u * 32, SB * TE * TW, "p (k w) -> p k w", w=TW) for u in range(2)]
        o += 64
        dv = [view(G, o + u * 16, 16, "p (k h) -> p k h", h=GH) for u in range(2)]
        o += 32
        a2 = [view(G, o + u * 32, 32, "p (w k h) -> p w k h", w=2, h=GH) for u in range(2)]
        o += 64
        lk = [view(G, o + u * 32, 32, "p (w k h) -> p w k h", w=2, h=GH) for u in range(2)]
        o += 64
        wl = [view(G, o + u * 16, 16, "p (k h) -> p k h", h=GH) for u in range(2)]
        o += 32
        assert o <= GW, o

        ts_row = sb("ts_row", [1, NSP], I32)
        ptick = sb("ptick", [1, 2])
        ej_row = sb("ej_row", [1, P], I32)
        QO = 2 * NT * D
        pd0 = view(A, QO, NQC * P)
        pd1 = view(A, QO + 512, NQC * P)
        pdm = view(A, QO + 1024, NQC * P)
        zrow = view(A, QO + 2048, D)
        pde = view(A, QO + 1536, MD)
        pdf = view(A, QO + 1600, 3 * MD)
        bres2 = view(C, 6200, D)
        zz = view(G, 3400, 512)
        rsd = view(G, 970, NT)
        ftc = [view(G, 1000 + g * 512, 512) for g in range(KD)]
        pn = [sb(f"pn{c}", [P, MD]) for c in range(NQC)]
        pn16 = sb("pn16", [P, MD])

        ps = ctx.enter_context(nc.psum_tensor("ps", [P, 8, 512], F32))
        psf = ps[:, :, :].rearrange("p b w -> p (b w)")
        psb = ps[:, 5, 0:256].bitcast(BF16)

        s_const = sem("constants_ready")
        s_x = sem("x_loaded")
        s_w = sem("projection_weights_loaded")
        s_att = sem("att_zeroed")
        s_attd = sem("att_loaded")
        v_step, a_step, g_step, p_step = sem("vector_steps"), sem("scalar_steps"), sem("gpsimd_steps"), sem("tensor_steps")
        s_wa = sem("score_weights_product")
        s_wac = sem("score_weights_ready")
        s_var = sem("variances_ready")
        s_sd = sem("deviations_ready")
        s_xn = sem("normalized_tiles")
        s_xt = sem("xn_transposed")
        s_xtc = sem("xn_transposed_in_sbuf")
        s_prj = sem("projected_tiles")
        s_prh = sem("h_psum_read")
        s_prv = sem("qkv_psum_read")
        s_hst = [sem(f"h_stored{u}") for u in range(2)]
        s_hrow = sem("h_row_in_sbuf")
        s_ss = sem("squared_norms")
        s_nrm = sem("norms")
        s_ast = sem("source_scores_stored")
        s_qn = sem("q_normalized")
        s_qt = sem("q_transposed")
        s_qtc = sem("q_transposed_in_sbuf")
        s_kx = sem("k_extended")
        s_kxr = sem("k_extended_read")
        s_phi = sem("pair_features")
        s_kv = sem("pair_features_used")
        s_kvd = sem("kv_sums_done")
        s_kvc = sem("kv_sums_in_sbuf")
        s_cft = sem("coefficients_transposed")
        s_cfc = sem("coefficients_in_sbuf")
        s_cf0 = sem("square_coefficients")
        s_cfd = sem("coefficients_done")
        s_pair = sem("pair_matrices")
        s_spl = [sem(f"split_part{g}") for g in range(KD)]
        s_stk = sem("stack_loaded")
        s_z = sem("pair_sums")
        s_zs = sem("pair_sums_squared")
        s_t = sem("gram_products")
        s_tq = sem("gram_terms")
        s_y = sem("mix_numerators")
        s_yT = sem("mix_outputs")
        s_zu = sem("squares_used")
        s_wpt = sem("output_weights_loaded")
        s_mo = sem("mix_projected")
        s_mor = sem("mix_added")
        s_ed = sem("edges_loaded")
        s_edc = sem("edge_padding_set")
        s_sg = [sem(f"scores_gathered{u}") for u in range(8)]
        s_sh = sem("neighbour_values_moved")
        s_shr = sem("chunk_values_ready")
        s_tr = sem("small_transposes")
        s_trc = sem("small_transposes_read")
        s_mxd = sem("maxima_stored")
        s_edst = sem("padded_edges_stored")
        s_off = sem("tile_offsets_counted")
        s_offp = sem("tile_offsets_summed")
        s_slot = sem("slot_tables_ready")
        s_slg = sem("slot_rows_gathered")
        s_slf = sem("slot_rows_converted")
        s_slt = sem("slot_rows_transposed")
        s_slc = sem("slot_words_placed")
        s_dlst = sem("local_destinations_stored")
        s_tab = sem("slot_words_stored")
        s_accz = sem("accumulator_cleared")
        s_tl = [sem(f"slot_words{u}") for u in range(2)]
        s_dl = [sem(f"destination_rows{u}") for u in range(2)]
        s_tf = [sem(f"slot_words_free{u}") for u in range(2)]
        s_gf = [sem(f"message_buffer_free{u}") for u in range(2)]
        s_tick = sem("batch_word_written")
        s_gg = [sem(f"rows_gathered{u}") for u in range(2)]
        s_oht = sem("onehot_rows")
        s_dp = sem("destination_scores")
        s_wl = sem("log_weights")
        s_we = sem("weights")
        s_msg = sem("messages")
        s_agg = sem("messages_summed")
        s_accd = sem("sums_added")
        s_w1 = sem("expert_weights_loaded")
        s_w2 = sem("late_expert_weights_loaded")
        s_hl = [sem(f"h_reloaded{u}") for u in range(2)]
        s_hf = [sem(f"h_reload_free{u}") for u in range(2)]
        s_fin = sem("final_exponents")
        s_fine = sem("final_weights")
        s_var2 = sem("variances2_ready")
        s_sd2 = sem("deviations2_ready")
        s_xn2 = sem("tokens_normalized")
        s_gt = sem("tokens_transposed")
        s_gtc = sem("tokens_transposed_in_sbuf")
        s_gs = sem("gate_scores")
        s_gsr = sem("gate_scores_read")
        s_gw = sem("gate_weights_loaded")
        s_sel = sem("experts_chosen")
        s_pre = sem("ranks_summed")
        s_e2 = sem("second_gate_exp")
        s_ez = sem("second_gate_gap")
        s_pos = sem("token_positions")
        s_ejp = sem("expert_row_product")
        s_ej = sem("expert_row_ready")
        s_zero = sem("token_slots_cleared")
        s_sc = sem("tokens_scattered")
        s_fx = [sem(f"expert_tokens{u}") for u in range(2)]
        s_ft = sem("expert_tokens_transposed")
        s_ftc = sem("expert_tokens_in_sbuf")
        s_f1 = sem("hidden_products")
        s_f1c = sem("hidden_in_sbuf")
        s_fh = sem("hidden_transposed")
        s_fhc = sem("hidden_activated")
        s_f2 = sem("expert_products")
        s_f2c = sem("expert_results")
        s_fy = [sem(f"expert_results_stored{u}") for u in range(2)]
        s_cg = [sem(f"results_gathered{u}") for u in range(2)]
        s_cf = [sem(f"results_free{u}") for u in range(2)]
        s_cm = sem("outputs_combined")
        s_out = sem("outputs_stored")
        s_zrow = sem("zero_row_ready")
        s_zero_v = sem("zeros_ready")
        s_pairb = sem("pair_matrices_ready")
        s_pairT = sem("pair_matrices_transposed")
        s_z16 = sem("half_shift_sums")
        s_z16s = sem("half_shift_squares")
        s_dn = sem("denominators_summed")
        s_den = sem("denominators_read")

        o = 0

        def word(n, *shape, pat=None, **kw):
            nonlocal o
            v = view(S, o, n, pat, **kw)
            o += n
            return v

        cnt, offs, fo, co, nsl, stt, sex, dif = (word(32) for _ in range(8))
        tint = word(32).bitcast(I32)
        ts_p, gs_p, sl_p, tsm, tsc = (word(2) for _ in range(5))
        gs_i = word(2).bitcast(I32)
        chv = word(12, pat="p (q h) -> p q h", h=GH)
        cin = word(12, pat="p (q h) -> p q h", h=GH)
        iota_e, cnt_e, ntl, endj, basej = (word(NE) for _ in range(5))
        nti = word(NE).bitcast(I32)
        ej, ejc = word(1), word(1)
        half32 = word(32)
        junk = word(GE // 2)
        rowval = word(1)
        wait_w = word(NT)
        mv2 = word(2 * NT, pat="p (t s) -> p t s", s=2)
        assert o <= 700, o

        o = 800

        def tail(n, pat=None, **kw):
            nonlocal o
            v = view(G, o, n, pat, **kw)
            o += n
            return v

        NH = NT * GH
        has, mlog, slog, mtop, den, f1, f2 = (tail(NH, "p (t h) -> p t h", h=GH) for _ in range(7))
        dlog = tail(2 * NH, "p (w t h) -> p w t h", w=2, h=GH)
        dexp = tail(2 * NH, "p (w t h) -> p w t h", w=2, h=GH)
        hb = [tail(D, "p (h c) -> p h c", h=GH) for _ in range(2)]
        tm = [tail(D, "p (h c) -> p h c", h=GH) for _ in range(2)]
        stats2 = view(G, 800, NT * 6, "p (t s) -> p t s", s=6)
        o = 1000
        NX = NT * NE
        bgb = tail(NE)
        wg_s = tail(KD * NE, "p (k e) -> p k e", k=KD)
        gsc = tail(NX, "p (t e) -> p t e", e=NE)
        top = tail(NX, "p (t e) -> p t e", e=NE)
        topi = tail(NX, "p (t e) -> p t e", e=NE).bitcast(U32)
        ti = tail(NT * 2, "p (t e) -> p t e", e=2)
        msk = [tail(NX, "p (t e) -> p t e", e=NE) for _ in range(2)]
        msum = tail(NX, "p (t e) -> p t e", e=NE)
        cum = tail(NX, "p (t e) -> p t e", e=NE)
        pos = tail(NX, "p (t e) -> p t e", e=NE)
        mp = tail(NX, "p (t e) -> p t e", e=NE)
        zeros_e = tail(32)
        g2T = [tail(D, "p (k n) -> p k n", k=KD) for _ in range(2)]
        assert o <= GW, o
        wait_s = sb("deviations2", [P, NT])[:, :]
        dif2 = sb("dif2", [P, NT, GH])[:, :, :]
        egap = sb("egap", [P, NT])
        eexp = sb("eexp", [P, NT])
        pr = [sb(f"prob{k}", [P, NT]) for k in range(2)]
        posf = [sb(f"posf{k}", [P, NT]) for k in range(2)]
        posi = [sb(f"posi{k}", [P, NT], I32) for k in range(2)]
        b1_s = sb("b1_s", [P, NE * HC])
        xn2 = view(C, 0, NT * D, "p (t c) -> p t c", t=NT)
        xfT = [view(C, u * D, D, "p (k n) -> p k n", k=KD) for u in range(2)]
        xf = [view(C, 512 + u * D, D) for u in range(2)]
        hs = [view(C, 1024 + u * HID, HID) for u in range(2)]
        hT = [view(C, 3072 + u * HID, HID, "p (c n) -> p c n", c=HC) for u in range(2)]
        ys = [view(C, 5120 + u * D, D) for u in range(2)]
        b2_s = view(G, 1000, NE * D, "p (e c) -> p e c", e=NE)
        yg = [[view(C, (2 * u + k) * D, D) for k in range(2)] for u in range(2)]

        def bc(t, shape_pairs):
            return ap(t, 0, [list(t.ap[0])] + shape_pairs)

        def over(v, n):
            return ap(v, 0, [list(q) for q in v.ap] + [[0, n]])

        def under(v, n):
            q = [list(z) for z in v.ap]
            return ap(v, 0, [q[0], [0, n]] + q[1:])

        def back(v):
            (ps_, pn), (st, n) = v.ap
            return ap(v, st * (n - 1), [[ps_, pn], [-st, n]])

        def late(t, lag):
            return not isinstance(t, int) or t >= lag

        def in_pairs(fori, n, body):
            body(0, 0)
            body(1, 1)
            with fori(n // 2) as i:
                body(2 * i, 0)
                body(2 * i + 1, 1)
            if n % 2:
                body(n - 1, 0)

        def plain(eng):
            def fori(m):
                return eng.Fori(1, m)
            return fori

        xt = x[0:(NT - 1) * P, :].rearrange("(t p) c -> p t c", p=P)
        ot = out[0:(NT - 1) * P, :].rearrange("(t p) c -> p t c", p=P)

        block = ctx.enter_context(nc.Block())

        @block.sync
        def _(sp):
            sp.dma_start(wcat_s, wcat).then_inc(s_w, 16)
            sp.dma_start(wgt_s, wgt).then_inc(s_w, 16)
            sp.dma_start(bqk_s, rows(bqkv, P, 2 * D)).then_inc(s_w, 16)
            sp.dma_start(bv_s, rows(bqkv, P, D, 2 * D)).then_inc(s_w, 16)
            sp.dma_start(tempb, rows(temp, P, MH)).then_inc(s_w, 16)
            for c in range(4):
                a, b = c * 6, (c + 1) * 6
                sp.dma_start(res[:, a:b, :], xt[:, a:b, :]).then_inc(s_x, 16)
            sp.wait_ge(s_const, 1)
            sp.dma_start(res[0:TAIL, NT - 1, :], x[(NT - 1) * P:N, :]).then_inc(s_x, 16)
            sp.wait_ge(s_att, 1)
            for h in range(GH):
                q = GD * (h % 2)
                for w, a in ((0, att_src), (GH, att_dst)):
                    sp.dma_start(att_s[q:q + GD, h // 2, w + h:w + h + 1],
                                 a[h:h + 1, :].rearrange("a c -> c a")).then_inc(s_attd, 16)

            def store_h(t, u):
                sp.wait_ge(s_hrow, t + 1)
                sp.dma_start(h_d.rearrange("(t p) c -> t p c", p=P)[ds(t, 1)].rearrange("o p c -> (o p) c"),
                             hrow[u][:, 0:HROW]).then_inc(s_hst[u], 16)
            in_pairs(plain(sp), NT, store_h)
            sp.dma_start(as_d.rearrange("(t p) h -> p t h", p=P), nas[:, :, 0:GH]).then_inc(s_ast, 16)

            sp.wait_ge(s_edc, 2)
            full = E // EP
            for t, v in ((src, src_i), (dst, dsc_i)):
                sp.dma_start(v[0:full, :], t[0:full * EP].rearrange("(p e) -> p e", e=EP)).then_inc(s_ed, 16)
                sp.dma_start(v[full:full + 1, 0:E - full * EP],
                             t[full * EP:E].rearrange("(a e) -> a e", a=1)).then_inc(s_ed, 16)
            sp.wait_ge(s_ed, 64)
            sp.dma_start(src_d.rearrange("g w -> (g w)").rearrange("(p e) -> p e", e=EP), src_i).then_inc(s_edst, 16)
            sp.dma_start(dst_d.rearrange("g w -> (g w)").rearrange("(p e) -> p e", e=EP), dsc_i).then_inc(s_edst, 16)
            for g in range(KD):
                sp.wait_ge(s_spl[g], NP // SPW)
                for h in range(QC):
                    for s in range(3):
                        sp.dma_start(stack[s * MD:(s + 1) * MD, g * QC + h, :],
                                     split[s][h * MD:(h + 1) * MD, g, :]).then_inc(s_stk, 16)

            sp.dma_start(wpt_s, wpt).then_inc(s_wpt, 16)
            sp.wait_ge(s_shr, 1)
            sp.dma_start(max_d.rearrange("g w -> (g w)").rearrange("(p e) -> p e", p=P),
                         mx5.rearrange("p e h -> p (e h)")).then_inc(s_mxd, 16)
            sp.wait_ge(s_slf, 1)
            for u in range(2):
                sp.dma_start(dl_d[u * P:(u + 1) * P, :], fdlb[:, u, :]).then_inc(s_dlst, 16)
            for u in range(2):
                sp.wait_ge(s_slc, u + 1)
                sp.dma_start(tab_d[:, u * P * TE:(u + 1) * P * TE, :],
                             tb[u].rearrange("p s k w -> p (s k) w")).then_inc(s_tab, 16)

            sp.wait_ge(s_slt, 2)
            sp.wait_ge(s_tab, 32)
            sp.wait_ge(s_dlst, 32)

            def load_batch(b, u):
                if late(b, 2):
                    sp.wait_ge(s_tf[u], (b - u) // 2 if isinstance(b, int) else s_of(b, u))
                sp.dma_start(tab[u], tab_d[:, ds(b * (SB * TE), SB * TE), :]).then_inc(s_tl[u], 16)
                sp.dma_start(dlb[u].rearrange("p (s e) -> p s e", s=SB),
                             dl_rows(b)).then_inc(s_dl[u], 16)

            def s_of(b, u):
                return loop_i[0]

            def dl_rows(b):
                base = dl_d[ds(b * SB, SB), :]
                return bass.AP(base.tensor, base.offset, [[0, P], [GE, SB], [1, GE]])

            loop_i = [None]
            load_batch(0, 0)
            load_batch(1, 1)
            with sp.Fori(1, NBT // 2) as i:
                loop_i[0] = i
                load_batch(2 * i, 0)
                load_batch(2 * i + 1, 1)

            sp.wait_ge(s_mor, NT)
            for e in range(NE):
                sp.dma_start(w1_s[:, e], w1[:, e]).then_inc(s_w1, 16)
                if e < NE // 2:
                    sp.dma_start(w2_s[:, e], w2[:, e]).then_inc(s_w1, 16)
            sp.wait_ge(s_accd, NS)
            for e in range(NE // 2, NE):
                sp.dma_start(w2_s[:, e], w2[:, e]).then_inc(s_w2, 16)
            sp.dma_start(b1_s[:, :], b1).then_inc(s_w2, 16)

            def reload_h(t, u):
                if late(t, 2):
                    sp.wait_ge(s_hf[u], (t - u) // 2 if isinstance(t, int) else loop_i[0])
                sp.dma_start(hb[u].rearrange("p h c -> p (h c)"),
                             h_d.rearrange("(t p) c -> t p c", p=P)[ds(t, 1)].rearrange("o p c -> (o p) c")[:, 0:D])\
                  .then_inc(s_hl[u], 16)
            reload_h(0, 0)
            reload_h(1, 1)
            with sp.Fori(1, NT // 2) as i:
                loop_i[0] = i
                reload_h(2 * i, 0)
                reload_h(2 * i + 1, 1)
            reload_h(NT - 1, 0)

            sp.wait_ge(s_var2, 1)
            sp.dma_start(bgb, rows(bg, P, NE)).then_inc(s_gw, 16)
            sp.dma_start(wg_s, wg).then_inc(s_gw, 16)
            sp.wait_ge(s_pos, 1)
            sp.dma_start(b2_s, ap(b2, 0, [[0, P], [D, NE], [1, D]])).then_inc(s_w2, 16)

            sp.wait_ge(s_sc, 16 * TOPK * NT)

            def load_tokens(j, u):
                if late(j, 2):
                    sp.wait_ge(s_ft, j - 1)
                sp.dma_start(xf[u], xs_d.rearrange("(t p) c -> t p c", p=P)[ds(j, 1)].rearrange("o p c -> (o p) c"))\
                  .then_inc(s_fx[u], 16)
            load_tokens(0, 0)
            load_tokens(1, 1)
            with sp.Fori(1, NJ // 2) as i:
                loop_i[0] = i
                load_tokens(2 * i, 0)
                load_tokens(2 * i + 1, 1)

            for t in range(NT):
                sp.wait_ge(s_cm, t + 1)
                if t < NT - 1:
                    sp.dma_start(ot[:, t, :], res[:, t, :]).then_inc(s_out, 16)
                else:
                    sp.dma_start(out[t * P:N, :], res[0:TAIL, t, :]).then_inc(s_out, 16)
            sp.wait_ge(s_out, 16 * NT)

        @block.gpsimd
        def _(pool):
            st = Steps(pool, g_step)
            pool.memset(res[:, NT - 1, :], 0.0).then_inc(s_const, 1)
            pool.memset(att_s, 0.0).then_inc(s_att, 1)
            pool.memset(identf[:, :], 0.0)
            st(pool.memset(onesf[:, :], 1.0))
            pool.affine_select(out=identf[:, :], in_=identf[:, :], compare_op=ALU.not_equal, fill=1.0,
                               base=0, pattern=[[-1, P]], channel_multiplier=1).then_inc(s_const, 1)
            pool.affine_select(out=lower[:, :], in_=onesf[:, :], compare_op=ALU.is_ge, fill=0.0,
                               base=-1, pattern=[[1, P]], channel_multiplier=-1).then_inc(s_const, 1)
            pool.iota(iota_f[:, :], pattern=[[1, P]], base=0, channel_multiplier=0,
                      allow_small_or_imprecise_dtypes=True).then_inc(s_const, 1)
            pool.iota(iota_p[:, :], pattern=[[0, 1]], base=0, channel_multiplier=1,
                      allow_small_or_imprecise_dtypes=True).then_inc(s_const, 1)
            pool.wait_ge(s_const, 5)
            for s in range(3):
                q = slice(s * MD, (s + 1) * MD)
                st(pool.iota(pd0[q].rearrange("p (c r i) -> p c r i", c=NQC, r=QC),
                             pattern=[[0, NQC], [0, QC], [1, MD]], base=0, channel_multiplier=-1,
                             allow_small_or_imprecise_dtypes=True))
                st(pool.iota(pd1[q].rearrange("p (c r i) -> p c r i", c=NQC, r=QC),
                             pattern=[[QC, NQC], [1, QC], [1, MD]], base=0, channel_multiplier=-1,
                             allow_small_or_imprecise_dtypes=True))
                pool.iota(pde[q], pattern=[[1, MD]], base=0, channel_multiplier=-1,
                          allow_small_or_imprecise_dtypes=True).then_inc(s_pair, 1)
                pool.wait_ge(s_pair, s + 1)

            pool.wait_ge(s_ast, 16)
            pool.wait_ge(s_ed, 64)
            for j in range(EP):
                pool.indirect_dma_start(sco[:, j, :], None, as_d, bass.IndirectOffsetOnAxis(src_i[:, j:j + 1], 0))\
                    .then_inc(s_sg[j % 8], 16)

            pool.wait_ge(s_slot, 1)
            pool.wait_ge(s_edst, 32)
            pool.wait_ge(s_mxd, 16)
            for u in range(2):
                idx = bass.IndirectOffsetOnAxis(gs_i[:, u:u + 1], 0)
                pool.indirect_dma_start(sl_src[:, u, :], None, src_d, idx).then_inc(s_slg, 16)
                pool.indirect_dma_start(sl_dst[:, u, :], None, dst_d, idx).then_inc(s_slg, 16)
                pool.indirect_dma_start(sl_max[:, u].rearrange("p w c -> p (w c)"), None, max_d, idx).then_inc(s_slg, 16)

            for u in range(2):
                pool.wait_ge(s_hst[u], 16 * ((NT + 1 - u) // 2))

            st(pool.memset(ptick[:, :], 0.0))

            def gather(b, u, n):
                if late(b, 1):
                    pool.wait_ge(s_tick, b)
                if late(b, 2):
                    pool.wait_ge(s_agg, b * SB - SB)
                pool.wait_ge(s_tl[u], 16 * n + 16)
                pool.tensor_tensor(ptick[:, 1:2], ptick[:, 0:1], ptick[:, 0:1], ALU.add).then_inc(s_tick, 1)
                for k in range(SB * TE):
                    pool.indirect_dma_start(gb[u][:, k, 0:HROW], None, h_d,
                                            bass.IndirectOffsetOnAxis(tab[u][:, k, 0:1].bitcast(I32), 0))\
                        .then_inc(s_gg[u], 16)
            gather(0, 0, 0)
            gather(1, 1, 0)
            with pool.Fori(1, NBT // 2) as i:
                gather(2 * i, 0, i)
                gather(2 * i + 1, 1, i)

            pool.wait_ge(s_zero, 16)
            pool.wait_ge(s_pos, 1)
            for t in range(NT):
                n = P if t < NT - 1 else TAIL
                for k in range(TOPK):
                    pool.indirect_dma_start(xs_d, bass.IndirectOffsetOnAxis(posi[k][0:n, t:t + 1], 0),
                                            xn2[0:n, t, :], None).then_inc(s_sc, 16)
            for u in range(2):
                pool.wait_ge(s_fy[u], 16 * (NJ // 2))
            for t in range(NT):
                u = t % 2
                if t >= 2:
                    pool.wait_ge(s_cm, t - 1)
                for k in range(TOPK):
                    pool.indirect_dma_start(yg[u][k], None, ys_d, bass.IndirectOffsetOnAxis(posi[k][:, t:t + 1], 0))\
                        .then_inc(s_cg[u], 16)

        @block.scalar
        def _(act):
            A_ = nc.scalar
            it = [None]

            def turns(n, *parts):
                def pair(i):
                    for part in parts:
                        part(2 * i, 0, i)
                        part(2 * i + 1, 1, i)
                pair(0)
                with act.Fori(1, n // 2) as i:
                    pair(i)
                if n % 2:
                    for part in parts:
                        part(n - 1, 0, n // 2)

            act.wait_ge(s_zrow, 1)
            act.dma_start(xs_d.rearrange("(j p) c -> p j c", p=P), ap(zrow, 0, [list(zrow.ap[0]), [0, NJ], [1, D]]))\
               .then_inc(s_zero, 16)
            act.wait_ge(s_wa, 1)
            act.copy(wacc_s, ps[:, 7, 0:KD * AH].rearrange("p (k n) -> p k n", k=KD)).then_inc(s_wac, 1)
            act.dma_start(bres_s, rows(gbias, P, D)).then_inc(s_w, 16)
            act.dma_start(bres2, rows(bproj, P, D)).then_inc(s_w, 16)
            act.wait_ge(s_var, 1)
            A_.activation(rsd, rstd, ACT.Sqrt).then_inc(s_sd, 1)

            def project(t, u, i):
                act.wait_ge(s_xt, t + 1)
                if late(t, 2):
                    act.wait_ge(s_prj, t - 1)
                A_.copy(xT[u], ps[:, 6 + u, 0:D].rearrange("p (k n) -> p k n", k=KD)).then_inc(s_xtc, 1)

            def rows_out(t, u, i):
                act.wait_ge(s_prj, t + 1)
                if late(t, 2):
                    act.wait_ge(s_hst[u], 16 * i)
                A_.copy(nas[:, ds(t, 1), :].rearrange("p o c -> p (o c)"), ps[:, 3 * u, D:D + AH])
                A_.copy(hrow[u], ps[:, 3 * u, 0:264]).then_inc(s_hrow, 1)
                act.wait_ge(s_ss, t + 1)
                if late(t, 2):
                    act.wait_ge(s_qn, t - 1)
                A_.activation(rn[u], ssq[u], ACT.Sqrt).then_inc(s_nrm, 1)

            turns(NT, project, rows_out)

            def q_out(t, u, i):
                act.wait_ge(s_qt, t + 1)
                if isinstance(t, int) and t == 0:
                    act.wait_ge(s_zero, 16)
                A_.copy(qT[:, :, ds(t * P, P)], ps[:, 6 + u, 0:D].rearrange("p (g n) -> p g n", g=KD))\
                  .then_inc(s_qtc, 1)
            turns(NT, q_out)

            def extend(t, u, i):
                if late(t, 2):
                    act.wait_ge(s_kv, t - 1)
                v = kx[u].rearrange("p (h c) -> p h c", h=MH)
                k = kh[:, ds(t, 1), :].rearrange("p o (h c) -> p (o h) c", c=MD)
                A_.copy(v[:, :, 0:MD], k)
                A_.copy(kb[u], kh[:, ds(t, 1), :].rearrange("p o c -> p (o c)"))
                A_.copy(vb[u], vv[:, ds(t, 1), :].rearrange("p o c -> p (o c)"))
                A_.copy(v[:, :, MD:MD + SQ], k[:, :, 0:SQ]).then_inc(s_kx, 1)
            act.wait_ge(s_qn, NT)
            act.wait_ge(s_prv, NT)
            act.wait_ge(s_qt, NT)
            turns(NT, extend)

            act.wait_ge(s_cfd, 1)
            n = 0
            for b in range(NB):
                for g in range(KD):
                    for c in range(NQC):
                        for h in range(QC):
                            act.wait_ge(s_z, n + 1)
                            if n >= ZB:
                                act.wait_ge(s_zu, n - ZB + 1)
                            A_.activation(zsq[n % ZB], ps[:, n % 2, 0:BW], ACT.Square).then_inc(s_zs, 1)
                            n += 1
                    act.wait_ge(s_z16, b * KD + g + 1)
                    if b * KD + g >= 1:
                        act.wait_ge(s_y, b * KD + g)
                    A_.activation(z16, ps[:, 2, 0:BW], ACT.Square).then_inc(s_z16s, 1)

            def weigh(b, u, i):
                act.wait_ge(s_wl, b + 1)
                A_.activation(gb[u][:, :, D:D + GH], wl[u], ACT.Exp).then_inc(s_we, 1)
            turns(NBT, weigh)

            act.wait_ge(s_fin, 1)
            A_.activation(dexp, dlog, ACT.Exp).then_inc(s_fine, 1)
            act.wait_ge(s_var2, 1)
            A_.activation(wait_s, wait_w, ACT.Sqrt).then_inc(s_sd2, 1)

            def tokens_T(t, u, i):
                act.wait_ge(s_gt, t + 1)
                if late(t, 2):
                    act.wait_ge(s_gs, t - 1)
                A_.copy(g2T[u], ps[:, 5 + u, 0:D].rearrange("p (k n) -> p k n", k=KD)).then_inc(s_gtc, 1)
            turns(NT, tokens_T)
            act.wait_ge(s_ez, 1)
            A_.activation(eexp[:, :], egap[:, :], ACT.Exp).then_inc(s_e2, 1)

            act.wait_ge(s_w2, 16 * (NE // 2 + 2))
            eng_e = []

            def expert(j, u, i):
                act.wait_ge(s_ft, j + 1)
                if late(j, 2):
                    act.wait_ge(s_f1, j - 1)
                A_.copy(xfT[u], ps[:, 7 * u, 0:D].rearrange("p (k n) -> p k n", k=KD)).then_inc(s_ftc, 1)
                ej = act.value_load(ej_row[0:1, ds(j, 1)], min_val=0, max_val=NE - 1)
                act.wait_ge(s_fh, j + 1)
                if late(j, 2):
                    act.wait_ge(s_f2, j - 1)
                for c in range(HC):
                    last = A_.activation(hT[u][:, c, :], ps[:, 3 + c // 4, (c % 4) * P:(c % 4 + 1) * P], ACT.Relu,
                                         bias=b1_s[:, ds(ej * HC + c, 1)])
                last.then_inc(s_fhc, 1)
                act.wait_ge(s_f2c, j + 1)
                act.dma_start(ys_d.rearrange("(t p) c -> t p c", p=P)[ds(j, 1)].rearrange("o p c -> (o p) c"), ys[u])\
                   .then_inc(s_fy[u], 16)
            act.wait_ge(s_ej, 1)
            turns(NJ, expert)
            for u in range(2):
                act.wait_ge(s_fy[u], 16 * (NJ // 2))

        @block.tensor
        def _(pe):
            MM, TR = nc.tensor.matmul, nc.tensor.transpose

            def turns(n, *parts):
                def pair(i):
                    for part in parts:
                        part(2 * i, 0)
                        part(2 * i + 1, 1)
                pair(0)
                with pe.Fori(1, n // 2) as i:
                    pair(i)
                if n % 2:
                    for part in parts:
                        part(n - 1, 0)

            pe.wait_ge(s_w, 16 * 5)
            pe.wait_ge(s_attd, 16 * AH)
            for k in range(KD):
                for c in range(KD):
                    last = MM(ps[:, 7, k * AH:(k + 1) * AH], wgt_s[:, c, k * P:(k + 1) * P], att_s[:, c, :],
                              start=(c == 0), stop=(c == KD - 1))
            last.then_inc(s_wa, 1)
            pe.wait_ge(s_pairb, 1)
            for c in range(NQC):
                last = TR(psb[:, c * MD:(c + 1) * MD], pairb[0:MD, c, :], identb[0:MD, 0:MD])
            last.then_inc(s_pairT, 1)
            pe.wait_ge(s_wac, 1)

            def transpose_x(t, u):
                pe.wait_ge(s_xn, t + 1)
                if late(t, 2):
                    pe.wait_ge(s_xtc, t - 1)
                for k in range(KD):
                    last = TR(ps[:, 6 + u, k * P:(k + 1) * P],
                              xn[u][:, k * P:(k + 1) * P], identf[:, :])
                last.then_inc(s_xt, 1)

            def project(t, u):
                pe.wait_ge(s_xtc, t + 1)
                if late(t, 2):
                    pe.wait_ge(s_hrow, t - 1)
                    pe.wait_ge(s_prv, t - 1)
                for o_, w, s in ((ps[:, 3 * u, 0:D], wcat_s, slice(0, D)), (ps[:, 3 * u, D:D + AH], wacc_s, slice(0, AH)),
                                 (ps[:, 3 * u + 1, :], wcat_s, slice(D, 3 * D)),
                                 (ps[:, 3 * u + 2, 0:D], wcat_s, slice(3 * D, 4 * D))):
                    for k in range(KD):
                        last = MM(o_, xT[u][:, k, :], w[:, k, s], start=(k == 0), stop=(k == KD - 1))
                last.then_inc(s_prj, 1)
            turns(NT, transpose_x, project)

            def q_T(t, u):
                pe.wait_ge(s_qn, t + 1)
                if late(t, 2):
                    pe.wait_ge(s_qtc, t - 1)
                for g in range(KD):
                    last = TR(ps[:, 6 + u, g * P:(g + 1) * P],
                              qn[:, t, g * P:(g + 1) * P], identf[:, :])
                last.then_inc(s_qt, 1)
            pe.wait_ge(s_xtc, NT)
            for t in range(NT):
                q_T(t, t % 2)

            pe.wait_ge(s_prv, NT)
            pe.wait_ge(s_hrow, NT)
            pe.wait_ge(s_zero_v, 1)
            for g in range(4):
                MM(ps[:, g, :], zz[:, 0:P], zz, start=True, stop=False, skip_group_check=True)

            def sums(t, u, n=P, final=False):
                pe.wait_ge(s_phi, t + 1)
                for g in range(KD):
                    k_ = kb[u][0:n, g * P:(g + 1) * P]
                    v_ = vb[u][0:n, g * P:(g + 1) * P]
                    f_ = f16[u][0:n, g * P:(g + 1) * P]
                    for h in range(QC):
                        MM(ps[h * MD:(h + 1) * MD, g, :],
                           v_[:, h * MD:(h + 1) * MD],
                           phi[u][0:n, g * QC + h, :], start=False, stop=final, skip_group_check=True)
                    b = ps[:, 2 + g, :]
                    kw = dict(start=False, stop=final, skip_group_check=True)
                    MM(b[:, 0:P], k_, v_, **kw)
                    MM(b[:, P:2 * P], k_, k_, **kw)
                    MM(b[:, 2 * P:3 * P], f_, v_, **kw)
                    MM(b[:, 3 * P:3 * P + 1], k_, onesf[0:n, 0:1], **kw)
                    last = MM(b[:, 3 * P + 1:3 * P + 2], v_, onesf[0:n, 0:1], **kw)
                last.then_inc(s_kv, 1)
            sums(0, 0)
            sums(1, 1)
            with pe.Fori(1, NT // 2) as i:
                sums(2 * i, 0)
                sums(2 * i + 1, 1)
            sums(NT - 1, 0, TAIL, True)

            pe.wait_ge(s_kvc, 1)
            for c in range(NQC):
                for g in range(KD):
                    last = TR(ps[:, 4 + g, c * P:(c + 1) * P], ftc[g][:, c * P:(c + 1) * P], identf[:, :])
            last.then_inc(s_cft, 1)
            pe.wait_ge(s_cfc, 1)
            for g in range(KD):
                for c in range(NQC):
                    MM(ps[0:MD, 6, g * P:(g + 1) * P], pn[c][:, :], coef[c][g], start=(c == 0), stop=False)
                last = MM(ps[0:MD, 6, g * P:(g + 1) * P], pn16[:, :], cf16[g], start=False, stop=True)
            last.then_inc(s_cf0, 1)

            pe.wait_ge(s_cfd, 1)
            pe.wait_ge(s_stk, 16 * 3 * MH)
            n = 0
            lag = []

            def use(m, h, g, c):
                pe.wait_ge(s_zs, m + 1)
                MM(ps[h * MD:(h + 1) * MD, 3 + g, 0:BW], coef[c][g][:, h * MD:(h + 1) * MD], zsq[m % ZB],
                   start=(c == 0), stop=False, skip_group_check=True).then_inc(s_zu, 1)
            for b in range(NB):
                col = slice(b * BW, (b + 1) * BW)
                for g in range(KD):
                    r = b * KD + g
                    if r >= KD:
                        pe.wait_ge(s_yT, r - KD + 1)
                    MM(ps[:, 5, 0:BW], gram[g], qT[:, g, col], start=True, stop=True).then_inc(s_t, 1)
                    if r >= 1:
                        pe.wait_ge(s_z16s, r)
                    for h in range(QC):
                        last = MM(ps[h * MD:(h + 1) * MD, 2, 0:BW], pair16[:, :], stack[0:3 * MD, g * QC + h, col],
                                  start=True, stop=True)
                    last.then_inc(s_z16, 1)
                    for c in range(NQC):
                        for h in range(QC):
                            if n >= 2:
                                pe.wait_ge(s_zs, n - 1)
                            MM(ps[:, n % 2, 0:BW], pairb[:, c, :], stack[0:3 * MD, g * QC + h, col],
                               start=True, stop=True).then_inc(s_z, 1)
                            lag.append((n, h, g, c))
                            n += 1
                            if len(lag) > 1:
                                use(*lag.pop(0))
                    while lag:
                        use(*lag.pop(0))
                    pe.wait_ge(s_z16s, r + 1)
                    MM(ps[:, 3 + g, 0:BW], cf16[g], z16, start=False, stop=False, skip_group_check=True)
                    MM(ps[:, 3 + g, 0:BW], lin[g], qT[:, g, col], start=False, stop=True, skip_group_check=True)\
                        .then_inc(s_y, 1)
                    pe.wait_ge(s_tq, r + 1)
                    if r >= 1:
                        pe.wait_ge(s_den, r)
                    MM(ps[:, 6, 0:BW], blocks[:, :], tq[r % 2], start=True, stop=True).then_inc(s_dn, 1)

            pe.wait_ge(s_yT, NB * KD)
            pe.wait_ge(s_wpt, 16)

            def mix_out(t, u):
                if late(t, 2):
                    pe.wait_ge(s_mor, t - 1)
                for g in range(KD):
                    last = MM(ps[:, u, 0:D], yT[:, g, ds(t * P, P)], wpt_s[:, g, :], start=(g == 0), stop=(g == KD - 1))
                last.then_inc(s_mo, 1)
            for t in range(NT):
                mix_out(t, t % 2)

            for d in range(2):
                pe.wait_ge(s_sh, 2 * d + 1)
                for q in range(3):
                    last = TR(ps[0:GH, 7, q * P:(q + 1) * P], chv[:, q, :], identf[:, :])
                last.then_inc(s_tr, 1)
                pe.wait_ge(s_sh, 2 * d + 2)
                for q in range(2):
                    last = TR(ps[:, 7, 3 * P + q * GH:3 * P + (q + 1) * GH], rowv[0:GH, 6 + q, :], identf[0:GH, 0:GH])
                last.then_inc(s_tr, 1)
            pe.wait_ge(s_off, 1)
            MM(ps[:, 7, 0:32], onesf[:, :], cnt, start=True, stop=True).then_inc(s_offp, 1)
            pe.wait_ge(s_off, 2)
            for u in range(2):
                last = MM(ps[0:1, 7, u * P:(u + 1) * P], tsc[:, u:u + 1], identf[:, :], start=True, stop=True)
            last.then_inc(s_offp, 1)
            pe.wait_ge(s_slf, 1)
            for u in range(2):
                if u:
                    pe.wait_ge(s_slc, u)
                for m in range(TE * TW):
                    w, k = m // TE, m % TE
                    if w == 0:
                        v = fsrc[:, u, k * P:(k + 1) * P]
                    elif w == 1:
                        v = fdl[:, u, k * P:(k + 1) * P]
                    else:
                        v = sl_max[:, u, k * P:(k + 1) * P, w - 2]
                    last = TR(ps[:, m // 4, (m % 4) * P:(m % 4 + 1) * P], v, identf[:, :])
                last.then_inc(s_slt, 1)

            pe.wait_ge(s_accz, 1)

            def batch(b, u):
                pe.wait_ge(s_oht, b + 1)
                if late(b, 2):
                    pe.wait_ge(s_wl, b - 1)
                for s in range(SB):
                    t = pe.value_load(ts_row[0:1, ds(b * SB + s, 1)], min_val=0, max_val=NT - 1)
                    for k in range(TE):
                        m = s * TE + k
                        last = MM(ps[:, u, m * 12:(m + 1) * 12], oht[u][:, m * P:(m + 1) * P], d3[:, ds(t * 12, 12)],
                                  start=True, stop=True)
                last.then_inc(s_dp, 1)

            def aggregate(b, u):
                pe.wait_ge(s_msg, b + 1)
                for s in range(SB):
                    if late(b, 1):
                        pe.wait_ge(s_accd, b * SB + (s - SB + 1))
                    for k in range(TE):
                        m = s * TE + k
                        last = MM(ps[:, 2 + s, 0:ACOL], oh[:, m, :], gb[u][:, m, :], start=(k == 0), stop=(k == TE - 1))
                    last.then_inc(s_agg, 1)

            def both(b, u):
                batch(b, u)
                aggregate(b, u)
            turns(NBT, both)

            pe.wait_ge(s_gw, 32)

            def gate(t, u):
                pe.wait_ge(s_xn2, t + 1)
                if late(t, 2):
                    pe.wait_ge(s_gtc, t - 1)
                for k in range(KD):
                    last = TR(ps[:, 5 + u, k * P:(k + 1) * P],
                              xn2[:, t, k * P:(k + 1) * P], identf[:, :])
                last.then_inc(s_gt, 1)
                pe.wait_ge(s_gtc, t + 1)
                for k in range(KD):
                    last = MM(ps[:, 7, ds(t * NE, NE)], g2T[u][:, k, :], wg_s[:, k, :], start=(k == 0), stop=(k == KD - 1))
                last.then_inc(s_gs, 1)
            for t in range(NT):
                gate(t, t % 2)
            pe.wait_ge(s_sel, 1)
            MM(ps[:, 0, 0:NX], lower[:, :], msum.rearrange("p t e -> p (t e)"), start=True, stop=True)
            MM(ps[:, 1, 0:NX], onesf[:, :], msum.rearrange("p t e -> p (t e)"), start=True, stop=True).then_inc(s_pre, 1)
            pe.wait_ge(s_sel, 2)
            MM(ps[0:1, 2, 0:P], ejc, identf[:, :], start=True, stop=True).then_inc(s_ejp, 1)

            pe.wait_ge(s_ej, 1)
            pe.wait_ge(s_w1, 16 * (NE + NE // 2))
            pe.wait_ge(s_w2, 16 * (NE // 2 + 2))

            def expert(j, u):
                pe.wait_ge(s_fx[u], tok(j, u))
                if late(j, 2):
                    pe.wait_ge(s_ftc, j - 1)
                for k in range(KD):
                    last = TR(ps[:, 7 * u, k * P:(k + 1) * P], xf[u][:, k * P:(k + 1) * P], identf[:, :])
                last.then_inc(s_ft, 1)
                e = pe.value_load(ej_row[0:1, ds(j, 1)], min_val=0, max_val=NE - 1)
                pe.wait_ge(s_ftc, j + 1)
                if late(j, 1):
                    pe.wait_ge(s_f1c, j)
                for n_ in range(2):
                    for k in range(KD):
                        last = MM(ps[:, 1 + n_, :], xfT[u][:, k, :],
                                  w1_s[:, ds(e, 1), k, n_ * 512:(n_ + 1) * 512].rearrange("p o n -> p (o n)"),
                                  start=(k == 0), stop=(k == KD - 1))
                last.then_inc(s_f1, 1)
                pe.wait_ge(s_f1c, j + 1)
                if late(j, 1):
                    pe.wait_ge(s_fhc, j)
                for c in range(HC):
                    last = TR(ps[:, 3 + c // 4, (c % 4) * P:(c % 4 + 1) * P], hs[u][:, c * P:(c + 1) * P], identf[:, :])
                last.then_inc(s_fh, 1)
                pe.wait_ge(s_fhc, j + 1)
                if late(j, 2):
                    pe.wait_ge(s_f2c, j - 1)
                for c in range(HC):
                    last = MM(ps[:, 5 + u, 0:D], hT[u][:, c, :],
                              w2_s[:, ds(e, 1), c, :].rearrange("p o n -> p (o n)"), start=(c == 0), stop=(c == HC - 1))
                last.then_inc(s_f2, 1)
            cur = [None]

            def tok(j, u):
                return 16 if isinstance(j, int) else 16 * cur[0] + 16
            expert(0, 0)
            expert(1, 1)
            with pe.Fori(1, NJ // 2) as i:
                cur[0] = i
                expert(2 * i, 0)
                expert(2 * i + 1, 1)

        @block.vector
        def _(dve):
            V = nc.vector
            st = Steps(dve, v_step)

            def turns(n, per, *parts):
                def pair(i):
                    for part in parts:
                        part(2 * i, 0, i)
                        part(2 * i + 1, 1, i)
                pair(0)
                st.n -= 2 * per
                with dve.Fori(1, n // 2) as i:
                    st.i, st.per, st.k = i, 2 * per, 0
                    pair(i)
                    assert st.k == 2 * per, (st.k, per)
                st.i = None
                st.n += (n // 2) * 2 * per
                if n % 2:
                    for part in parts:
                        part(n - 1, 0, n // 2)

            V.memset(zrow, 0.0).then_inc(s_zrow, 1)
            V.memset(zz, 0.0).then_inc(s_zero_v, 1)
            V.memset(ssmin[:, 0:MH], (EPS_N / QSCALE) ** 2)
            V.memset(ssmin[:, MH:2 * MH], EPS_N ** 2)
            st(V.memset(blocks[:, :], 0.0))
            for h in range(QC):
                V.memset(blocks[h * MD:(h + 1) * MD, h * MD:(h + 1) * MD], 1.0)
            dve.wait_ge(s_const, 5)
            V.tensor_copy(identb[:, :], identf[:, :])
            dve.wait_ge(s_pair, 3)
            q = slice(0, 3 * MD)
            V.tensor_scalar(pdm[q], pd1[q], 0.0, None, ALU.is_equal)
            st(V.tensor_scalar(pd0[q], pd0[q], 0.0, None, ALU.is_equal))
            st(V.tensor_tensor(pd0[q], pd0[q], pdm[q], ALU.max))
            st(V.tensor_scalar(pdm[q], pd1[q], float(MD), None, ALU.is_equal))
            V.tensor_tensor(pairb[:, :, :].rearrange("p c f -> p (c f)"), pd0[0:3 * MD], pdm[0:3 * MD], ALU.max)\
                .then_inc(s_pairb, 1)
            dve.wait_ge(s_pairb, 1)
            V.tensor_scalar(pdf[q, 0:MD], pde[q, 0:MD], 0.0, None, ALU.is_equal)
            V.tensor_scalar(pdf[q, MD:2 * MD], pde[q, 0:MD], float(SQ), None, ALU.is_equal)
            st(V.tensor_scalar(pdf[q, 2 * MD:3 * MD], pde[q, 0:MD], float(-SQ), None, ALU.is_equal))
            st(V.tensor_tensor(pdf[q, 0:MD], pdf[q, 0:MD], pdf[q, MD:2 * MD], ALU.max))
            st(V.tensor_tensor(pair16[:, :], pdf[q, 0:MD], pdf[q, 2 * MD:3 * MD], ALU.max))
            for h in range(QC):
                V.tensor_scalar(pn16[h * MD:(h + 1) * MD, :], pair16[0:MD, :], -1.0, None, ALU.mult)
            dve.wait_ge(s_pairT, 1)
            for c in range(NQC):
                ins = V.tensor_scalar(pn[c][:, :], psb[:, c * MD:(c + 1) * MD], -1.0, None, ALU.mult)
            st(ins)
            st(V.tensor_copy(pn[0][0:MD, :], identf[0:MD, 0:MD]))

            dve.wait_ge(s_x, 16 * 5)
            for t in range(NT):
                ins = V.bn_stats(stats[:, t, :], res[:, t, :])
            st(ins)
            for t in range(NT):
                ins = V.bn_aggr(mv[:, t, :], stats[:, t, :])
            st(ins)
            V.tensor_scalar(rstd, mv[:, :, 1], EPS_LN, None, ALU.add).then_inc(s_var, 1)
            dve.wait_ge(s_sd, 1)
            st(V.reciprocal(rstd, rsd))
            dve.wait_ge(s_w, 16 * 7)

            def normalize(t, u, i):
                if late(t, 2):
                    dve.wait_ge(s_xt, t - 1)
                tt = ds(t, 1)
                V.tensor_scalar(xn[u], res[:, tt, :].rearrange("p o c -> p (o c)"),
                                mv[:, tt, 0], rstd[:, tt], ALU.subtract, ALU.mult).then_inc(s_xn, 1)

            def heads(t, u, i):
                dve.wait_ge(s_prj, t + 1)
                if late(t, 2):
                    dve.wait_ge(s_nrm, t - 1)
                V.tensor_tensor(qk[u].rearrange("p h c -> p (h c)"), ps[:, 3 * u + 1, :], bqk_s, ALU.add)
                V.tensor_tensor(vv[:, ds(t, 1), :].rearrange("p o c -> p (o c)"), ps[:, 3 * u + 2, 0:D], bv_s, ALU.add)\
                    .then_inc(s_prv, 1)
                dve.wait_ge(s_prv, t + 1)
                st(V.tensor_tensor(qksq[u], qk[u], qk[u], ALU.mult))
                st(V.tensor_reduce(ssq[u], qksq[u], X, ALU.add))
                V.tensor_tensor(ssq[u], ssq[u], ssmin, ALU.max).then_inc(s_ss, 1)
                dve.wait_ge(s_nrm, t + 1)
                st(V.reciprocal(rn[u], rn[u]))
                st(V.tensor_tensor(rn[u][:, 0:MH], rn[u][:, 0:MH], tempb, ALU.mult))
                V.tensor_tensor(kh[:, ds(t, 1), :].rearrange("p o (h c) -> p (o h) c", c=MD), qk[u][:, MH:2 * MH, :],
                                over(rn[u][:, MH:2 * MH], MD), ALU.mult)
                V.tensor_tensor(qn[:, ds(t, 1), :].rearrange("p o (h c) -> p (o h) c", c=MD), qk[u][:, 0:MH, :],
                                over(rn[u][:, 0:MH], MD), ALU.mult).then_inc(s_qn, 1)
            turns(NT, 4, normalize, heads)
            st(V.tensor_tensor(bres_s, bres_s, bres2, ALU.add))
            st(V.tensor_tensor(res[:, :, :], res[:, :, :], under(bres_s, NT), ALU.add))

            dve.wait_ge(s_prj, NT)
            dve.wait_ge(s_hst[0], 16 * ((NT + 1) // 2))
            dve.wait_ge(s_hst[1], 16 * (NT // 2))
            V.memset(src_i, 0).then_inc(s_edc, 1)
            V.memset(dsc_i, PAD_DST).then_inc(s_edc, 1)

            def pairs(t, u, i):
                dve.wait_ge(s_kx, t + 1)
                if late(t, 2):
                    dve.wait_ge(s_kv, t - 1)
                k0 = ap(kx[u], 0, [list(kx[u].ap[0]), [48, MH], [0, SQ], [1, MD]])
                k1 = ap(kx[u], 0, [list(kx[u].ap[0]), [48, MH], [1, SQ], [1, MD]])
                kk = kx[u].rearrange("p (h c) -> p h c", h=MH)
                V.tensor_tensor(f16[u].rearrange("p (h c) -> p h c", h=MH), kk[:, :, 0:MD], kk[:, :, SQ:SQ + MD], ALU.mult)
                V.tensor_tensor(phi[u].rearrange("p h (r i) -> p h r i", i=MD), k0, k1, ALU.mult).then_inc(s_phi, 1)
            turns(NT, 0, pairs)

            dve.wait_ge(s_kv, NT)
            for g in range(KD):
                b = ps[:, 2 + g, :]
                V.tensor_scalar(ftc[g], ps[:, g, :], 0.5, None, ALU.mult)
                V.tensor_tensor(lin[g], b[:, 0:P], blocks[:, :], ALU.mult)
                V.scalar_tensor_tensor(gram[g], b[:, P:2 * P], 0.5, blocks[:, :], ALU.mult, ALU.mult)
                V.scalar_tensor_tensor(cf16[g], b[:, 2 * P:3 * P], 0.25, blocks[:, :], ALU.mult, ALU.mult)
                V.tensor_copy(sk[g][:, :], b[:, 3 * P:3 * P + 1])
                ins = V.tensor_copy(sv[g][:, :], b[:, 3 * P + 1:3 * P + 2])
            ins.then_inc(s_kvc, 1)

            dve.wait_ge(s_qtc, NT)
            for g in range(KD):
                for c in range(NP // SPW):
                    col = slice(c * SPW, (c + 1) * SPW)
                    st(V.tensor_copy(split[0][:, g, col], qT[:, g, col]))
                    st(V.tensor_tensor(rem, qT[:, g, col], split[0][:, g, col], ALU.subtract))
                    st(V.tensor_copy(split[1][:, g, col], rem))
                    st(V.tensor_tensor(rem, rem, split[1][:, g, col], ALU.subtract))
                    V.tensor_copy(split[2][:, g, col], rem).then_inc(s_spl[g], 1)
                    dve.wait_ge(s_spl[g], c + 1)

            dve.wait_ge(s_cft, 1)
            for g in range(KD):
                for c in range(NQC):
                    ins = V.tensor_copy(coef[c][g], ps[:, 4 + g, c * P:(c + 1) * P])
            ins.then_inc(s_cfc, 1)
            dve.wait_ge(s_cf0, 1)
            for g in range(KD):
                ins = V.tensor_copy(coef[0][g][0:MD, :], ps[0:MD, 6, g * P:(g + 1) * P])
            ins.then_inc(s_cfd, 1)

            dve.wait_ge(s_stk, 16 * 3 * MH)
            for b in range(NB):
                col = slice(b * BW, (b + 1) * BW)
                for g in range(KD):
                    r = b * KD + g
                    dve.wait_ge(s_t, r + 1)
                    if r >= 2:
                        dve.wait_ge(s_dn, r - 1)
                    V.scalar_tensor_tensor(tq[r % 2], ps[:, 5, 0:BW], sk[g][:, 0:1], qT[:, g, col], ALU.add, ALU.mult)\
                        .then_inc(s_tq, 1)
                    dve.wait_ge(s_dn, r + 1)
                    V.tensor_scalar(rden[r % 2], ps[:, 6, 0:BW], float(N), None, ALU.add).then_inc(s_den, 1)
                    dve.wait_ge(s_den, r + 1)
                    st(V.reciprocal(rden[r % 2], rden[r % 2]))
                    dve.wait_ge(s_y, r + 1)
                    V.scalar_tensor_tensor(yT[:, g, col], ps[:, 3 + g, 0:BW], sv[g][:, 0:1], rden[r % 2],
                                           ALU.add, ALU.mult).then_inc(s_yT, 1)
            for t in range(NT):
                dve.wait_ge(s_mo, t + 1)
                V.tensor_tensor(res[:, t, :], res[:, t, :], ps[:, t % 2, 0:D], ALU.add).then_inc(s_mor, 1)

            for j in range(8):
                dve.wait_ge(s_sg[j], 16 * (EP // 8))
            dve.wait_ge(s_edst, 32)
            st(V.tensor_copy(dsc, dsc_i))
            V.memset(fadd[:, 0:1], 0.0)
            V.memset(badd[:, EP - 1:EP], 0.0)
            st(V.tensor_tensor(fadd[:, 1:EP], dsc[:, 1:EP], dsc[:, 0:EP - 1], ALU.is_equal))
            st(V.tensor_scalar(fadd[:, 1:EP], fadd[:, 1:EP], -1.0, BIG, ALU.add, ALU.mult))
            st(V.tensor_copy(badd[:, 0:EP - 1], fadd[:, 1:EP]))
            for h in range(GH):
                ins = V.tensor_tensor_scan(fwd[:, :, h], fadd, sco[:, :, h], -BIG, ALU.add, ALU.max)
            st(ins)
            V.tensor_copy(chv[:, 0, :], fwd[:, EP - 1, :])
            V.tensor_copy(chv[:, 1, :], ap(dsc, EP - 1, [list(dsc.ap[0]), [0, GH]]))
            V.tensor_copy(chv[:, 2, :], ap(dsc, 0, [list(dsc.ap[0]), [0, GH]])).then_inc(s_sh, 1)
            rv = rowv[0:GH]
            R0, R1, R2, R3, R4, R5, R6, R7 = (rv[:, q, :] for q in range(8))
            n1 = P - 1
            dve.wait_ge(s_tr, 1)
            st(V.tensor_copy(rv[:, 0:3, :], ps[0:GH, 7, 0:3 * P].rearrange("p (q n) -> p q n", q=3)))
            V.memset(R3[:, 0:1], -BIG)
            V.memset(R6[:, 0:1], -BIG)
            V.memset(R7, 0.0)
            V.tensor_tensor(R3[:, 1:P], R1[:, 1:P], R1[:, 0:n1], ALU.is_equal)
            st(V.tensor_tensor(R5[:, 1:P], R2[:, 1:P], R1[:, 0:n1], ALU.is_equal))
            V.tensor_scalar(R5[:, 1:P], R5[:, 1:P], -1.0, BIG, ALU.add, ALU.mult)
            st(V.tensor_scalar(R3[:, 1:P], R3[:, 1:P], -1.0, BIG, ALU.add, ALU.mult))
            st(V.tensor_tensor_scan(R4, R3, R0, -BIG, ALU.add, ALU.max))
            V.tensor_tensor(R6[:, 1:P], R5[:, 1:P], R4[:, 0:n1], ALU.add).then_inc(s_sh, 1)
            dve.wait_ge(s_tr, 2)
            st(V.tensor_copy(cin[:, 0:2, :], ps[:, 7, 3 * P:3 * P + 2 * GH].rearrange("p (q h) -> p q h", q=2)))
            for h in range(GH):
                ins = V.tensor_tensor_scan(fwd[:, :, h], fadd, sco[:, :, h], cin[:, 0, h:h + 1], ALU.add, ALU.max)
            st(ins)
            for h in range(GH):
                ins = V.tensor_tensor_scan(back(mx5[:, :, h]), back(badd), back(fwd[:, :, h]), -BIG, ALU.add, ALU.max)
            st(ins)
            V.tensor_copy(chv[:, 0, :], mx5[:, 0, 0:GH]).then_inc(s_sh, 1)
            dve.wait_ge(s_tr, 3)
            st(V.tensor_copy(R0, ps[0:GH, 7, 0:P]))
            V.memset(R3[:, n1:P], -BIG)
            V.memset(R6[:, n1:P], -BIG)
            V.tensor_tensor(R3[:, 0:n1], R2[:, 0:n1], R2[:, 1:P], ALU.is_equal)
            st(V.tensor_tensor(R7[:, 0:n1], R1[:, 0:n1], R2[:, 1:P], ALU.is_equal))
            V.tensor_scalar(R5[:, 0:n1], R7[:, 0:n1], -1.0, BIG, ALU.add, ALU.mult)
            st(V.tensor_scalar(R3[:, 0:n1], R3[:, 0:n1], -1.0, BIG, ALU.add, ALU.mult))
            st(V.tensor_tensor_scan(back(R4), back(R3), back(R0), -BIG, ALU.add, ALU.max))
            V.tensor_tensor(R6[:, 0:n1], R5[:, 0:n1], R4[:, 1:P], ALU.add).then_inc(s_sh, 1)
            dve.wait_ge(s_tr, 4)
            st(V.tensor_copy(cin[:, 0:2, :], ps[:, 7, 3 * P:3 * P + 2 * GH].rearrange("p (q h) -> p q h", q=2)))
            for h in range(GH):
                V.tensor_tensor_scan(back(mx5[:, :, h]), back(badd), back(fwd[:, :, h]), cin[:, 0, h:h + 1],
                                     ALU.add, ALU.max)
            V.tensor_scalar(mx5[:, 0:EP - 1, GH], badd[:, 0:EP - 1], -1.0, None, ALU.is_lt)
            V.tensor_scalar(mx5[:, EP - 1, GH:GH + 1], cin[:, 1, 0:1], -1.0, 1.0, ALU.mult, ALU.add).then_inc(s_shr, 1)

            st(V.memset(cnt, 0.0))
            for t in range(1, NT):
                st(V.tensor_scalar(fadd, dsc, float(t * P), None, ALU.is_lt, ALU.add, accum_out=cnt[:, t:t + 1]))
            V.memset(offs, 0.0).then_inc(s_off, 1)
            dve.wait_ge(s_offp, 1)
            st(V.tensor_copy(offs, ps[:, 7, 0:32]))
            st(V.memset(offs[:, NT:NT + 1], float(E)))
            st(V.tensor_copy(tint, offs))
            st(V.tensor_scalar(tint, tint, GE.bit_length() - 1, None, ALU.logical_shift_right))
            st(V.tensor_copy(fo, tint))
            st(V.tensor_scalar(tint, offs, float(GE - 1), None, ALU.add))
            st(V.tensor_scalar(tint, tint, GE.bit_length() - 1, None, ALU.logical_shift_right))
            st(V.tensor_copy(co, tint))
            a, z = slice(0, NT), slice(1, NT + 1)
            V.tensor_tensor(nsl[:, a], co[:, z], fo[:, a], ALU.subtract)
            st(V.tensor_tensor(half32[:, a], offs[:, z], offs[:, a], ALU.is_gt))
            st(V.tensor_tensor(nsl[:, a], nsl[:, a], half32[:, a], ALU.mult))
            st(V.memset(half32, 0.0))
            st(V.tensor_tensor_scan(stt[:, a], nsl[:, a], half32[:, a], 0.0, ALU.add, ALU.add))
            st(V.tensor_tensor(sex[:, a], stt[:, a], nsl[:, a], ALU.subtract))
            st(V.tensor_tensor(dif[:, a], fo[:, a], sex[:, a], ALU.subtract))
            V.tensor_copy(sl_p[:, 0:1], iota_p[:, :])
            st(V.tensor_scalar(sl_p[:, 1:2], iota_p[:, :], float(P), None, ALU.add))
            for u in range(2):
                st(V.tensor_scalar(half32[:, a], stt[:, a], sl_p[:, u:u + 1], None, ALU.is_le, ALU.add,
                                   accum_out=ts_p[:, u:u + 1]))
            for u in range(2):
                st(V.scalar_tensor_tensor(half32[:, a], iota_f[:, a], ts_p[:, u:u + 1], dif[:, a],
                                          ALU.is_equal, ALU.mult, accum_out=gs_p[:, u:u + 1]))
            V.tensor_scalar(tsm, ts_p, float(P), None, ALU.mult)
            V.tensor_scalar(tsc, ts_p, float(NT - 1), None, ALU.min).then_inc(s_off, 1)
            st(V.tensor_tensor(gs_p, gs_p, sl_p, ALU.add))
            st(V.tensor_scalar(gs_p, gs_p, float(NG - 1), None, ALU.min))
            V.tensor_copy(gs_i, gs_p).then_inc(s_slot, 1)
            dve.wait_ge(s_offp, 2)
            st(V.tensor_copy(ts_row[:, :], ps[0:1, 7, 0:NSP]))

            dve.wait_ge(s_slg, 16 * 6)
            V.tensor_copy(fsrc, sl_src)
            for u in range(2):
                ins = V.tensor_scalar(fdl[:, u, :], sl_dst[:, u, :], tsm[:, u:u + 1], None, ALU.subtract)
            st(ins)
            V.tensor_copy(fdlb, fdl).then_inc(s_slf, 1)
            for u in range(2):
                dve.wait_ge(s_slt, u + 1)
                V.tensor_copy(tb[u][:, :, :, 0].bitcast(I32).rearrange("p s k -> p k s"),
                              psf[:, 0:TE * P].rearrange("p (k s) -> p k s", k=TE))
                V.tensor_copy(tb[u][:, :, :, 1:TW].rearrange("p s k w -> p w k s"),
                              psf[:, TE * P:TW * TE * P].rearrange("p (w k s) -> p w k s", w=TW - 1, k=TE))\
                    .then_inc(s_slc, 1)
            d3v = d3[:, :].rearrange("p (t h q) -> p t h q", h=GH, q=3)
            a_d = nas[:, :, GH:AH]
            r1 = dif2
            st(V.tensor_copy(d3v[:, :, :, 0], a_d))
            st(V.tensor_tensor(r1, a_d, d3v[:, :, :, 0], ALU.subtract))
            st(V.tensor_copy(d3v[:, :, :, 1], r1))
            st(V.tensor_tensor(r1, r1, d3v[:, :, :, 1], ALU.subtract))
            st(V.tensor_copy(d3v[:, :, :, 2], r1))
            dve.wait_ge(s_tab, 32)
            dve.wait_ge(s_dlst, 32)
            V.memset(acc[:, :], 0.0).then_inc(s_accz, 1)
            dve.wait_ge(s_accz, 1)

            def batch(b, u, i):
                dve.wait_ge(s_dl[u], 16 * i + 16)
                if late(b, 2):
                    dve.wait_ge(s_dp, b - 1)
                V.tensor_scalar(oht[u], dlb[u], iota_p[:, 0:1], None, ALU.is_equal).then_inc(s_oht, 1)
                dve.wait_ge(s_tl[u], 16 * i + 16)
                if late(b, 1):
                    dve.wait_ge(s_agg, b * SB)
                V.tensor_tensor(oh, under(iota_f[:, :], SB * TE), over(tab[u][:, :, 1], P), ALU.is_equal)
                dve.wait_ge(s_dp, b + 1)
                st(V.tensor_reduce(dv[u].rearrange("p k h -> p (k h)"),
                                   ps[:, u, 0:SB * TE * 12].rearrange("p (k q) -> p k q", q=3), X, ALU.add))
                dve.wait_ge(s_gg[u], 16 * SB * TE * i + 16 * SB * TE)
                V.tensor_tensor(a2[u][:, 0], dv[u], gb[u][:, :, D:D + GH], ALU.add)
                st(V.tensor_tensor(a2[u][:, 1], dv[u], tab[u][:, :, 2:2 + GH], ALU.add))
                st(V.scalar_tensor_tensor(lk[u].rearrange("p w k h -> p (w k h)"), a2[u].rearrange("p w k h -> p (w k h)"),
                                          0.2, a2[u].rearrange("p w k h -> p (w k h)"), ALU.mult, ALU.max))
                V.tensor_tensor(wl[u], lk[u][:, 0], lk[u][:, 1], ALU.subtract).then_inc(s_wl, 1)
                V.tensor_tensor(gb[u][:, :, D + GH:ACOL], tab[u][:, :, 2:2 + GH], over(tab[u][:, :, 2 + GH], GH), ALU.mult)\
                    .then_inc(s_tf[u], 1)
                dve.wait_ge(s_we, b + 1)
                m = gb[u][:, :, 0:D].rearrange("p k (h c) -> p k h c", c=GD)
                V.tensor_tensor(m, m, over(gb[u][:, :, D:D + GH], GD), ALU.mult).then_inc(s_msg, 1)
                for s in range(SB):
                    t = dve.value_load(ts_row[0:1, ds(b * SB + s, 1)], min_val=0, max_val=NT - 1)
                    dve.wait_ge(s_agg, b * SB + (s + 1))
                    if s or late(b, 1):
                        dve.wait_ge(s_accd, b * SB + s)
                    a = acc[:, ds(t * ACOL, ACOL)]
                    V.tensor_tensor(a, a, ps[:, 2 + s, 0:ACOL], ALU.add).then_inc(s_accd, 1)
            turns(NBT, 3, batch)

            dve.wait_ge(s_accd, NS)
            dve.wait_ge(s_agg, NS)
            accv = acc[:, :].rearrange("p (t c) -> p t c", c=ACOL)
            eden, emax = accv[:, :, D:D + GH], accv[:, :, D + GH:ACOL]
            a_s = nas[:, :, 0:GH]
            V.tensor_scalar(has, eden, 0.0, None, ALU.is_gt)
            V.tensor_tensor(mlog, emax, a_d, ALU.add)
            st(V.tensor_tensor(slog, a_s, a_d, ALU.add))
            V.scalar_tensor_tensor(f1, mlog, 0.2, mlog, ALU.mult, ALU.max)
            V.scalar_tensor_tensor(f2, slog, 0.2, slog, ALU.mult, ALU.max)
            st(V.tensor_scalar(has, has, -1.0, BIG, ALU.add, ALU.mult))
            st(V.tensor_tensor(f1, f1, has, ALU.add))
            st(V.tensor_tensor(mtop, f1, f2, ALU.max))
            V.tensor_tensor(dlog[:, 0], f1, mtop, ALU.subtract)
            V.tensor_tensor(dlog[:, 1], f2, mtop, ALU.subtract).then_inc(s_fin, 1)
            dve.wait_ge(s_fine, 1)
            st(V.tensor_tensor(den, eden, dexp[:, 0], ALU.mult))
            st(V.tensor_tensor(den, den, dexp[:, 1], ALU.add))
            st(V.reciprocal(den, den))
            V.tensor_tensor(f1, dexp[:, 0], den, ALU.mult)
            st(V.tensor_tensor(f2, dexp[:, 1], den, ALU.mult))

            def attend(t, u, i):
                dve.wait_ge(s_hl[u], 16 * i + 16)
                r = res[:, ds(t, 1), :].rearrange("p o (h c) -> p (o h) c", c=GD)
                tt = ds(t, 1)
                V.tensor_tensor(tm[0], accv[:, tt, 0:D].rearrange("p o (h c) -> p (o h) c", c=GD),
                                over(f1[:, tt, :].rearrange("p o h -> p (o h)"), GD), ALU.mult)
                V.tensor_tensor(tm[1], hb[u], over(f2[:, tt, :].rearrange("p o h -> p (o h)"), GD), ALU.mult)\
                    .then_inc(s_hf[u], 1)
                dve.wait_ge(s_hf[u], i + 1)
                st(V.tensor_tensor(r, r, tm[0], ALU.add))
                st(V.tensor_tensor(r, r, tm[1], ALU.add))
            turns(NT, 2, attend)

            for t in range(NT):
                ins = V.bn_stats(stats2[:, t, :], res[:, t, :])
            st(ins)
            for t in range(NT):
                ins = V.bn_aggr(mv2[:, t, :], stats2[:, t, :])
            st(ins)
            V.tensor_scalar(wait_w, mv2[:, :, 1], EPS_LN, None, ALU.add).then_inc(s_var2, 1)
            dve.wait_ge(s_sd2, 1)
            st(V.reciprocal(wait_w, wait_s))
            for t in range(NT):
                V.tensor_scalar(xn2[:, t, :], res[:, t, :], mv2[:, t, 0:1], wait_w[:, t:t + 1], ALU.subtract, ALU.mult)\
                    .then_inc(s_xn2, 1)

            V.tensor_copy(iota_e, iota_f[:, 0:NE])
            st(V.memset(zeros_e, 0.0))
            V.tensor_scalar(rowval, iota_p[:, :], float(TAIL), None, ALU.is_lt)
            dve.wait_ge(s_gs, NT)
            dve.wait_ge(s_gw, 32)
            st(V.tensor_tensor(gsc, ps[:, 7, 0:NX].rearrange("p (t e) -> p t e", e=NE), under(bgb, NT), ALU.add))
            for t in range(NT):
                ins = V.max(top[:, t, :], gsc[:, t, :])
            st(ins)
            for t in range(NT):
                ins = V.max_index(topi[:, t, :], top[:, t, :], gsc[:, t, :])
            st(ins)
            V.tensor_tensor(egap[:, :], top[:, :, 1], top[:, :, 0], ALU.subtract).then_inc(s_ez, 1)
            st(V.tensor_copy(ti, topi[:, :, 0:2]))
            for k in range(TOPK):
                ins = V.tensor_tensor(msk[k], under(iota_e, NT), over(ti[:, :, k], NE), ALU.is_equal)
            st(ins)
            for k in range(TOPK):
                ins = V.tensor_scalar(msk[k][:, NT - 1, :], msk[k][:, NT - 1, :], rowval[:, 0:1], None, ALU.mult)
            st(ins)
            V.tensor_tensor(msum, msk[0], msk[1], ALU.add).then_inc(s_sel, 1)
            dve.wait_ge(s_e2, 1)
            st(V.tensor_scalar(pr[0][:, :], eexp[:, :], 1.0, None, ALU.add))
            st(V.reciprocal(pr[0][:, :], pr[0][:, :]))
            st(V.tensor_tensor(pr[1][:, :], eexp[:, :], pr[0][:, :], ALU.mult))
            dve.wait_ge(s_pre, 1)
            tot = ps[:, 1, 0:NX].rearrange("p (t e) -> p t e", e=NE)
            for e in range(NE):
                ins = V.tensor_tensor_scan(cum[:, :, e], tot[:, :, e], zeros_e[:, 0:NT], 0.0, ALU.add, ALU.add)
            st(ins)
            st(V.tensor_tensor(pos, cum, tot, ALU.subtract))
            st(V.tensor_tensor(pos, pos, ps[:, 0, 0:NX].rearrange("p (t e) -> p t e", e=NE), ALU.add))
            st(V.tensor_scalar(nti, cum[:, NT - 1, :], float(P - 1), None, ALU.add))
            st(V.tensor_scalar(nti, nti, P.bit_length() - 1, None, ALU.logical_shift_right))
            st(V.tensor_copy(ntl, nti))
            st(V.tensor_tensor_scan(endj, ntl, zeros_e[:, 0:NE], 0.0, ALU.add, ALU.add))
            st(V.tensor_tensor(basej, endj, ntl, ALU.subtract))
            st(V.tensor_scalar(basej, basej, float(P), None, ALU.mult))
            st(V.tensor_tensor(pos, pos, under(basej, NT), ALU.add))
            st(V.tensor_scalar(cnt_e, endj, iota_p[:, 0:1], None, ALU.is_le, ALU.add, accum_out=ej))
            V.tensor_scalar(ejc, ej, float(NE - 1), None, ALU.min).then_inc(s_sel, 1)
            for k in range(TOPK):
                st(V.tensor_tensor(mp, msk[k], pos, ALU.mult))
                st(V.tensor_reduce(posf[k][:, :], mp, X, ALU.add))
                ins = V.tensor_copy(posi[k][:, :], posf[k][:, :])
            ins.then_inc(s_pos, 1)
            dve.wait_ge(s_ejp, 1)
            V.tensor_copy(ej_row[:, :], ps[0:1, 2, 0:P]).then_inc(s_ej, 1)

            dve.wait_ge(s_w2, 16 * (NE // 2 + 2))
            dve.wait_ge(s_sc, 16 * TOPK * NT)

            def expert(j, u, i):
                dve.wait_ge(s_f1, j + 1)
                if late(j, 2):
                    dve.wait_ge(s_fh, j - 1)
                V.tensor_copy(hs[u], psf[:, 512:512 + HID]).then_inc(s_f1c, 1)
                e = dve.value_load(ej_row[0:1, ds(j, 1)], min_val=0, max_val=NE - 1)
                dve.wait_ge(s_f2, j + 1)
                if late(j, 2):
                    dve.wait_ge(s_fy[u], 16 * i)
                V.tensor_tensor(ys[u], ps[:, 5 + u, 0:D], b2_s[:, ds(e, 1), :].rearrange("p o c -> p (o c)"), ALU.add)\
                    .then_inc(s_f2c, 1)
            dve.wait_ge(s_ej, 1)
            turns(NJ, 0, expert)

            for t in range(NT):
                u = t % 2
                dve.wait_ge(s_cg[u], 16 * TOPK * (t // 2 + 1))
                st(V.scalar_tensor_tensor(res[:, t, :], yg[u][0], pr[0][:, t:t + 1], res[:, t, :], ALU.mult, ALU.add))
                V.scalar_tensor_tensor(res[:, t, :], yg[u][1], pr[1][:, t:t + 1], res[:, t, :], ALU.mult, ALU.add)\
                    .then_inc(s_cm, 1)


def kernel(**inputs):
    import numpy as np
    import concourse.bacc as bacc
    from concourse.bass_utils import run_bass_kernel_spmd

    get = {k: np.asarray(v) for k, v in inputs.items()}

    def chunks(w):
        return w.reshape(-1, 128, w.shape[-1]).transpose(1, 0, 2)

    w1 = get["L0_ffn_W1"].transpose(0, 2, 1).reshape(NE, KD, P, HID).transpose(2, 0, 1, 3)
    w2 = get["L0_ffn_W2"].transpose(0, 2, 1).reshape(NE, HC, P, D).transpose(2, 0, 1, 3)
    arrays = {
        "x": get["x"], "src": get["src"], "dst": get["dst"],
        "wcat": chunks(np.concatenate([get["L0_gnn_W"], get["L0_mix_Wqkv"].T], axis=1)),
        "wgt": chunks(get["L0_gnn_W"].T),
        "att_src": get["L0_gnn_att_src"], "att_dst": get["L0_gnn_att_dst"], "gbias": get["L0_gnn_bias"],
        "bqkv": get["L0_mix_bqkv"], "wpt": chunks(get["L0_mix_Wproj"].T), "bproj": get["L0_mix_bproj"],
        "temp": get["L0_mix_temperature"].reshape(MH),
        "wg": chunks(get["L0_ffn_Wg"].T), "bg": get["L0_ffn_bg"],
        "w1": w1, "b1": get["L0_ffn_b1"].reshape(NE, HC, P).transpose(2, 0, 1).reshape(P, NE * HC),
        "w2": w2, "b2": get["L0_ffn_b2"],
    }
    nc = bacc.Bacc("TRN2", target_bir_lowering=False, num_devices=1)
    args, feed = [], {}
    for name, a in arrays.items():
        a = np.ascontiguousarray(a)
        feed[f"in_{name}"] = a
        args.append(nc.dram_tensor(f"in_{name}", a.shape, mybir.dt.from_np(a.dtype), kind="ExternalInput").ap())
    out = nc.dram_tensor("out", (N, D), F32, kind="ExternalOutput").ap()
    gps_layer(nc, *args, out)
    r = run_bass_kernel_spmd(nc, [feed], core_ids=[0])
    return r.results[0]["out"]
```

```python
from contextlib import ExitStack, contextmanager

import concourse.bass as bass
from concourse import mybir

F32 = mybir.dt.float32
I32 = mybir.dt.int32
U32 = mybir.dt.uint32
BF16 = mybir.dt.bfloat16
ALU = mybir.AluOpType
ACT = mybir.ActivationFunctionType
X = mybir.AxisListType.X
ds = bass.ds

P = 128
N = 3125
D = 256
E = 50000
GH, GD = 4, 64
MH, MD = 8, 32
NE, HID = 8, 1024
NT = -(-N // P)
TAIL = N - (NT - 1) * P
NP = NT * P
KD = D // P
HC = HID // P
AH = 2 * GH
HROW = D + GH
SQ = MD // 2
QC = P // MD
NQC = SQ // QC
NB = 8
BW = NP // NB
EP = 392
EPAD = EP * P
GE = 256
NG = EPAD // GE
NS = NG + NT - 1
TE = GE // P
NSP = 2 * P
SB = 2
NBT = NS // SB
assert NS % (2 * SB) == 0 and NG * GE == EPAD and BW * NB == NP
TW = 7
ACOL = D + 2 * GH
PAD_DST = 4096
BIG = 1e30
TOPK = 2
NJ = (TOPK * N + NE * (P - 1)) // P
NJ += NJ % 2
EPS_LN = 1e-5
EPS_N = 1e-12
QSCALE = float(MD) ** 0.25
assert NE == MH


class Steps:

    def __init__(self, eng, sem):
        self.eng, self.sem, self.n, self.i, self.per, self.k = eng, sem, 0, None, 0, 0

    def __call__(self, ins):
        self.eng.wait_ge(self.sem, self.mark(ins))

    def mark(self, ins):
        ins.then_inc(self.sem, 1)
        if self.i is None:
            self.n += 1
            return self.n
        self.k += 1
        return self.i * self.per + (self.n + self.k)

    @contextmanager
    def loop(self, first, end, per):
        self.n -= first * per
        with self.eng.Fori(first, end) as i:
            self.i, self.per, self.k = i, per, 0
            yield i
            assert self.k == per, (self.k, per)
        self.i = None
        self.n += end * per


def skewed(loop, n, w, parts):
    far = max(lag for _, lag in parts)

    def turn(i, q):
        for part, lag in parts:
            d = (q - lag) // w
            if isinstance(i, int):
                t = i * w + q - lag
                if 0 <= t < n:
                    part(t, t % w, t // w)
            else:
                part(i * w + (q - lag), (q - lag) % w, i + d if d else i)
    first, end = -(-(far + w) // w), n // w
    for i in range(first):
        for q in range(w):
            turn(i, q)
    with loop(first, end) as i:
        for q in range(w):
            turn(i, q)
    for i in range(end, -(-(n + far) // w)):
        for q in range(w):
            turn(i, q)


def gps_layer(nc, x, src, dst, wcat, wgt, att_src, att_dst, gbias, bqkv, wpt, bproj, temp,
              wg, bg, w1, b1, w2, b2, out):
    ctx = ExitStack()

    def sb(name, shape, dt=F32):
        return ctx.enter_context(nc.sbuf_tensor(name, shape, dt))

    def sem(name):
        return ctx.enter_context(nc.semaphore(name))

    def dram(name, shape, dt=F32):
        return nc.dram_tensor(name, shape, dt, kind="Internal").ap()

    def ap(t, off, pairs):
        return bass.AP(t.tensor, t.offset + off, pairs)

    def rows(t, n, w, off=0):
        return ap(t, off, [[0, n], [1, w]])

    with ctx:
        h_d = dram("h_d", [NP, HROW])
        as_d = dram("as_d", [NP, GH])
        src_d = dram("src_d", [NG, GE], I32)
        dst_d = dram("dst_d", [NG, GE], I32)
        max_d = dram("max_d", [NG, GE * (GH + 1)])
        dl_d = dram("dl_d", [NSP, GE], BF16)
        tab_d = dram("tab_d", [P, NSP * TE, TW])
        xs_d = dram("xs_d", [NJ * P, D])
        ys_d = dram("ys_d", [NJ * P, D])

        AW = 32000
        GW = 4000
        arena = sb("arena", [P, AW + GW])
        res = sb("res", [P, NT, D])
        acc = sb("acc", [P, NT * ACOL])
        identf = sb("identf", [P, P])
        identb = sb("identb", [P, P], BF16)
        onesf = sb("onesf", [P, P])
        lower = sb("lower", [P, P])
        blocks = sb("blocks", [P, P])
        iota_f = sb("iota_f", [P, P])
        iota_p = sb("iota_p", [P, 1])
        nas = sb("nas", [P, NT, AH])
        d3 = sb("d3", [P, NT * GH * 3], BF16)
        small = sb("small", [P, 700])

        A = arena[:, :]
        G = arena[:, AW:AW + GW]
        C = acc[:, :]
        S = small[:, :]

        def view(base, off, words, pat=None, **kw):
            v = base[:, off:off + words]
            return v.rearrange(pat, **kw) if pat else v

        kh = view(A, 0, NT * D, "p (t c) -> p t c", t=NT)
        vv = view(A, NT * D, NT * D, "p (t c) -> p t c", t=NT)
        qT = view(A, 2 * NT * D, KD * NP, "p (g n) -> p g n", g=KD)
        STK = 2 * NT * D + KD * NP
        stack = view(A, STK, MH * NP // 2).bitcast(BF16).rearrange("p (h n) -> p h n", h=MH)
        xn = [view(A, STK + u * D, D) for u in range(2)]
        qn = view(A, STK + NT * D, NT * D, "p (t c) -> p t c", t=NT)
        FW = SQ * MD
        kx = [view(A, STK + u * MH * 48, MH * 48) for u in range(2)]
        phi = [view(A, STK + 2 * MH * 48 + u * MH * FW, MH * FW, "p (h f) -> p h f", h=MH) for u in range(2)]
        f16, kb, vb = ([view(A, STK + 2 * MH * 48 + 2 * MH * FW + (2 * q + u) * D, D) for u in range(2)]
                       for q in range(3))
        split = [view(A, s * NP, NP).bitcast(BF16).rearrange("p (g n) -> p g n", g=KD) for s in range(3)]
        SPW = 800
        rem = view(A, 3 * NP, SPW)
        yT = view(A, 0, KD * NP, "p (g n) -> p g n", g=KD)
        ZB = 4
        zsq = [view(A, KD * NP + b * BW, BW) for b in range(ZB)]
        tq = [view(A, KD * NP + (ZB + b) * BW, BW) for b in range(2)]
        rden = [view(A, KD * NP + (ZB + 2 + b) * BW, BW) for b in range(2)]
        z16 = view(A, KD * NP + (ZB + 4) * BW, BW)
        MW = KD * NP + (ZB + 5) * BW
        wpt_s = view(A, MW, KD * D, "p (g c) -> p g c", g=KD)
        MW += KD * D

        def square():
            nonlocal MW
            MW += P
            return view(A, MW - P, P)

        coef = [[square() for g in range(KD)] for c in range(NQC)]
        cf16 = [square() for g in range(KD)]
        lin = [square() for g in range(KD)]
        gram = [square() for g in range(KD)]
        assert MW <= 2 * NT * D
        sk = [sb(f"sk{g}", [P, 1]) for g in range(KD)]
        sv = [sb(f"sv{g}", [P, 1]) for g in range(KD)]
        pairb = sb("pairb", [3 * MD, NQC, P], BF16)
        pair16 = sb("pair16", [3 * MD, MD], BF16)
        w1_s = view(A, 0, NE * KD * HID, "p (e k n) -> p e k n", e=NE, k=KD)
        w2_s = view(A, NE * KD * HID, NE * HC * D, "p (e c n) -> p e c n", e=NE, c=HC)

        wa_off = 0
        wcat_s = view(C, 0, KD * 1024, "p (k n) -> p k n", k=KD)
        wacc_s = view(C, 2048, KD * AH, "p (k n) -> p k n", k=KD)
        bqk_s = view(C, 2064, 2 * D)
        bv_s = view(C, 2576, D)
        bres_s = view(C, 2832, D)
        xT = [view(C, 3088 + u * D, KD * P, "p (k n) -> p k n", k=KD) for u in range(2)]
        hrow = [view(C, 3600 + u * 264, 264) for u in range(2)]
        qk = [view(C, 4128 + u * 512, 512, "p (h c) -> p h c", c=MD) for u in range(2)]
        qksq = [view(C, 5152 + u * 512, 512, "p (h c) -> p h c", c=MD) for u in range(2)]
        wgt_s = view(G, 0, KD * D, "p (k n) -> p k n", k=KD)
        att_s = view(G, 512, KD * AH, "p (k n) -> p k n", k=KD)
        stats = view(G, 600, NT * 6, "p (t s) -> p t s", s=6)
        mv = view(G, 760, NT * 2, "p (t s) -> p t s", s=2)
        rstd = view(G, 820, NT)
        ssq = [view(G, 860 + u * 16, 16) for u in range(2)]
        rn = [view(G, 900 + u * 16, 16) for u in range(2)]
        tempb = view(G, 940, MH)
        ssmin = view(G, 950, 2 * MH)
        dsc_i = view(C, 0, EP).bitcast(I32)
        src_i = view(C, EP, EP).bitcast(I32)
        dsc = view(C, 2 * EP, EP)
        fadd = view(C, 3 * EP, EP)
        badd = view(C, 4 * EP, EP)
        sco = view(C, 5 * EP, EP * GH, "p (e h) -> p e h", h=GH)
        mx5 = view(C, 5 * EP, EP * (GH + 1), "p (e h) -> p e h", h=GH + 1)
        fwd = view(C, 10 * EP, EP * GH, "p (e h) -> p e h", h=GH)
        rowv = view(C, 14 * EP, 8 * P, "p (q n) -> p q n", n=P)
        sl_src = view(C, 0, 2 * GE, "p (u w) -> p u w", u=2).bitcast(I32)
        sl_dst = view(C, 2 * GE, 2 * GE, "p (u w) -> p u w", u=2).bitcast(I32)
        sl_max = view(C, 4 * GE, 2 * GE * (GH + 1), "p (u w c) -> p u w c", u=2, c=GH + 1)
        tb = [view(G, 0, P * TE * TW, "p (s k w) -> p s k w", k=TE, w=TW),
              view(C, 14 * GE, P * TE * TW, "p (s k w) -> p s k w", k=TE, w=TW)]
        fsrc = view(G, P * TE * TW, 2 * GE, "p (u w) -> p u w", u=2)
        fdl = view(G, P * TE * TW + 2 * GE, 2 * GE, "p (u w) -> p u w", u=2)
        fdlb = view(G, P * TE * TW + 4 * GE, GE).bitcast(BF16).rearrange("p (u w) -> p u w", u=2)

        W2 = NE * KD * HID
        EL = 2
        BO = W2 + (NE - EL) * HC * D
        H = arena[:, BO:]
        NBUF = 4
        o = 0

        def batch_words(n, pat=None, count=2, **kw):
            nonlocal o
            o += count * n
            return [view(H, o - (u + 1) * n, n, pat, **kw) for u in range(count)]

        gb = batch_words(SB * TE * ACOL, "p (k c) -> p k c", NBUF, c=ACOL)
        oh = batch_words(SB * TE * P, "p (k v) -> p k v", v=P)
        oht = [v.bitcast(BF16) for v in batch_words(SB * TE * P // 2)]
        dlb = [v.bitcast(BF16) for v in batch_words(SB * TE * P // 2, count=NBUF)]
        tab = batch_words(SB * TE * TW, "p (k w) -> p k w", NBUF, w=TW)
        dv = batch_words(SB * TE * GH, "p (k h) -> p k h", h=GH)
        a2 = batch_words(2 * SB * TE * GH, "p (w k h) -> p w k h", w=2, h=GH)
        lk = batch_words(2 * SB * TE * GH, "p (w k h) -> p w k h", w=2, h=GH)
        wl = batch_words(SB * TE * GH, "p (k h) -> p k h", h=GH)
        assert o <= AW + GW - BO, o

        ts_row = sb("ts_row", [1, NSP], I32)
        ptick = sb("ptick", [1, 2])
        ej_row = sb("ej_row", [1, P], I32)
        QO = 2 * NT * D
        pd0 = view(A, QO, NQC * P)
        pd1 = view(A, QO + 512, NQC * P)
        pdm = view(A, QO + 1024, NQC * P)
        zrow = view(A, QO + 2048, D)
        pde = view(A, QO + 1536, MD)
        pdf = view(A, QO + 1600, 3 * MD)
        bres2 = view(C, 6200, D)
        zz = view(G, 3400, 512)
        rsd = view(G, 970, NT)
        ftc = [view(G, 1000 + g * 512, 512) for g in range(KD)]
        pn = [sb(f"pn{c}", [P, MD]) for c in range(NQC)]
        pn16 = sb("pn16", [P, MD])

        ps = ctx.enter_context(nc.psum_tensor("ps", [P, 8, 512], F32))
        psf = ps[:, :, :].rearrange("p b w -> p (b w)")
        psb = ps[:, 5, 0:256].bitcast(BF16)

        s_const = sem("constants_ready")
        s_x = sem("x_loaded")
        s_w = sem("projection_weights_loaded")
        s_att = sem("att_zeroed")
        s_attd = sem("att_loaded")
        v_step, a_step, g_step, p_step = sem("vector_steps"), sem("scalar_steps"), sem("gpsimd_steps"), sem("tensor_steps")
        s_wa = sem("score_weights_product")
        s_wac = sem("score_weights_ready")
        s_var = sem("variances_ready")
        s_sd = sem("deviations_ready")
        s_xn = sem("normalized_tiles")
        s_xt = sem("xn_transposed")
        s_xtc = sem("xn_transposed_in_sbuf")
        s_prj = sem("projected_tiles")
        s_prh = sem("h_psum_read")
        s_prv = sem("qkv_psum_read")
        s_hst = [sem(f"h_stored{u}") for u in range(2)]
        s_hrow = sem("h_row_in_sbuf")
        s_ss = sem("squared_norms")
        s_nrm = sem("norms")
        s_ast = sem("source_scores_stored")
        s_qn = sem("q_normalized")
        s_qt = sem("q_transposed")
        s_qtc = sem("q_transposed_in_sbuf")
        s_kx = sem("k_extended")
        s_kxr = sem("k_extended_read")
        s_phi = sem("pair_features")
        s_kv = sem("pair_features_used")
        s_kvd = sem("kv_sums_done")
        s_kvc = sem("kv_sums_in_sbuf")
        s_cft = sem("coefficients_transposed")
        s_cfc = sem("coefficients_in_sbuf")
        s_cf0 = sem("square_coefficients")
        s_cfd = sem("coefficients_done")
        s_pair = sem("pair_matrices")
        s_spl = [sem(f"split_part{g}") for g in range(KD)]
        s_stk = sem("stack_loaded")
        s_z = sem("pair_sums")
        s_zs = sem("pair_sums_squared")
        s_t = sem("gram_products")
        s_tq = sem("gram_terms")
        s_y = sem("mix_numerators")
        s_yT = sem("mix_outputs")
        s_zu = sem("squares_used")
        s_wpt = sem("output_weights_loaded")
        s_mo = sem("mix_projected")
        s_mor = sem("mix_added")
        s_ed = sem("edges_loaded")
        s_edc = sem("edge_padding_set")
        s_sg = [sem(f"scores_gathered{u}") for u in range(8)]
        s_sh = sem("neighbour_values_moved")
        s_shr = sem("chunk_values_ready")
        s_tr = sem("small_transposes")
        s_trc = sem("small_transposes_read")
        s_mxd = sem("maxima_stored")
        s_edst = sem("padded_edges_stored")
        s_off = sem("tile_offsets_counted")
        s_offp = sem("tile_offsets_summed")
        s_slot = sem("slot_tables_ready")
        s_slg = sem("slot_rows_gathered")
        s_slf = sem("slot_rows_converted")
        s_slt = sem("slot_rows_transposed")
        s_slc = sem("slot_words_placed")
        s_dlst = sem("local_destinations_stored")
        s_tab = sem("slot_words_stored")
        s_accz = sem("accumulator_cleared")
        s_tl = [sem(f"slot_words{u}") for u in range(NBUF)]
        s_dl = [sem(f"destination_rows{u}") for u in range(NBUF)]
        s_tick = sem("batch_word_written")
        s_gg = [sem(f"rows_gathered{u}") for u in range(NBUF)]
        s_oht = sem("onehot_rows")
        s_dp = sem("destination_scores")
        s_dv = sem("destination_scores_read")
        s_wl = sem("log_weights")
        s_we = sem("weights")
        s_msg = sem("messages")
        s_agg = sem("messages_summed")
        s_accd = sem("sums_added")
        s_w1 = sem("expert_weights_loaded")
        s_w2 = sem("late_expert_weights_loaded")
        s_hl = [sem(f"h_reloaded{u}") for u in range(2)]
        s_hf = [sem(f"h_reload_free{u}") for u in range(2)]
        s_fin = sem("final_exponents")
        s_fine = sem("final_weights")
        s_var2 = sem("variances2_ready")
        s_sd2 = sem("deviations2_ready")
        s_xn2 = sem("tokens_normalized")
        s_gt = sem("tokens_transposed")
        s_gtc = sem("tokens_transposed_in_sbuf")
        s_gs = sem("gate_scores")
        s_gsr = sem("gate_scores_read")
        s_gw = sem("gate_weights_loaded")
        s_sel = sem("experts_chosen")
        s_pre = sem("ranks_summed")
        s_e2 = sem("second_gate_exp")
        s_ez = sem("second_gate_gap")
        s_pos = sem("token_positions")
        s_ejp = sem("expert_row_product")
        s_ej = sem("expert_row_ready")
        s_zero = sem("token_slots_cleared")
        s_sc = sem("tokens_scattered")
        s_fx = [sem(f"expert_tokens{u}") for u in range(2)]
        s_ft = sem("expert_tokens_transposed")
        s_ftc = sem("expert_tokens_in_sbuf")
        s_w1c = sem("first_weights_copied")
        s_f1 = sem("hidden_products")
        s_fhc = sem("hidden_activated")
        s_f2 = sem("expert_products")
        s_f2c = sem("expert_results")
        s_fy = [sem(f"expert_results_stored{u}") for u in range(2)]
        s_cg = [sem(f"results_gathered{u}") for u in range(2)]
        s_cf = [sem(f"results_free{u}") for u in range(2)]
        s_cm = sem("outputs_combined")
        s_out = sem("outputs_stored")
        s_zrow = sem("zero_row_ready")
        s_zero_v = sem("zeros_ready")
        s_pairb = sem("pair_matrices_ready")
        s_pairT = sem("pair_matrices_transposed")
        s_z16 = sem("half_shift_sums")
        s_z16s = sem("half_shift_squares")
        s_dn = sem("denominators_summed")
        s_den = sem("denominators_read")

        o = 0

        def word(n, *shape, pat=None, **kw):
            nonlocal o
            v = view(S, o, n, pat, **kw)
            o += n
            return v

        cnt, offs, fo, co, nsl, stt, sex, dif = (word(32) for _ in range(8))
        tint = word(32).bitcast(I32)
        ts_p, gs_p, sl_p, tsm, tsc = (word(2) for _ in range(5))
        gs_i = word(2).bitcast(I32)
        chv = word(12, pat="p (q h) -> p q h", h=GH)
        cin = word(12, pat="p (q h) -> p q h", h=GH)
        iota_e, cnt_e, ntl, endj, basej = (word(NE) for _ in range(5))
        nti = word(NE).bitcast(I32)
        ej, ejc = word(1), word(1)
        half32 = word(32)
        junk = word(GE // 2)
        rowval = word(1)
        wait_w = word(NT)
        mv2 = word(2 * NT, pat="p (t s) -> p t s", s=2)
        assert o <= 700, o

        o = 800

        def tail(n, pat=None, **kw):
            nonlocal o
            v = view(G, o, n, pat, **kw)
            o += n
            return v

        NH = NT * GH
        has, mlog, slog, mtop, den, f1, f2 = (tail(NH, "p (t h) -> p t h", h=GH) for _ in range(7))
        dlog = tail(2 * NH, "p (w t h) -> p w t h", w=2, h=GH)
        dexp = tail(2 * NH, "p (w t h) -> p w t h", w=2, h=GH)
        hb = [tail(D, "p (h c) -> p h c", h=GH) for _ in range(2)]
        tm = [tail(D, "p (h c) -> p h c", h=GH) for _ in range(2)]
        stats2 = view(G, 800, NT * 6, "p (t s) -> p t s", s=6)
        o = 1000
        NX = NT * NE
        bgb = tail(NE)
        wg_s = tail(KD * NE, "p (k e) -> p k e", k=KD)
        gsc = tail(NX, "p (t e) -> p t e", e=NE)
        top = tail(NX, "p (t e) -> p t e", e=NE)
        topi = tail(NX, "p (t e) -> p t e", e=NE).bitcast(U32)
        ti = tail(NT * 2, "p (t e) -> p t e", e=2)
        msk = [tail(NX, "p (t e) -> p t e", e=NE) for _ in range(2)]
        msum = tail(NX, "p (t e) -> p t e", e=NE)
        cum = tail(NX, "p (t e) -> p t e", e=NE)
        pos = tail(NX, "p (t e) -> p t e", e=NE)
        mp = tail(NX, "p (t e) -> p t e", e=NE)
        zeros_e = tail(32)
        g2T = [tail(D, "p (k n) -> p k n", k=KD) for _ in range(2)]
        assert o <= GW, o
        wait_s = sb("deviations2", [P, NT])[:, :]
        dif2 = sb("dif2", [P, NT, GH])[:, :, :]
        egap = sb("egap", [P, NT])
        eexp = sb("eexp", [P, NT])
        pr = [sb(f"prob{k}", [P, NT]) for k in range(2)]
        posf = [sb(f"posf{k}", [P, NT]) for k in range(2)]
        posi = [sb(f"posi{k}", [P, NT], I32) for k in range(2)]
        b1_s = sb("b1_s", [P, NE * HC])
        xn2 = view(C, 0, NT * D, "p (t c) -> p t c", t=NT)
        xfT = [view(C, u * D, D, "p (k n) -> p k n", k=KD) for u in range(2)]
        xf = [view(C, 512 + u * D, D) for u in range(2)]
        HH = HID // 2
        w1c = [view(C, 1024 + u * KD * HH, KD * HH, "p (k n) -> p k n", k=KD) for u in range(2)]
        hT = [view(C, 3072 + u * HID, HID, "p (c n) -> p c n", c=HC) for u in range(2)]
        ys = [view(C, 5120 + u * D, D) for u in range(2)]
        b2_s = view(G, 1000, NE * D, "p (e c) -> p e c", e=NE)
        yg = [[view(C, (2 * u + k) * D, D) for k in range(2)] for u in range(2)]

        def bc(t, shape_pairs):
            return ap(t, 0, [list(t.ap[0])] + shape_pairs)

        def over(v, n):
            return ap(v, 0, [list(q) for q in v.ap] + [[0, n]])

        def under(v, n):
            q = [list(z) for z in v.ap]
            return ap(v, 0, [q[0], [0, n]] + q[1:])

        def back(v):
            (ps_, pn), (st, n) = v.ap
            return ap(v, st * (n - 1), [[ps_, pn], [-st, n]])

        def late(t, lag):
            return not isinstance(t, int) or t >= lag

        def in_pairs(fori, n, body):
            body(0, 0)
            body(1, 1)
            with fori(n // 2) as i:
                body(2 * i, 0)
                body(2 * i + 1, 1)
            if n % 2:
                body(n - 1, 0)

        def plain(eng):
            def fori(m):
                return eng.Fori(1, m)
            return fori

        xt = x[0:(NT - 1) * P, :].rearrange("(t p) c -> p t c", p=P)
        ot = out[0:(NT - 1) * P, :].rearrange("(t p) c -> p t c", p=P)

        block = ctx.enter_context(nc.Block())

        @block.sync
        def _(sp):
            sp.dma_start(wcat_s, wcat).then_inc(s_w, 16)
            sp.dma_start(wgt_s, wgt).then_inc(s_w, 16)
            sp.dma_start(bqk_s, rows(bqkv, P, 2 * D)).then_inc(s_w, 16)
            sp.dma_start(bv_s, rows(bqkv, P, D, 2 * D)).then_inc(s_w, 16)
            sp.dma_start(tempb, rows(temp, P, MH)).then_inc(s_w, 16)
            for c in range(4):
                a, b = c * 6, (c + 1) * 6
                sp.dma_start(res[:, a:b, :], xt[:, a:b, :]).then_inc(s_x, 16)
            sp.wait_ge(s_const, 1)
            sp.dma_start(res[0:TAIL, NT - 1, :], x[(NT - 1) * P:N, :]).then_inc(s_x, 16)
            sp.wait_ge(s_att, 1)
            for h in range(GH):
                q = GD * (h % 2)
                for w, a in ((0, att_src), (GH, att_dst)):
                    sp.dma_start(att_s[q:q + GD, h // 2, w + h:w + h + 1],
                                 a[h:h + 1, :].rearrange("a c -> c a")).then_inc(s_attd, 16)

            def store_h(t, u):
                sp.wait_ge(s_hrow, t + 1)
                sp.dma_start(h_d.rearrange("(t p) c -> t p c", p=P)[ds(t, 1)].rearrange("o p c -> (o p) c"),
                             hrow[u][:, 0:HROW]).then_inc(s_hst[u], 16)
            in_pairs(plain(sp), NT, store_h)
            sp.dma_start(as_d.rearrange("(t p) h -> p t h", p=P), nas[:, :, 0:GH]).then_inc(s_ast, 16)

            sp.wait_ge(s_edc, 2)
            full = E // EP
            for t, v in ((src, src_i), (dst, dsc_i)):
                sp.dma_start(v[0:full, :], t[0:full * EP].rearrange("(p e) -> p e", e=EP)).then_inc(s_ed, 16)
                sp.dma_start(v[full:full + 1, 0:E - full * EP],
                             t[full * EP:E].rearrange("(a e) -> a e", a=1)).then_inc(s_ed, 16)
            sp.wait_ge(s_ed, 64)
            sp.dma_start(src_d.rearrange("g w -> (g w)").rearrange("(p e) -> p e", e=EP), src_i).then_inc(s_edst, 16)
            sp.dma_start(dst_d.rearrange("g w -> (g w)").rearrange("(p e) -> p e", e=EP), dsc_i).then_inc(s_edst, 16)
            for g in range(KD):
                sp.wait_ge(s_spl[g], NP // SPW)
                for h in range(QC):
                    for s in range(3):
                        sp.dma_start(stack[s * MD:(s + 1) * MD, g * QC + h, :],
                                     split[s][h * MD:(h + 1) * MD, g, :]).then_inc(s_stk, 16)

            sp.dma_start(wpt_s, wpt).then_inc(s_wpt, 16)
            sp.wait_ge(s_shr, 1)
            sp.dma_start(max_d.rearrange("g w -> (g w)").rearrange("(p e) -> p e", p=P),
                         mx5.rearrange("p e h -> p (e h)")).then_inc(s_mxd, 16)
            sp.wait_ge(s_slf, 1)
            for u in range(2):
                sp.dma_start(dl_d[u * P:(u + 1) * P, :], fdlb[:, u, :]).then_inc(s_dlst, 16)
            for u in range(2):
                sp.wait_ge(s_slc, u + 1)
                sp.dma_start(tab_d[:, u * P * TE:(u + 1) * P * TE, :],
                             tb[u].rearrange("p s k w -> p (s k) w")).then_inc(s_tab, 16)

            sp.wait_ge(s_slt, 2)
            sp.wait_ge(s_tab, 32)
            sp.wait_ge(s_dlst, 32)

            def load_batch(b, u, i):
                if late(b, NBUF):
                    sp.wait_ge(s_msg, b - (NBUF - 1))
                sp.dma_start(tab[u], tab_d[:, ds(b * (SB * TE), SB * TE), :]).then_inc(s_tl[u], 16)
                d = dl_d[ds(b * SB, SB), :]
                sp.dma_start(dlb[u].rearrange("p (s e) -> p s e", s=SB),
                             bass.AP(d.tensor, d.offset, [[0, P], [GE, SB], [1, GE]])).then_inc(s_dl[u], 16)
            skewed(sp.Fori, NBT, NBUF, [(load_batch, 0)])

            sp.wait_ge(s_mor, NT)
            for e in range(NE):
                sp.dma_start(w1_s[:, e], w1[:, e]).then_inc(s_w1, 16)
                if e < NE - EL:
                    sp.dma_start(w2_s[:, e], w2[:, e]).then_inc(s_w1, 16)
            sp.wait_ge(s_accd, NS)
            for e in range(NE - EL, NE):
                sp.dma_start(w2_s[:, e], w2[:, e]).then_inc(s_w2, 16)
            sp.dma_start(b1_s[:, :], b1).then_inc(s_w2, 16)

            loop_i = [None]

            def reload_h(t, u):
                if late(t, 2):
                    sp.wait_ge(s_hf[u], (t - u) // 2 if isinstance(t, int) else loop_i[0])
                sp.dma_start(hb[u].rearrange("p h c -> p (h c)"),
                             h_d.rearrange("(t p) c -> t p c", p=P)[ds(t, 1)].rearrange("o p c -> (o p) c")[:, 0:D])\
                  .then_inc(s_hl[u], 16)
            reload_h(0, 0)
            reload_h(1, 1)
            with sp.Fori(1, NT // 2) as i:
                loop_i[0] = i
                reload_h(2 * i, 0)
                reload_h(2 * i + 1, 1)
            reload_h(NT - 1, 0)

            sp.wait_ge(s_var2, 1)
            sp.dma_start(bgb, rows(bg, P, NE)).then_inc(s_gw, 16)
            sp.dma_start(wg_s, wg).then_inc(s_gw, 16)
            sp.wait_ge(s_pos, 1)
            sp.dma_start(b2_s, ap(b2, 0, [[0, P], [D, NE], [1, D]])).then_inc(s_w2, 16)

            sp.wait_ge(s_sc, 16 * TOPK * NT)

            def load_tokens(j, u):
                if late(j, 2):
                    sp.wait_ge(s_ft, j - 1)
                sp.dma_start(xf[u], xs_d.rearrange("(t p) c -> t p c", p=P)[ds(j, 1)].rearrange("o p c -> (o p) c"))\
                  .then_inc(s_fx[u], 16)
            load_tokens(0, 0)
            load_tokens(1, 1)
            with sp.Fori(1, NJ // 2) as i:
                loop_i[0] = i
                load_tokens(2 * i, 0)
                load_tokens(2 * i + 1, 1)

            for t in range(NT):
                sp.wait_ge(s_cm, t + 1)
                if t < NT - 1:
                    sp.dma_start(ot[:, t, :], res[:, t, :]).then_inc(s_out, 16)
                else:
                    sp.dma_start(out[t * P:N, :], res[0:TAIL, t, :]).then_inc(s_out, 16)
            sp.wait_ge(s_out, 16 * NT)

        @block.gpsimd
        def _(pool):
            st = Steps(pool, g_step)
            pool.memset(res[:, NT - 1, :], 0.0).then_inc(s_const, 1)
            pool.memset(att_s, 0.0).then_inc(s_att, 1)
            pool.memset(identf[:, :], 0.0)
            st(pool.memset(onesf[:, :], 1.0))
            pool.affine_select(out=identf[:, :], in_=identf[:, :], compare_op=ALU.not_equal, fill=1.0,
                               base=0, pattern=[[-1, P]], channel_multiplier=1).then_inc(s_const, 1)
            pool.affine_select(out=lower[:, :], in_=onesf[:, :], compare_op=ALU.is_ge, fill=0.0,
                               base=-1, pattern=[[1, P]], channel_multiplier=-1).then_inc(s_const, 1)
            pool.iota(iota_f[:, :], pattern=[[1, P]], base=0, channel_multiplier=0,
                      allow_small_or_imprecise_dtypes=True).then_inc(s_const, 1)
            pool.iota(iota_p[:, :], pattern=[[0, 1]], base=0, channel_multiplier=1,
                      allow_small_or_imprecise_dtypes=True).then_inc(s_const, 1)
            pool.wait_ge(s_const, 5)
            for s in range(3):
                q = slice(s * MD, (s + 1) * MD)
                st(pool.iota(pd0[q].rearrange("p (c r i) -> p c r i", c=NQC, r=QC),
                             pattern=[[0, NQC], [0, QC], [1, MD]], base=0, channel_multiplier=-1,
                             allow_small_or_imprecise_dtypes=True))
                st(pool.iota(pd1[q].rearrange("p (c r i) -> p c r i", c=NQC, r=QC),
                             pattern=[[QC, NQC], [1, QC], [1, MD]], base=0, channel_multiplier=-1,
                             allow_small_or_imprecise_dtypes=True))
                pool.iota(pde[q], pattern=[[1, MD]], base=0, channel_multiplier=-1,
                          allow_small_or_imprecise_dtypes=True).then_inc(s_pair, 1)
                pool.wait_ge(s_pair, s + 1)

            pool.wait_ge(s_ast, 16)
            pool.wait_ge(s_ed, 64)
            for j in range(EP):
                pool.indirect_dma_start(sco[:, j, :], None, as_d, bass.IndirectOffsetOnAxis(src_i[:, j:j + 1], 0))\
                    .then_inc(s_sg[j % 8], 16)

            pool.wait_ge(s_slot, 1)
            pool.wait_ge(s_edst, 32)
            pool.wait_ge(s_mxd, 16)
            for u in range(2):
                idx = bass.IndirectOffsetOnAxis(gs_i[:, u:u + 1], 0)
                pool.indirect_dma_start(sl_src[:, u, :], None, src_d, idx).then_inc(s_slg, 16)
                pool.indirect_dma_start(sl_dst[:, u, :], None, dst_d, idx).then_inc(s_slg, 16)
                pool.indirect_dma_start(sl_max[:, u].rearrange("p w c -> p (w c)"), None, max_d, idx).then_inc(s_slg, 16)

            for u in range(2):
                pool.wait_ge(s_hst[u], 16 * ((NT + 1 - u) // 2))

            st(pool.memset(ptick[:, :], 0.0))

            def gather(b, u, i):
                if late(b, 1):
                    pool.wait_ge(s_tick, b)
                if late(b, NBUF):
                    pool.wait_ge(s_agg, b * SB - SB * (NBUF - 1))
                pool.wait_ge(s_tl[u], 16 * i + 16)
                pool.tensor_tensor(ptick[:, 1:2], ptick[:, 0:1], ptick[:, 0:1], ALU.add).then_inc(s_tick, 1)
                for k in range(SB * TE):
                    pool.indirect_dma_start(gb[u][:, k, 0:HROW], None, h_d,
                                            bass.IndirectOffsetOnAxis(tab[u][:, k, 0:1].bitcast(I32), 0))\
                        .then_inc(s_gg[u], 16)
            skewed(pool.Fori, NBT, NBUF, [(gather, 0)])

            pool.wait_ge(s_zero, 16)
            pool.wait_ge(s_pos, 1)
            for t in range(NT):
                n = P if t < NT - 1 else TAIL
                for k in range(TOPK):
                    pool.indirect_dma_start(xs_d, bass.IndirectOffsetOnAxis(posi[k][0:n, t:t + 1], 0),
                                            xn2[0:n, t, :], None).then_inc(s_sc, 16)
            for u in range(2):
                pool.wait_ge(s_fy[u], 16 * (NJ // 2))
            for t in range(NT):
                u = t % 2
                if t >= 2:
                    pool.wait_ge(s_cm, t - 1)
                for k in range(TOPK):
                    pool.indirect_dma_start(yg[u][k], None, ys_d, bass.IndirectOffsetOnAxis(posi[k][:, t:t + 1], 0))\
                        .then_inc(s_cg[u], 16)

        @block.scalar
        def _(act):
            A_ = nc.scalar
            it = [None]

            def turns(n, w, *parts):
                skewed(act.Fori, n, w, parts)

            act.wait_ge(s_zrow, 1)
            act.dma_start(xs_d.rearrange("(j p) c -> p j c", p=P), ap(zrow, 0, [list(zrow.ap[0]), [0, NJ], [1, D]]))\
               .then_inc(s_zero, 16)
            act.wait_ge(s_wa, 1)
            act.copy(wacc_s, ps[:, 7, 0:KD * AH].rearrange("p (k n) -> p k n", k=KD)).then_inc(s_wac, 1)
            act.dma_start(bres_s, rows(gbias, P, D)).then_inc(s_w, 16)
            act.dma_start(bres2, rows(bproj, P, D)).then_inc(s_w, 16)
            act.wait_ge(s_var, 1)
            A_.activation(rsd, rstd, ACT.Sqrt).then_inc(s_sd, 1)

            def project(t, u, i):
                act.wait_ge(s_xt, t + 1)
                if late(t, 2):
                    act.wait_ge(s_prj, t - 1)
                A_.copy(xT[u], ps[:, 6 + u, 0:D].rearrange("p (k n) -> p k n", k=KD)).then_inc(s_xtc, 1)

            def rows_out(t, u, i):
                act.wait_ge(s_prj, t + 1)
                if late(t, 2):
                    act.wait_ge(s_hst[u], 16 * i)
                A_.copy(nas[:, ds(t, 1), :].rearrange("p o c -> p (o c)"), ps[:, 3 * u, D:D + AH])
                A_.copy(hrow[u], ps[:, 3 * u, 0:264]).then_inc(s_hrow, 1)

            def norms(t, u, i):
                act.wait_ge(s_ss, t + 1)
                if late(t, 2):
                    act.wait_ge(s_qn, t - 1)
                A_.activation(rn[u], ssq[u], ACT.Sqrt).then_inc(s_nrm, 1)

            turns(NT, 2, (project, 0), (rows_out, 2), (norms, 3))

            def q_out(t, u, i):
                act.wait_ge(s_qt, t + 1)
                if isinstance(t, int) and t == 0:
                    act.wait_ge(s_zero, 16)
                A_.copy(qT[:, :, ds(t * P, P)], ps[:, 6 + u, 0:D].rearrange("p (g n) -> p g n", g=KD))\
                  .then_inc(s_qtc, 1)
            turns(NT, 2, (q_out, 0))

            def extend(t, u, i):
                if late(t, 2):
                    act.wait_ge(s_kv, t - 1)
                v = kx[u].rearrange("p (h c) -> p h c", h=MH)
                k = kh[:, ds(t, 1), :].rearrange("p o (h c) -> p (o h) c", c=MD)
                A_.copy(v[:, :, 0:MD], k)
                A_.copy(kb[u], kh[:, ds(t, 1), :].rearrange("p o c -> p (o c)"))
                A_.copy(vb[u], vv[:, ds(t, 1), :].rearrange("p o c -> p (o c)"))
                A_.copy(v[:, :, MD:MD + SQ], k[:, :, 0:SQ]).then_inc(s_kx, 1)
            act.wait_ge(s_qn, NT)
            act.wait_ge(s_prv, NT)
            act.wait_ge(s_qt, NT)
            turns(NT, 2, (extend, 0))

            act.wait_ge(s_cfd, 1)
            n = 0
            for b in range(NB):
                for g in range(KD):
                    for c in range(NQC):
                        for h in range(QC):
                            act.wait_ge(s_z, n + 1)
                            if n >= ZB:
                                act.wait_ge(s_zu, n - ZB + 1)
                            A_.activation(zsq[n % ZB], ps[:, n % 2, 0:BW], ACT.Square).then_inc(s_zs, 1)
                            n += 1
                    act.wait_ge(s_z16, b * KD + g + 1)
                    if b * KD + g >= 1:
                        act.wait_ge(s_y, b * KD + g)
                    A_.activation(z16, ps[:, 2, 0:BW], ACT.Square).then_inc(s_z16s, 1)

            def weigh(b, u, i):
                act.wait_ge(s_wl, b + 1)
                A_.activation(gb[u][:, :, D:D + GH], wl[u % 2], ACT.Exp).then_inc(s_we, 1)
            turns(NBT, NBUF, (weigh, 0))

            act.wait_ge(s_fin, 1)
            A_.activation(dexp, dlog, ACT.Exp).then_inc(s_fine, 1)
            act.wait_ge(s_var2, 1)
            A_.activation(wait_s, wait_w, ACT.Sqrt).then_inc(s_sd2, 1)

            def tokens_T(t, u, i):
                act.wait_ge(s_gt, t + 1)
                if late(t, 2):
                    act.wait_ge(s_gs, t - 1)
                A_.copy(g2T[u], ps[:, 5 + u, 0:D].rearrange("p (k n) -> p k n", k=KD)).then_inc(s_gtc, 1)
            turns(NT, 2, (tokens_T, 0))
            act.wait_ge(s_ez, 1)
            A_.activation(eexp[:, :], egap[:, :], ACT.Exp).then_inc(s_e2, 1)

            act.wait_ge(s_w2, 16 * (EL + 2))

            def tokens_T2(j, u, i):
                act.wait_ge(s_ft, j + 1)
                if late(j, 2):
                    act.wait_ge(s_f1, 2 * j - 2)
                A_.copy(xfT[u], ps[:, 7 * u, 0:D].rearrange("p (k n) -> p k n", k=KD)).then_inc(s_ftc, 1)

            def hidden(j, u, i):
                ej = act.value_load(ej_row[0:1, ds(j, 1)], min_val=0, max_val=NE - 1)
                if late(j, 2):
                    act.wait_ge(s_f2, j - 1)
                for n_ in range(2):
                    act.wait_ge(s_f1, 2 * j + (1 + n_))
                    for c in range(n_ * HC // 2, (n_ + 1) * HC // 2):
                        last = A_.activation(hT[u][:, c, :], ps[:, 1 + 2 * u + n_, (c % 4) * P:(c % 4 + 1) * P], ACT.Relu,
                                             bias=b1_s[:, ds(ej * HC + c, 1)])
                last.then_inc(s_fhc, 1)

            def store_y(j, u, i):
                act.wait_ge(s_f2c, j + 1)
                act.dma_start(ys_d.rearrange("(t p) c -> t p c", p=P)[ds(j, 1)].rearrange("o p c -> (o p) c"), ys[u])\
                   .then_inc(s_fy[u], 16)
            act.wait_ge(s_ej, 1)
            turns(NJ, 2, (tokens_T2, 0), (hidden, 1), (store_y, 3))
            for u in range(2):
                act.wait_ge(s_fy[u], 16 * (NJ // 2))

        @block.tensor
        def _(pe):
            MM, TR = nc.tensor.matmul, nc.tensor.transpose

            def turns(n, w, *parts):
                skewed(pe.Fori, n, w, parts)

            pe.wait_ge(s_w, 16 * 5)
            pe.wait_ge(s_attd, 16 * AH)
            for k in range(KD):
                for c in range(KD):
                    last = MM(ps[:, 7, k * AH:(k + 1) * AH], wgt_s[:, c, k * P:(k + 1) * P], att_s[:, c, :],
                              start=(c == 0), stop=(c == KD - 1))
            last.then_inc(s_wa, 1)
            pe.wait_ge(s_pairb, 1)
            for c in range(NQC):
                last = TR(psb[:, c * MD:(c + 1) * MD], pairb[0:MD, c, :], identb[0:MD, 0:MD])
            last.then_inc(s_pairT, 1)
            pe.wait_ge(s_wac, 1)

            def transpose_x(t, u, i):
                pe.wait_ge(s_xn, t + 1)
                if late(t, 2):
                    pe.wait_ge(s_xtc, t - 1)
                for k in range(KD):
                    last = TR(ps[:, 6 + u, k * P:(k + 1) * P],
                              xn[u][:, k * P:(k + 1) * P], identf[:, :])
                last.then_inc(s_xt, 1)

            def project(t, u, i):
                pe.wait_ge(s_xtc, t + 1)
                if late(t, 2):
                    pe.wait_ge(s_hrow, t - 1)
                    pe.wait_ge(s_prv, t - 1)
                for o_, w, s in ((ps[:, 3 * u, 0:D], wcat_s, slice(0, D)), (ps[:, 3 * u, D:D + AH], wacc_s, slice(0, AH)),
                                 (ps[:, 3 * u + 1, :], wcat_s, slice(D, 3 * D)),
                                 (ps[:, 3 * u + 2, 0:D], wcat_s, slice(3 * D, 4 * D))):
                    for k in range(KD):
                        last = MM(o_, xT[u][:, k, :], w[:, k, s], start=(k == 0), stop=(k == KD - 1))
                last.then_inc(s_prj, 1)
            turns(NT, 2, (transpose_x, 0), (project, 1))

            def q_T(t, u):
                pe.wait_ge(s_qn, t + 1)
                if late(t, 2):
                    pe.wait_ge(s_qtc, t - 1)
                for g in range(KD):
                    last = TR(ps[:, 6 + u, g * P:(g + 1) * P],
                              qn[:, t, g * P:(g + 1) * P], identf[:, :])
                last.then_inc(s_qt, 1)
            pe.wait_ge(s_xtc, NT)
            for t in range(NT):
                q_T(t, t % 2)

            pe.wait_ge(s_prv, NT)
            pe.wait_ge(s_hrow, NT)
            pe.wait_ge(s_zero_v, 1)
            for g in range(4):
                MM(ps[:, g, :], zz[:, 0:P], zz, start=True, stop=False, skip_group_check=True)

            def sums(t, u, n=P, final=False):
                pe.wait_ge(s_phi, t + 1)
                for g in range(KD):
                    k_ = kb[u][0:n, g * P:(g + 1) * P]
                    v_ = vb[u][0:n, g * P:(g + 1) * P]
                    f_ = f16[u][0:n, g * P:(g + 1) * P]
                    for h in range(QC):
                        MM(ps[h * MD:(h + 1) * MD, g, :],
                           v_[:, h * MD:(h + 1) * MD],
                           phi[u][0:n, g * QC + h, :], start=False, stop=final, skip_group_check=True)
                    b = ps[:, 2 + g, :]
                    kw = dict(start=False, stop=final, skip_group_check=True)
                    MM(b[:, 0:P], k_, v_, **kw)
                    MM(b[:, P:2 * P], k_, k_, **kw)
                    MM(b[:, 2 * P:3 * P], f_, v_, **kw)
                    MM(b[:, 3 * P:3 * P + 1], k_, onesf[0:n, 0:1], **kw)
                    last = MM(b[:, 3 * P + 1:3 * P + 2], v_, onesf[0:n, 0:1], **kw)
                last.then_inc(s_kv, 1)
            sums(0, 0)
            sums(1, 1)
            with pe.Fori(1, NT // 2) as i:
                sums(2 * i, 0)
                sums(2 * i + 1, 1)
            sums(NT - 1, 0, TAIL, True)

            pe.wait_ge(s_kvc, 1)
            for c in range(NQC):
                for g in range(KD):
                    last = TR(ps[:, 4 + g, c * P:(c + 1) * P], ftc[g][:, c * P:(c + 1) * P], identf[:, :])
            last.then_inc(s_cft, 1)
            pe.wait_ge(s_cfc, 1)
            for g in range(KD):
                for c in range(NQC):
                    MM(ps[0:MD, 6, g * P:(g + 1) * P], pn[c][:, :], coef[c][g], start=(c == 0), stop=False)
                last = MM(ps[0:MD, 6, g * P:(g + 1) * P], pn16[:, :], cf16[g], start=False, stop=True)
            last.then_inc(s_cf0, 1)

            pe.wait_ge(s_cfd, 1)
            pe.wait_ge(s_stk, 16 * 3 * MH)
            n = 0
            lag = []

            def use(m, h, g, c):
                pe.wait_ge(s_zs, m + 1)
                MM(ps[h * MD:(h + 1) * MD, 3 + g, 0:BW], coef[c][g][:, h * MD:(h + 1) * MD], zsq[m % ZB],
                   start=(c == 0), stop=False, skip_group_check=True).then_inc(s_zu, 1)
            for b in range(NB):
                col = slice(b * BW, (b + 1) * BW)
                for g in range(KD):
                    r = b * KD + g
                    if r >= KD:
                        pe.wait_ge(s_yT, r - KD + 1)
                    MM(ps[:, 5, 0:BW], gram[g], qT[:, g, col], start=True, stop=True).then_inc(s_t, 1)
                    if r >= 1:
                        pe.wait_ge(s_z16s, r)
                    for h in range(QC):
                        last = MM(ps[h * MD:(h + 1) * MD, 2, 0:BW], pair16[:, :], stack[0:3 * MD, g * QC + h, col],
                                  start=True, stop=True)
                    last.then_inc(s_z16, 1)
                    for c in range(NQC):
                        for h in range(QC):
                            if n >= 2:
                                pe.wait_ge(s_zs, n - 1)
                            MM(ps[:, n % 2, 0:BW], pairb[:, c, :], stack[0:3 * MD, g * QC + h, col],
                               start=True, stop=True).then_inc(s_z, 1)
                            lag.append((n, h, g, c))
                            n += 1
                            if len(lag) > 1:
                                use(*lag.pop(0))
                    while lag:
                        use(*lag.pop(0))
                    pe.wait_ge(s_z16s, r + 1)
                    MM(ps[:, 3 + g, 0:BW], cf16[g], z16, start=False, stop=False, skip_group_check=True)
                    MM(ps[:, 3 + g, 0:BW], lin[g], qT[:, g, col], start=False, stop=True, skip_group_check=True)\
                        .then_inc(s_y, 1)
                    pe.wait_ge(s_tq, r + 1)
                    if r >= 1:
                        pe.wait_ge(s_den, r)
                    MM(ps[:, 6, 0:BW], blocks[:, :], tq[r % 2], start=True, stop=True).then_inc(s_dn, 1)

            pe.wait_ge(s_yT, NB * KD)
            pe.wait_ge(s_wpt, 16)

            def mix_out(t, u):
                if late(t, 2):
                    pe.wait_ge(s_mor, t - 1)
                for g in range(KD):
                    last = MM(ps[:, u, 0:D], yT[:, g, ds(t * P, P)], wpt_s[:, g, :], start=(g == 0), stop=(g == KD - 1))
                last.then_inc(s_mo, 1)
            for t in range(NT):
                mix_out(t, t % 2)

            for d in range(2):
                pe.wait_ge(s_sh, 2 * d + 1)
                for q in range(3):
                    last = TR(ps[0:GH, 7, q * P:(q + 1) * P], chv[:, q, :], identf[:, :])
                last.then_inc(s_tr, 1)
                pe.wait_ge(s_sh, 2 * d + 2)
                for q in range(2):
                    last = TR(ps[:, 7, 3 * P + q * GH:3 * P + (q + 1) * GH], rowv[0:GH, 6 + q, :], identf[0:GH, 0:GH])
                last.then_inc(s_tr, 1)
            pe.wait_ge(s_off, 1)
            MM(ps[:, 7, 0:32], onesf[:, :], cnt, start=True, stop=True).then_inc(s_offp, 1)
            pe.wait_ge(s_off, 2)
            for u in range(2):
                last = MM(ps[0:1, 7, u * P:(u + 1) * P], tsc[:, u:u + 1], identf[:, :], start=True, stop=True)
            last.then_inc(s_offp, 1)
            pe.wait_ge(s_slf, 1)
            for u in range(2):
                if u:
                    pe.wait_ge(s_slc, u)
                for m in range(TE * TW):
                    w, k = m // TE, m % TE
                    if w == 0:
                        v = fsrc[:, u, k * P:(k + 1) * P]
                    elif w == 1:
                        v = fdl[:, u, k * P:(k + 1) * P]
                    else:
                        v = sl_max[:, u, k * P:(k + 1) * P, w - 2]
                    last = TR(ps[:, m // 4, (m % 4) * P:(m % 4 + 1) * P], v, identf[:, :])
                last.then_inc(s_slt, 1)

            pe.wait_ge(s_accz, 1)

            def scores(b, u, i):
                pe.wait_ge(s_oht, b + 1)
                if late(b, 2):
                    pe.wait_ge(s_dv, b - 1)
                for s in range(SB):
                    t = pe.value_load(ts_row[0:1, ds(b * SB + s, 1)], min_val=0, max_val=NT - 1)
                    for k in range(TE):
                        m = s * TE + k
                        last = MM(ps[:, u % 2, m * 12:(m + 1) * 12], oht[u % 2][:, m * P:(m + 1) * P],
                                  d3[:, ds(t * 12, 12)], start=True, stop=True)
                last.then_inc(s_dp, 1)

            def aggregate(b, u, i):
                pe.wait_ge(s_msg, b + 1)
                if late(b, 2):
                    pe.wait_ge(s_accd, b * SB - SB)
                for s in range(SB):
                    for k in range(TE):
                        m = s * TE + k
                        last = MM(ps[:, 2 + u % 2 * SB + s, 0:ACOL], oh[u % 2][:, m, :], gb[u][:, m, :],
                                  start=(k == 0), stop=(k == TE - 1))
                    last.then_inc(s_agg, 1)

            turns(NBT, NBUF, (scores, 0), (aggregate, 2))

            pe.wait_ge(s_gw, 32)

            def gate(t, u):
                pe.wait_ge(s_xn2, t + 1)
                if late(t, 2):
                    pe.wait_ge(s_gtc, t - 1)
                for k in range(KD):
                    last = TR(ps[:, 5 + u, k * P:(k + 1) * P],
                              xn2[:, t, k * P:(k + 1) * P], identf[:, :])
                last.then_inc(s_gt, 1)
                pe.wait_ge(s_gtc, t + 1)
                for k in range(KD):
                    last = MM(ps[:, 7, ds(t * NE, NE)], g2T[u][:, k, :], wg_s[:, k, :], start=(k == 0), stop=(k == KD - 1))
                last.then_inc(s_gs, 1)
            for t in range(NT):
                gate(t, t % 2)
            pe.wait_ge(s_sel, 1)
            MM(ps[:, 0, 0:NX], lower[:, :], msum.rearrange("p t e -> p (t e)"), start=True, stop=True)
            MM(ps[:, 1, 0:NX], onesf[:, :], msum.rearrange("p t e -> p (t e)"), start=True, stop=True).then_inc(s_pre, 1)
            pe.wait_ge(s_sel, 2)
            MM(ps[0:1, 2, 0:P], ejc, identf[:, :], start=True, stop=True).then_inc(s_ejp, 1)

            pe.wait_ge(s_ej, 1)
            pe.wait_ge(s_w1, 16 * (NE + NE - EL))
            pe.wait_ge(s_w2, 16 * (EL + 2))

            def tokens_T2(j, u, i):
                pe.wait_ge(s_fx[u], 16 * i + 16)
                if late(j, 2):
                    pe.wait_ge(s_ftc, j - 1)
                for k in range(KD):
                    last = TR(ps[:, 7 * u, k * P:(k + 1) * P], xf[u][:, k * P:(k + 1) * P], identf[:, :])
                last.then_inc(s_ft, 1)

            def hidden(j, u, i):
                pe.wait_ge(s_ftc, j + 1)
                if late(j, 2):
                    pe.wait_ge(s_fhc, j - 1)
                for n_ in range(2):
                    pe.wait_ge(s_w1c, 2 * j + (1 + n_))
                    for c in range(HC // 2):
                        for k in range(KD):
                            last = MM(ps[:, 1 + 2 * u + n_, c * P:(c + 1) * P], w1c[n_][:, k, c * P:(c + 1) * P],
                                      xfT[u][:, k, :], start=(k == 0), stop=(k == KD - 1))
                    last.then_inc(s_f1, 1)

            def results(j, u, i):
                e = pe.value_load(ej_row[0:1, ds(j, 1)], min_val=0, max_val=NE - 1)
                pe.wait_ge(s_fhc, j + 1)
                if late(j, 2):
                    pe.wait_ge(s_f2c, j - 1)
                for c in range(HC):
                    last = MM(ps[:, 5 + u, 0:D], hT[u][:, c, :],
                              w2_s[:, ds(e, 1), c, :].rearrange("p o n -> p (o n)"), start=(c == 0), stop=(c == HC - 1))
                last.then_inc(s_f2, 1)
            turns(NJ, 2, (tokens_T2, 0), (hidden, 1), (results, 2))

        @block.vector
        def _(dve):
            V = nc.vector
            st = Steps(dve, v_step)

            def turns(n, w, per, *parts):
                skewed(lambda first, end: st.loop(first, end, per), n, w, parts)

            V.memset(zrow, 0.0).then_inc(s_zrow, 1)
            V.memset(zz, 0.0).then_inc(s_zero_v, 1)
            V.memset(ssmin[:, 0:MH], (EPS_N / QSCALE) ** 2)
            V.memset(ssmin[:, MH:2 * MH], EPS_N ** 2)
            st(V.memset(blocks[:, :], 0.0))
            for h in range(QC):
                V.memset(blocks[h * MD:(h + 1) * MD, h * MD:(h + 1) * MD], 1.0)
            dve.wait_ge(s_const, 5)
            V.tensor_copy(identb[:, :], identf[:, :])
            dve.wait_ge(s_pair, 3)
            q = slice(0, 3 * MD)
            V.tensor_scalar(pdm[q], pd1[q], 0.0, None, ALU.is_equal)
            st(V.tensor_scalar(pd0[q], pd0[q], 0.0, None, ALU.is_equal))
            st(V.tensor_tensor(pd0[q], pd0[q], pdm[q], ALU.max))
            st(V.tensor_scalar(pdm[q], pd1[q], float(MD), None, ALU.is_equal))
            V.tensor_tensor(pairb[:, :, :].rearrange("p c f -> p (c f)"), pd0[0:3 * MD], pdm[0:3 * MD], ALU.max)\
                .then_inc(s_pairb, 1)
            dve.wait_ge(s_pairb, 1)
            V.tensor_scalar(pdf[q, 0:MD], pde[q, 0:MD], 0.0, None, ALU.is_equal)
            V.tensor_scalar(pdf[q, MD:2 * MD], pde[q, 0:MD], float(SQ), None, ALU.is_equal)
            st(V.tensor_scalar(pdf[q, 2 * MD:3 * MD], pde[q, 0:MD], float(-SQ), None, ALU.is_equal))
            st(V.tensor_tensor(pdf[q, 0:MD], pdf[q, 0:MD], pdf[q, MD:2 * MD], ALU.max))
            st(V.tensor_tensor(pair16[:, :], pdf[q, 0:MD], pdf[q, 2 * MD:3 * MD], ALU.max))
            for h in range(QC):
                V.tensor_scalar(pn16[h * MD:(h + 1) * MD, :], pair16[0:MD, :], -1.0, None, ALU.mult)
            dve.wait_ge(s_pairT, 1)
            for c in range(NQC):
                ins = V.tensor_scalar(pn[c][:, :], psb[:, c * MD:(c + 1) * MD], -1.0, None, ALU.mult)
            st(ins)
            st(V.tensor_copy(pn[0][0:MD, :], identf[0:MD, 0:MD]))

            dve.wait_ge(s_x, 16 * 5)
            for t in range(NT):
                ins = V.bn_stats(stats[:, t, :], res[:, t, :])
            st(ins)
            for t in range(NT):
                ins = V.bn_aggr(mv[:, t, :], stats[:, t, :])
            st(ins)
            V.tensor_scalar(rstd, mv[:, :, 1], EPS_LN, None, ALU.add).then_inc(s_var, 1)
            dve.wait_ge(s_sd, 1)
            st(V.reciprocal(rstd, rsd))
            dve.wait_ge(s_w, 16 * 7)

            def normalize(t, u, i):
                if late(t, 2):
                    dve.wait_ge(s_xt, t - 1)
                tt = ds(t, 1)
                V.tensor_scalar(xn[u], res[:, tt, :].rearrange("p o c -> p (o c)"),
                                mv[:, tt, 0], rstd[:, tt], ALU.subtract, ALU.mult).then_inc(s_xn, 1)

            def heads(t, u, i):
                dve.wait_ge(s_prj, t + 1)
                if late(t, 2):
                    dve.wait_ge(s_nrm, t - 1)
                    dve.wait_ge(s_qn, t - 1)
                V.tensor_tensor(qk[u].rearrange("p h c -> p (h c)"), ps[:, 3 * u + 1, :], bqk_s, ALU.add)
                V.tensor_tensor(vv[:, ds(t, 1), :].rearrange("p o c -> p (o c)"), ps[:, 3 * u + 2, 0:D], bv_s, ALU.add)\
                    .then_inc(s_prv, 1)
                dve.wait_ge(s_prv, t + 1)
                st(V.tensor_tensor(qksq[u], qk[u], qk[u], ALU.mult))
                st(V.tensor_reduce(ssq[u], qksq[u], X, ALU.add))
                V.tensor_tensor(ssq[u], ssq[u], ssmin, ALU.max).then_inc(s_ss, 1)

            def unit(t, u, i):
                dve.wait_ge(s_nrm, t + 1)
                st(V.reciprocal(rn[u], rn[u]))
                st(V.tensor_tensor(rn[u][:, 0:MH], rn[u][:, 0:MH], tempb, ALU.mult))
                V.tensor_tensor(kh[:, ds(t, 1), :].rearrange("p o (h c) -> p (o h) c", c=MD), qk[u][:, MH:2 * MH, :],
                                over(rn[u][:, MH:2 * MH], MD), ALU.mult)
                V.tensor_tensor(qn[:, ds(t, 1), :].rearrange("p o (h c) -> p (o h) c", c=MD), qk[u][:, 0:MH, :],
                                over(rn[u][:, 0:MH], MD), ALU.mult).then_inc(s_qn, 1)
            turns(NT, 2, 8, (normalize, 0), (heads, 3), (unit, 4))
            st(V.tensor_tensor(bres_s, bres_s, bres2, ALU.add))
            st(V.tensor_tensor(res[:, :, :], res[:, :, :], under(bres_s, NT), ALU.add))

            dve.wait_ge(s_prj, NT)
            dve.wait_ge(s_hst[0], 16 * ((NT + 1) // 2))
            dve.wait_ge(s_hst[1], 16 * (NT // 2))
            V.memset(src_i, 0).then_inc(s_edc, 1)
            V.memset(dsc_i, PAD_DST).then_inc(s_edc, 1)

            def pairs(t, u, i):
                dve.wait_ge(s_kx, t + 1)
                if late(t, 2):
                    dve.wait_ge(s_kv, t - 1)
                k0 = ap(kx[u], 0, [list(kx[u].ap[0]), [48, MH], [0, SQ], [1, MD]])
                k1 = ap(kx[u], 0, [list(kx[u].ap[0]), [48, MH], [1, SQ], [1, MD]])
                kk = kx[u].rearrange("p (h c) -> p h c", h=MH)
                V.tensor_tensor(f16[u].rearrange("p (h c) -> p h c", h=MH), kk[:, :, 0:MD], kk[:, :, SQ:SQ + MD], ALU.mult)
                V.tensor_tensor(phi[u].rearrange("p h (r i) -> p h r i", i=MD), k0, k1, ALU.mult).then_inc(s_phi, 1)
            turns(NT, 2, 0, (pairs, 0))

            dve.wait_ge(s_kv, NT)
            for g in range(KD):
                b = ps[:, 2 + g, :]
                V.tensor_scalar(ftc[g], ps[:, g, :], 0.5, None, ALU.mult)
                V.tensor_tensor(lin[g], b[:, 0:P], blocks[:, :], ALU.mult)
                V.scalar_tensor_tensor(gram[g], b[:, P:2 * P], 0.5, blocks[:, :], ALU.mult, ALU.mult)
                V.scalar_tensor_tensor(cf16[g], b[:, 2 * P:3 * P], 0.25, blocks[:, :], ALU.mult, ALU.mult)
                V.tensor_copy(sk[g][:, :], b[:, 3 * P:3 * P + 1])
                ins = V.tensor_copy(sv[g][:, :], b[:, 3 * P + 1:3 * P + 2])
            ins.then_inc(s_kvc, 1)

            dve.wait_ge(s_qtc, NT)
            for g in range(KD):
                for c in range(NP // SPW):
                    col = slice(c * SPW, (c + 1) * SPW)
                    st(V.tensor_copy(split[0][:, g, col], qT[:, g, col]))
                    st(V.tensor_tensor(rem, qT[:, g, col], split[0][:, g, col], ALU.subtract))
                    st(V.tensor_copy(split[1][:, g, col], rem))
                    st(V.tensor_tensor(rem, rem, split[1][:, g, col], ALU.subtract))
                    V.tensor_copy(split[2][:, g, col], rem).then_inc(s_spl[g], 1)
                    dve.wait_ge(s_spl[g], c + 1)

            dve.wait_ge(s_cft, 1)
            for g in range(KD):
                for c in range(NQC):
                    ins = V.tensor_copy(coef[c][g], ps[:, 4 + g, c * P:(c + 1) * P])
            ins.then_inc(s_cfc, 1)
            dve.wait_ge(s_cf0, 1)
            for g in range(KD):
                ins = V.tensor_copy(coef[0][g][0:MD, :], ps[0:MD, 6, g * P:(g + 1) * P])
            ins.then_inc(s_cfd, 1)

            dve.wait_ge(s_stk, 16 * 3 * MH)
            for b in range(NB):
                col = slice(b * BW, (b + 1) * BW)
                for g in range(KD):
                    r = b * KD + g
                    dve.wait_ge(s_t, r + 1)
                    if r >= 2:
                        dve.wait_ge(s_dn, r - 1)
                    V.scalar_tensor_tensor(tq[r % 2], ps[:, 5, 0:BW], sk[g][:, 0:1], qT[:, g, col], ALU.add, ALU.mult)\
                        .then_inc(s_tq, 1)
                    dve.wait_ge(s_dn, r + 1)
                    V.tensor_scalar(rden[r % 2], ps[:, 6, 0:BW], float(N), None, ALU.add).then_inc(s_den, 1)
                    dve.wait_ge(s_den, r + 1)
                    st(V.reciprocal(rden[r % 2], rden[r % 2]))
                    dve.wait_ge(s_y, r + 1)
                    V.scalar_tensor_tensor(yT[:, g, col], ps[:, 3 + g, 0:BW], sv[g][:, 0:1], rden[r % 2],
                                           ALU.add, ALU.mult).then_inc(s_yT, 1)
            for t in range(NT):
                dve.wait_ge(s_mo, t + 1)
                V.tensor_tensor(res[:, t, :], res[:, t, :], ps[:, t % 2, 0:D], ALU.add).then_inc(s_mor, 1)

            for j in range(8):
                dve.wait_ge(s_sg[j], 16 * (EP // 8))
            dve.wait_ge(s_edst, 32)
            st(V.tensor_copy(dsc, dsc_i))
            V.memset(fadd[:, 0:1], 0.0)
            V.memset(badd[:, EP - 1:EP], 0.0)
            st(V.tensor_tensor(fadd[:, 1:EP], dsc[:, 1:EP], dsc[:, 0:EP - 1], ALU.is_equal))
            st(V.tensor_scalar(fadd[:, 1:EP], fadd[:, 1:EP], -1.0, BIG, ALU.add, ALU.mult))
            st(V.tensor_copy(badd[:, 0:EP - 1], fadd[:, 1:EP]))
            for h in range(GH):
                ins = V.tensor_tensor_scan(fwd[:, :, h], fadd, sco[:, :, h], -BIG, ALU.add, ALU.max)
            st(ins)
            V.tensor_copy(chv[:, 0, :], fwd[:, EP - 1, :])
            V.tensor_copy(chv[:, 1, :], ap(dsc, EP - 1, [list(dsc.ap[0]), [0, GH]]))
            V.tensor_copy(chv[:, 2, :], ap(dsc, 0, [list(dsc.ap[0]), [0, GH]])).then_inc(s_sh, 1)
            rv = rowv[0:GH]
            R0, R1, R2, R3, R4, R5, R6, R7 = (rv[:, q, :] for q in range(8))
            n1 = P - 1
            dve.wait_ge(s_tr, 1)
            st(V.tensor_copy(rv[:, 0:3, :], ps[0:GH, 7, 0:3 * P].rearrange("p (q n) -> p q n", q=3)))
            V.memset(R3[:, 0:1], -BIG)
            V.memset(R6[:, 0:1], -BIG)
            V.memset(R7, 0.0)
            V.tensor_tensor(R3[:, 1:P], R1[:, 1:P], R1[:, 0:n1], ALU.is_equal)
            st(V.tensor_tensor(R5[:, 1:P], R2[:, 1:P], R1[:, 0:n1], ALU.is_equal))
            V.tensor_scalar(R5[:, 1:P], R5[:, 1:P], -1.0, BIG, ALU.add, ALU.mult)
            st(V.tensor_scalar(R3[:, 1:P], R3[:, 1:P], -1.0, BIG, ALU.add, ALU.mult))
            st(V.tensor_tensor_scan(R4, R3, R0, -BIG, ALU.add, ALU.max))
            V.tensor_tensor(R6[:, 1:P], R5[:, 1:P], R4[:, 0:n1], ALU.add).then_inc(s_sh, 1)
            dve.wait_ge(s_tr, 2)
            st(V.tensor_copy(cin[:, 0:2, :], ps[:, 7, 3 * P:3 * P + 2 * GH].rearrange("p (q h) -> p q h", q=2)))
            for h in range(GH):
                ins = V.tensor_tensor_scan(fwd[:, :, h], fadd, sco[:, :, h], cin[:, 0, h:h + 1], ALU.add, ALU.max)
            st(ins)
            for h in range(GH):
                ins = V.tensor_tensor_scan(back(mx5[:, :, h]), back(badd), back(fwd[:, :, h]), -BIG, ALU.add, ALU.max)
            st(ins)
            V.tensor_copy(chv[:, 0, :], mx5[:, 0, 0:GH]).then_inc(s_sh, 1)
            dve.wait_ge(s_tr, 3)
            st(V.tensor_copy(R0, ps[0:GH, 7, 0:P]))
            V.memset(R3[:, n1:P], -BIG)
            V.memset(R6[:, n1:P], -BIG)
            V.tensor_tensor(R3[:, 0:n1], R2[:, 0:n1], R2[:, 1:P], ALU.is_equal)
            st(V.tensor_tensor(R7[:, 0:n1], R1[:, 0:n1], R2[:, 1:P], ALU.is_equal))
            V.tensor_scalar(R5[:, 0:n1], R7[:, 0:n1], -1.0, BIG, ALU.add, ALU.mult)
            st(V.tensor_scalar(R3[:, 0:n1], R3[:, 0:n1], -1.0, BIG, ALU.add, ALU.mult))
            st(V.tensor_tensor_scan(back(R4), back(R3), back(R0), -BIG, ALU.add, ALU.max))
            V.tensor_tensor(R6[:, 0:n1], R5[:, 0:n1], R4[:, 1:P], ALU.add).then_inc(s_sh, 1)
            dve.wait_ge(s_tr, 4)
            st(V.tensor_copy(cin[:, 0:2, :], ps[:, 7, 3 * P:3 * P + 2 * GH].rearrange("p (q h) -> p q h", q=2)))
            for h in range(GH):
                V.tensor_tensor_scan(back(mx5[:, :, h]), back(badd), back(fwd[:, :, h]), cin[:, 0, h:h + 1],
                                     ALU.add, ALU.max)
            V.tensor_scalar(mx5[:, 0:EP - 1, GH], badd[:, 0:EP - 1], -1.0, None, ALU.is_lt)
            V.tensor_scalar(mx5[:, EP - 1, GH:GH + 1], cin[:, 1, 0:1], -1.0, 1.0, ALU.mult, ALU.add).then_inc(s_shr, 1)

            st(V.memset(cnt, 0.0))
            for t in range(1, NT):
                st(V.tensor_scalar(fadd, dsc, float(t * P), None, ALU.is_lt, ALU.add, accum_out=cnt[:, t:t + 1]))
            V.memset(offs, 0.0).then_inc(s_off, 1)
            dve.wait_ge(s_offp, 1)
            st(V.tensor_copy(offs, ps[:, 7, 0:32]))
            st(V.memset(offs[:, NT:NT + 1], float(E)))
            st(V.tensor_copy(tint, offs))
            st(V.tensor_scalar(tint, tint, GE.bit_length() - 1, None, ALU.logical_shift_right))
            st(V.tensor_copy(fo, tint))
            st(V.tensor_scalar(tint, offs, float(GE - 1), None, ALU.add))
            st(V.tensor_scalar(tint, tint, GE.bit_length() - 1, None, ALU.logical_shift_right))
            st(V.tensor_copy(co, tint))
            a, z = slice(0, NT), slice(1, NT + 1)
            V.tensor_tensor(nsl[:, a], co[:, z], fo[:, a], ALU.subtract)
            st(V.tensor_tensor(half32[:, a], offs[:, z], offs[:, a], ALU.is_gt))
            st(V.tensor_tensor(nsl[:, a], nsl[:, a], half32[:, a], ALU.mult))
            st(V.memset(half32, 0.0))
            st(V.tensor_tensor_scan(stt[:, a], nsl[:, a], half32[:, a], 0.0, ALU.add, ALU.add))
            st(V.tensor_tensor(sex[:, a], stt[:, a], nsl[:, a], ALU.subtract))
            st(V.tensor_tensor(dif[:, a], fo[:, a], sex[:, a], ALU.subtract))
            V.tensor_copy(sl_p[:, 0:1], iota_p[:, :])
            st(V.tensor_scalar(sl_p[:, 1:2], iota_p[:, :], float(P), None, ALU.add))
            for u in range(2):
                st(V.tensor_scalar(half32[:, a], stt[:, a], sl_p[:, u:u + 1], None, ALU.is_le, ALU.add,
                                   accum_out=ts_p[:, u:u + 1]))
            for u in range(2):
                st(V.scalar_tensor_tensor(half32[:, a], iota_f[:, a], ts_p[:, u:u + 1], dif[:, a],
                                          ALU.is_equal, ALU.mult, accum_out=gs_p[:, u:u + 1]))
            V.tensor_scalar(tsm, ts_p, float(P), None, ALU.mult)
            V.tensor_scalar(tsc, ts_p, float(NT - 1), None, ALU.min).then_inc(s_off, 1)
            st(V.tensor_tensor(gs_p, gs_p, sl_p, ALU.add))
            st(V.tensor_scalar(gs_p, gs_p, float(NG - 1), None, ALU.min))
            V.tensor_copy(gs_i, gs_p).then_inc(s_slot, 1)
            dve.wait_ge(s_offp, 2)
            st(V.tensor_copy(ts_row[:, :], ps[0:1, 7, 0:NSP]))

            dve.wait_ge(s_slg, 16 * 6)
            V.tensor_copy(fsrc, sl_src)
            for u in range(2):
                ins = V.tensor_scalar(fdl[:, u, :], sl_dst[:, u, :], tsm[:, u:u + 1], None, ALU.subtract)
            st(ins)
            V.tensor_copy(fdlb, fdl).then_inc(s_slf, 1)
            for u in range(2):
                dve.wait_ge(s_slt, u + 1)
                V.tensor_copy(tb[u][:, :, :, 0].bitcast(I32).rearrange("p s k -> p k s"),
                              psf[:, 0:TE * P].rearrange("p (k s) -> p k s", k=TE))
                V.tensor_copy(tb[u][:, :, :, 1:TW].rearrange("p s k w -> p w k s"),
                              psf[:, TE * P:TW * TE * P].rearrange("p (w k s) -> p w k s", w=TW - 1, k=TE))\
                    .then_inc(s_slc, 1)
            d3v = d3[:, :].rearrange("p (t h q) -> p t h q", h=GH, q=3)
            a_d = nas[:, :, GH:AH]
            r1 = dif2
            st(V.tensor_copy(d3v[:, :, :, 0], a_d))
            st(V.tensor_tensor(r1, a_d, d3v[:, :, :, 0], ALU.subtract))
            st(V.tensor_copy(d3v[:, :, :, 1], r1))
            st(V.tensor_tensor(r1, r1, d3v[:, :, :, 1], ALU.subtract))
            st(V.tensor_copy(d3v[:, :, :, 2], r1))
            dve.wait_ge(s_tab, 32)
            dve.wait_ge(s_dlst, 32)
            V.memset(acc[:, :], 0.0).then_inc(s_accz, 1)
            dve.wait_ge(s_accz, 1)

            def onehots(b, u, i):
                v = u % 2
                dve.wait_ge(s_dl[u], 16 * i + 16)
                if late(b, 2):
                    dve.wait_ge(s_dp, b - 1)
                V.tensor_scalar(oht[v], dlb[u], iota_p[:, 0:1], None, ALU.is_equal).then_inc(s_oht, 1)

            def masks(b, u, i):
                if late(b, 2):
                    dve.wait_ge(s_agg, b * SB - SB)
                V.tensor_tensor(oh[u % 2], under(iota_f[:, :], SB * TE), over(tab[u][:, :, 1], P), ALU.is_equal)

            def weights(b, u, i):
                v = u % 2
                dve.wait_ge(s_dp, b + 1)
                dve.wait_ge(s_tl[u], 16 * i + 16)
                st(V.tensor_reduce(dv[v].rearrange("p k h -> p (k h)"),
                                   ps[:, v, 0:SB * TE * 12].rearrange("p (k q) -> p k q", q=3), X, ALU.add))
                V.tensor_tensor(a2[v][:, 1], dv[v], tab[u][:, :, 2:2 + GH], ALU.add).then_inc(s_dv, 1)
                dve.wait_ge(s_gg[u], 16 * SB * TE * i + 16 * SB * TE)
                st(V.tensor_tensor(a2[v][:, 0], dv[v], gb[u][:, :, D:D + GH], ALU.add))
                leaky = V.scalar_tensor_tensor(lk[v].rearrange("p w k h -> p (w k h)"),
                                               a2[v].rearrange("p w k h -> p (w k h)"), 0.2,
                                               a2[v].rearrange("p w k h -> p (w k h)"), ALU.mult, ALU.max)
                lky = st.mark(leaky)
                V.tensor_tensor(gb[u][:, :, D + GH:ACOL], tab[u][:, :, 2:2 + GH], over(tab[u][:, :, 2 + GH], GH), ALU.mult)
                dve.wait_ge(v_step, lky)
                if late(b, 2):
                    dve.wait_ge(s_we, b - 1)
                V.tensor_tensor(wl[v], lk[v][:, 0], lk[v][:, 1], ALU.subtract).then_inc(s_wl, 1)

            def messages(b, u, i):
                dve.wait_ge(s_we, b + 1)
                m = gb[u][:, :, 0:D].rearrange("p k (h c) -> p k h c", c=GD)
                V.tensor_tensor(m, m, over(gb[u][:, :, D:D + GH], GD), ALU.mult).then_inc(s_msg, 1)

            def accumulate(b, u, i):
                for s in range(SB):
                    t = dve.value_load(ts_row[0:1, ds(b * SB + s, 1)], min_val=0, max_val=NT - 1)
                    dve.wait_ge(s_agg, b * SB + (s + 1))
                    if s or late(b, 1):
                        dve.wait_ge(s_accd, b * SB + s)
                    a = acc[:, ds(t * ACOL, ACOL)]
                    V.tensor_tensor(a, a, ps[:, 2 + u % 2 * SB + s, 0:ACOL], ALU.add).then_inc(s_accd, 1)
            turns(NBT, NBUF, 3 * NBUF, (onehots, 0), (weights, 1), (masks, 2), (messages, 2), (accumulate, 3))

            dve.wait_ge(s_accd, NS)
            dve.wait_ge(s_agg, NS)
            accv = acc[:, :].rearrange("p (t c) -> p t c", c=ACOL)
            eden, emax = accv[:, :, D:D + GH], accv[:, :, D + GH:ACOL]
            a_s = nas[:, :, 0:GH]
            V.tensor_scalar(has, eden, 0.0, None, ALU.is_gt)
            V.tensor_tensor(mlog, emax, a_d, ALU.add)
            st(V.tensor_tensor(slog, a_s, a_d, ALU.add))
            V.scalar_tensor_tensor(f1, mlog, 0.2, mlog, ALU.mult, ALU.max)
            V.scalar_tensor_tensor(f2, slog, 0.2, slog, ALU.mult, ALU.max)
            st(V.tensor_scalar(has, has, -1.0, BIG, ALU.add, ALU.mult))
            st(V.tensor_tensor(f1, f1, has, ALU.add))
            st(V.tensor_tensor(mtop, f1, f2, ALU.max))
            V.tensor_tensor(dlog[:, 0], f1, mtop, ALU.subtract)
            V.tensor_tensor(dlog[:, 1], f2, mtop, ALU.subtract).then_inc(s_fin, 1)
            dve.wait_ge(s_fine, 1)
            st(V.tensor_tensor(den, eden, dexp[:, 0], ALU.mult))
            st(V.tensor_tensor(den, den, dexp[:, 1], ALU.add))
            st(V.reciprocal(den, den))
            V.tensor_tensor(f1, dexp[:, 0], den, ALU.mult)
            st(V.tensor_tensor(f2, dexp[:, 1], den, ALU.mult))

            def attend(t, u, i):
                dve.wait_ge(s_hl[u], 16 * i + 16)
                r = res[:, ds(t, 1), :].rearrange("p o (h c) -> p (o h) c", c=GD)
                tt = ds(t, 1)
                V.tensor_tensor(tm[0], accv[:, tt, 0:D].rearrange("p o (h c) -> p (o h) c", c=GD),
                                over(f1[:, tt, :].rearrange("p o h -> p (o h)"), GD), ALU.mult)
                V.tensor_tensor(tm[1], hb[u], over(f2[:, tt, :].rearrange("p o h -> p (o h)"), GD), ALU.mult)\
                    .then_inc(s_hf[u], 1)
                dve.wait_ge(s_hf[u], i + 1)
                st(V.tensor_tensor(r, r, tm[0], ALU.add))
                st(V.tensor_tensor(r, r, tm[1], ALU.add))
            turns(NT, 2, 4, (attend, 0))

            for t in range(NT):
                ins = V.bn_stats(stats2[:, t, :], res[:, t, :])
            st(ins)
            for t in range(NT):
                ins = V.bn_aggr(mv2[:, t, :], stats2[:, t, :])
            st(ins)
            V.tensor_scalar(wait_w, mv2[:, :, 1], EPS_LN, None, ALU.add).then_inc(s_var2, 1)
            dve.wait_ge(s_sd2, 1)
            st(V.reciprocal(wait_w, wait_s))
            for t in range(NT):
                V.tensor_scalar(xn2[:, t, :], res[:, t, :], mv2[:, t, 0:1], wait_w[:, t:t + 1], ALU.subtract, ALU.mult)\
                    .then_inc(s_xn2, 1)

            V.tensor_copy(iota_e, iota_f[:, 0:NE])
            st(V.memset(zeros_e, 0.0))
            V.tensor_scalar(rowval, iota_p[:, :], float(TAIL), None, ALU.is_lt)
            dve.wait_ge(s_gs, NT)
            dve.wait_ge(s_gw, 32)
            st(V.tensor_tensor(gsc, ps[:, 7, 0:NX].rearrange("p (t e) -> p t e", e=NE), under(bgb, NT), ALU.add))
            for t in range(NT):
                ins = V.max(top[:, t, :], gsc[:, t, :])
            st(ins)
            for t in range(NT):
                ins = V.max_index(topi[:, t, :], top[:, t, :], gsc[:, t, :])
            st(ins)
            V.tensor_tensor(egap[:, :], top[:, :, 1], top[:, :, 0], ALU.subtract).then_inc(s_ez, 1)
            st(V.tensor_copy(ti, topi[:, :, 0:2]))
            for k in range(TOPK):
                ins = V.tensor_tensor(msk[k], under(iota_e, NT), over(ti[:, :, k], NE), ALU.is_equal)
            st(ins)
            for k in range(TOPK):
                ins = V.tensor_scalar(msk[k][:, NT - 1, :], msk[k][:, NT - 1, :], rowval[:, 0:1], None, ALU.mult)
            st(ins)
            V.tensor_tensor(msum, msk[0], msk[1], ALU.add).then_inc(s_sel, 1)
            dve.wait_ge(s_e2, 1)
            st(V.tensor_scalar(pr[0][:, :], eexp[:, :], 1.0, None, ALU.add))
            st(V.reciprocal(pr[0][:, :], pr[0][:, :]))
            st(V.tensor_tensor(pr[1][:, :], eexp[:, :], pr[0][:, :], ALU.mult))
            dve.wait_ge(s_pre, 1)
            tot = ps[:, 1, 0:NX].rearrange("p (t e) -> p t e", e=NE)
            for e in range(NE):
                ins = V.tensor_tensor_scan(cum[:, :, e], tot[:, :, e], zeros_e[:, 0:NT], 0.0, ALU.add, ALU.add)
            st(ins)
            st(V.tensor_tensor(pos, cum, tot, ALU.subtract))
            st(V.tensor_tensor(pos, pos, ps[:, 0, 0:NX].rearrange("p (t e) -> p t e", e=NE), ALU.add))
            st(V.tensor_scalar(nti, cum[:, NT - 1, :], float(P - 1), None, ALU.add))
            st(V.tensor_scalar(nti, nti, P.bit_length() - 1, None, ALU.logical_shift_right))
            st(V.tensor_copy(ntl, nti))
            st(V.tensor_tensor_scan(endj, ntl, zeros_e[:, 0:NE], 0.0, ALU.add, ALU.add))
            st(V.tensor_tensor(basej, endj, ntl, ALU.subtract))
            st(V.tensor_scalar(basej, basej, float(P), None, ALU.mult))
            st(V.tensor_tensor(pos, pos, under(basej, NT), ALU.add))
            st(V.tensor_scalar(cnt_e, endj, iota_p[:, 0:1], None, ALU.is_le, ALU.add, accum_out=ej))
            V.tensor_scalar(ejc, ej, float(NE - 1), None, ALU.min).then_inc(s_sel, 1)
            for k in range(TOPK):
                st(V.tensor_tensor(mp, msk[k], pos, ALU.mult))
                st(V.tensor_reduce(posf[k][:, :], mp, X, ALU.add))
                ins = V.tensor_copy(posi[k][:, :], posf[k][:, :])
            ins.then_inc(s_pos, 1)
            dve.wait_ge(s_ejp, 1)
            V.tensor_copy(ej_row[:, :], ps[0:1, 2, 0:P]).then_inc(s_ej, 1)

            dve.wait_ge(s_w2, 16 * (EL + 2))
            dve.wait_ge(s_sc, 16 * TOPK * NT)

            def first_weights(j, u, i):
                e = dve.value_load(ej_row[0:1, ds(j, 1)], min_val=0, max_val=NE - 1)
                for n_ in range(2):
                    if late(j, 1):
                        dve.wait_ge(s_f1, 2 * j - (1 - n_))
                    V.tensor_copy(w1c[n_], w1_s[:, ds(e, 1), :, n_ * HH:(n_ + 1) * HH].rearrange("p o k n -> p (o k) n"))\
                        .then_inc(s_w1c, 1)

            def results(j, u, i):
                e = dve.value_load(ej_row[0:1, ds(j, 1)], min_val=0, max_val=NE - 1)
                dve.wait_ge(s_f2, j + 1)
                if late(j, 2):
                    dve.wait_ge(s_fy[u], 16 * i)
                V.tensor_tensor(ys[u], ps[:, 5 + u, 0:D], b2_s[:, ds(e, 1), :].rearrange("p o c -> p (o c)"), ALU.add)\
                    .then_inc(s_f2c, 1)
            dve.wait_ge(s_ej, 1)
            dve.wait_ge(s_w1, 16 * (NE + NE - EL))
            turns(NJ, 2, 0, (first_weights, 0), (results, 2))

            for t in range(NT):
                u = t % 2
                dve.wait_ge(s_cg[u], 16 * TOPK * (t // 2 + 1))
                st(V.scalar_tensor_tensor(res[:, t, :], yg[u][0], pr[0][:, t:t + 1], res[:, t, :], ALU.mult, ALU.add))
                V.scalar_tensor_tensor(res[:, t, :], yg[u][1], pr[1][:, t:t + 1], res[:, t, :], ALU.mult, ALU.add)\
                    .then_inc(s_cm, 1)


def kernel(**inputs):
    import numpy as np
    import concourse.bacc as bacc
    from concourse.bass_utils import run_bass_kernel_spmd

    get = {k: np.asarray(v) for k, v in inputs.items()}

    def chunks(w):
        return w.reshape(-1, 128, w.shape[-1]).transpose(1, 0, 2)

    w1 = get["L0_ffn_W1"].transpose(0, 2, 1).reshape(NE, KD, P, HID).transpose(2, 0, 1, 3)
    w2 = get["L0_ffn_W2"].transpose(0, 2, 1).reshape(NE, HC, P, D).transpose(2, 0, 1, 3)
    arrays = {
        "x": get["x"], "src": get["src"], "dst": get["dst"],
        "wcat": chunks(np.concatenate([get["L0_gnn_W"], get["L0_mix_Wqkv"].T], axis=1)),
        "wgt": chunks(get["L0_gnn_W"].T),
        "att_src": get["L0_gnn_att_src"], "att_dst": get["L0_gnn_att_dst"], "gbias": get["L0_gnn_bias"],
        "bqkv": get["L0_mix_bqkv"], "wpt": chunks(get["L0_mix_Wproj"].T), "bproj": get["L0_mix_bproj"],
        "temp": get["L0_mix_temperature"].reshape(MH),
        "wg": chunks(get["L0_ffn_Wg"].T), "bg": get["L0_ffn_bg"],
        "w1": w1, "b1": get["L0_ffn_b1"].reshape(NE, HC, P).transpose(2, 0, 1).reshape(P, NE * HC),
        "w2": w2, "b2": get["L0_ffn_b2"],
    }
    nc = bacc.Bacc("TRN2", target_bir_lowering=False, num_devices=1)
    args, feed = [], {}
    for name, a in arrays.items():
        a = np.ascontiguousarray(a)
        feed[f"in_{name}"] = a
        args.append(nc.dram_tensor(f"in_{name}", a.shape, mybir.dt.from_np(a.dtype), kind="ExternalInput").ap())
    out = nc.dram_tensor("out", (N, D), F32, kind="ExternalOutput").ap()
    gps_layer(nc, *args, out)
    r = run_bass_kernel_spmd(nc, [feed], core_ids=[0])
    return r.results[0]["out"]
```

```python
from contextlib import ExitStack, contextmanager

import concourse.bass as bass
from concourse import mybir

F32 = mybir.dt.float32
I32 = mybir.dt.int32
U32 = mybir.dt.uint32
BF16 = mybir.dt.bfloat16
ALU = mybir.AluOpType
ACT = mybir.ActivationFunctionType
X = mybir.AxisListType.X
ds = bass.ds

P = 128
N = 3125
D = 256
E = 50000
GH, GD = 4, 64
MH, MD = 8, 32
NE, HID = 8, 1024
NT = -(-N // P)
TAIL = N - (NT - 1) * P
NP = NT * P
KD = D // P
HC = HID // P
AH = 2 * GH
HROW = D + GH
SQ = MD // 2
QC = P // MD
NQC = SQ // QC
NB = 8
BW = NP // NB
EP = 392
EPAD = EP * P
GE = 256
NG = EPAD // GE
NS = NG + NT - 1
TE = GE // P
NSP = 2 * P
SB = 2
NBT = NS // SB
assert NS % (2 * SB) == 0 and NG * GE == EPAD and BW * NB == NP
ACOL = D + 2 * GH
PAD_DST = 4096
BIG = 1e30
TOPK = 2
JB = 4
XR = D + 2
NJ = (TOPK * N + NE * (P - 1)) // P
NJ += NJ % 2
EPS_LN = 1e-5
EPS_N = 1e-12
QSCALE = float(MD) ** 0.25
assert NE == MH


class Steps:

    def __init__(self, eng, sem):
        self.eng, self.sem, self.n, self.i, self.per, self.k = eng, sem, 0, None, 0, 0

    def __call__(self, ins):
        self.eng.wait_ge(self.sem, self.mark(ins))

    def mark(self, ins):
        ins.then_inc(self.sem, 1)
        if self.i is None:
            self.n += 1
            return self.n
        self.k += 1
        return self.i * self.per + (self.n + self.k)

    @contextmanager
    def loop(self, first, end, per):
        self.n -= first * per
        with self.eng.Fori(first, end) as i:
            self.i, self.per, self.k = i, per, 0
            yield i
            assert self.k == per, (self.k, per)
        self.i = None
        self.n += end * per


def skewed(loop, n, w, parts):
    far = max(lag for _, lag in parts)

    def turn(i, q):
        for part, lag in parts:
            d = (q - lag) // w
            if isinstance(i, int):
                t = i * w + q - lag
                if 0 <= t < n:
                    part(t, t % w, t // w)
            else:
                part(i * w + (q - lag), (q - lag) % w, i + d if d else i)
    first, end = -(-(far + w) // w), n // w
    for i in range(first):
        for q in range(w):
            turn(i, q)
    with loop(first, end) as i:
        for q in range(w):
            turn(i, q)
    for i in range(end, -(-(n + far) // w)):
        for q in range(w):
            turn(i, q)


def gps_layer(nc, x, src, dst, wcat, wgt, att_src, att_dst, gbias, bqkv, wpt, bproj, temp,
              wg, bg, w12, b1, b2, out):
    ctx = ExitStack()

    def sb(name, shape, dt=F32):
        return ctx.enter_context(nc.sbuf_tensor(name, shape, dt))

    def sem(name):
        return ctx.enter_context(nc.semaphore(name))

    def dram(name, shape, dt=F32):
        return nc.dram_tensor(name, shape, dt, kind="Internal").ap()

    def ap(t, off, pairs):
        return bass.AP(t.tensor, t.offset + off, pairs)

    def rows(t, n, w, off=0):
        return ap(t, off, [[0, n], [1, w]])

    with ctx:
        XW = 6
        XC = -(-NT // XW)

        LW = 5
        LC = NT // LW
        assert LC * LW == NT

        h_d = dram("h_d", [NP, HROW])
        as_d = dram("as_d", [NP, GH])
        src_d = dram("src_d", [NG, GE], I32)
        dst_d = dram("dst_d", [NG, GE], I32)
        max_d = dram("max_d", [NG, GE * (GH + 1)])
        dl_d = dram("dl_d", [NSP, GE], BF16)
        xs_d = dram("xs_d", [NJ * P, XR])
        sum_d = dram("sum_d", [NP + P, D])

        AW = 32000
        GW = 4000
        arena = sb("arena", [P, AW + GW])
        res = sb("res", [P, NT, D])
        acc = sb("acc", [P, NT * ACOL])
        identf = sb("identf", [P, P])
        identb = sb("identb", [P, P], BF16)
        onesf = sb("onesf", [P, P])
        lower = sb("lower", [P, P])
        blocks = sb("blocks", [P, P])
        iota_f = sb("iota_f", [P, P])
        iota_p = sb("iota_p", [P, 1])
        nas = sb("nas", [P, NT, AH])
        d3 = sb("d3", [P, NT * GH * 3], BF16)
        small = sb("small", [P, 700])

        A = arena[:, :]
        G = arena[:, AW:AW + GW]
        C = acc[:, :]
        S = small[:, :]

        def view(base, off, words, pat=None, **kw):
            v = base[:, off:off + words]
            return v.rearrange(pat, **kw) if pat else v

        kh = view(A, 0, NT * D, "p (t c) -> p t c", t=NT)
        vv = view(A, NT * D, NT * D, "p (t c) -> p t c", t=NT)
        qT = view(A, 2 * NT * D, KD * NP, "p (g n) -> p g n", g=KD)
        STK = 2 * NT * D + KD * NP
        stack = view(A, STK, MH * NP // 2).bitcast(BF16).rearrange("p (h n) -> p h n", h=MH)
        XB = 4
        xn = [view(A, STK + u * D, D) for u in range(XB)]
        xT = view(A, 2 * NT * D, KD * NP, "p (k n) -> p k n", k=KD)
        qn = view(A, STK + NT * D, NT * D, "p (t c) -> p t c", t=NT)
        FW = SQ * MD
        kx = [view(A, STK + u * MH * 48, MH * 48) for u in range(2)]
        phi = [view(A, STK + 2 * MH * 48 + u * MH * FW, MH * FW, "p (h f) -> p h f", h=MH) for u in range(2)]
        f16, kb, vb = ([view(A, STK + 2 * MH * 48 + 2 * MH * FW + (2 * q + u) * D, D) for u in range(2)]
                       for q in range(3))
        split = [view(A, s * NP, NP).bitcast(BF16).rearrange("p (g n) -> p g n", g=KD) for s in range(3)]
        SPW = 800
        SPC = NP // SPW
        NSP_ = KD * SPC
        rem = [view(A, 3 * NP + u * SPW, SPW) for u in range(2)]
        yT = view(A, 0, KD * NP, "p (g n) -> p g n", g=KD)
        zsq = [view(A, KD * NP, QC * BW), view(G, 0, QC * BW)]
        MW = KD * NP + QC * BW
        tq, rden = ([view(A, MW + (2 * q + b) * BW, BW) for b in range(2)] for q in range(2))
        z16 = view(A, MW + 4 * BW, BW)
        zc = view(A, MW + 5 * BW, BW)
        MW += 6 * BW
        wpt_s = view(A, MW, KD * D, "p (g c) -> p g c", g=KD)
        MW += KD * D

        def square():
            nonlocal MW
            MW += P
            return view(A, MW - P, P)

        coef = [[square() for g in range(KD)] for c in range(NQC)]
        cf16 = [square() for g in range(KD)]
        lin = [square() for g in range(KD)]
        gram = [square() for g in range(KD)]
        assert MW <= 2 * NT * D
        sk = [sb(f"sk{g}", [P, 1]) for g in range(KD)]
        sv = [sb(f"sv{g}", [P, 1]) for g in range(KD)]
        pairb = sb("pairb", [3 * MD, NQC, P], BF16)
        pair16 = sb("pair16", [3 * MD, MD], BF16)
        w1_s = view(A, 0, NE * KD * HID, "p (e k n) -> p e k n", e=NE, k=KD)
        w2_s = view(A, NE * KD * HID, NE * HC * D, "p (e c n) -> p e c n", e=NE, c=HC)

        wa_off = 0
        wcat_s = view(C, 0, KD * 1024, "p (k n) -> p k n", k=KD)
        wacc_s = view(C, 2048, KD * AH, "p (k n) -> p k n", k=KD)
        bqk_s = view(C, 2064, 2 * D)
        bv_s = view(C, 2576, D)
        bres_s = view(C, 2832, D)
        hrow = [view(C, 3600 + u * 264, 264) for u in range(2)]
        qk = [view(C, 4128 + u * 512, 512, "p (h c) -> p h c", c=MD) for u in range(2)]
        qksq = [view(C, 5152 + u * 512, 512, "p (h c) -> p h c", c=MD) for u in range(2)]
        wgt_s = view(G, 0, KD * D, "p (k n) -> p k n", k=KD)
        att_s = view(G, 512, KD * AH, "p (k n) -> p k n", k=KD)
        stats = view(G, 600, NT * 6, "p (t s) -> p t s", s=6)
        mv = view(G, 760, NT * 2, "p (t s) -> p t s", s=2)
        rstd = view(G, 820, NT)
        ssq = [view(G, 860 + u * 16, 16) for u in range(2)]
        rn = [view(G, 900 + u * 16, 16) for u in range(2)]
        tempb = view(G, 940, MH)
        ssmin = view(G, 950, 2 * MH)
        sco = view(G, 2024, EP * GH, "p (e h) -> p e h", h=GH)
        src_i = view(G, 2024 + EP * GH, EP).bitcast(I32)
        fadd = view(C, 2 * EP, EP)
        badd = view(C, 3 * EP, EP)
        mx5 = view(C, 4 * EP, EP * (GH + 1), "p (e h) -> p e h", h=GH + 1)
        fwd = view(C, 9 * EP, EP * GH, "p (e h) -> p e h", h=GH)
        rowv = view(C, 13 * EP, 8 * P, "p (q n) -> p q n", n=P)
        zz = view(C, 13 * EP, 512)
        below = view(G, 1000, EP)
        sl_src = view(C, 4 * EP, 2 * GE, "p (u w) -> p u w", u=2).bitcast(I32)
        sl_dst = view(C, 4 * EP + 2 * GE, 2 * GE, "p (u w) -> p u w", u=2).bitcast(I32)
        fsrc = view(C, 4 * EP + 4 * GE, 2 * GE, "p (u w) -> p u w", u=2)
        fdl = view(C, 4 * EP + 6 * GE, 2 * GE, "p (u w) -> p u w", u=2)
        fdlb = view(C, 13 * EP + 8 * P, GE).bitcast(BF16).rearrange("p (u w) -> p u w", u=2)
        sl_max = view(C, 4 * EP, 2 * GE * (GH + 1), "p (u w c) -> p u w c", u=2, c=GH + 1)
        tables = sb("tables", [P, 2 * NS * TE])[:, :]
        dsc_i = view(tables, 0, EP).bitcast(I32)
        dsc = view(tables, EP, EP)
        tsrc = view(tables, 0, NS * TE, "p (s k) -> p s k", k=TE).bitcast(I32)
        tdl = view(tables, NS * TE, NS * TE, "p (s k) -> p s k", k=TE)
        tmax = view(G, 0, NS * TE * (GH + 1), "p (s k c) -> p s k c", k=TE, c=GH + 1)
        tsrc_f, tdl_f = (v.rearrange("p s k -> p (s k)") for v in (tsrc, tdl))
        tmax_f = tmax.rearrange("p s k c -> p (s k) c")

        W2 = NE * KD * HID
        EL = 4
        BO = W2 + (NE - EL) * HC * D
        H = arena[:, BO:AW]
        NBUF = 4
        PIECES = NBT // NBUF - 1
        PIECE = BO // PIECES
        o = 0

        def batch_words(n, pat=None, count=2, **kw):
            nonlocal o
            o += count * n
            return [view(H, o - (u + 1) * n, n, pat, **kw) for u in range(count)]

        gb = batch_words(SB * TE * ACOL, "p (k c) -> p k c", NBUF, c=ACOL)
        oh = batch_words(SB * TE * P, "p (k v) -> p k v", v=P)
        oht = [v.bitcast(BF16) for v in batch_words(SB * TE * P // 2)]
        dlb = [v.bitcast(BF16) for v in batch_words(SB * TE * P // 2, count=NBUF)]
        sidx = [v.bitcast(I32) for v in batch_words(SB * TE, count=NBUF)]
        dv = batch_words(SB * TE * GH, "p (k h) -> p k h", h=GH)
        a2 = batch_words(2 * SB * TE * GH, "p (w k h) -> p w k h", w=2, h=GH)
        lk = batch_words(2 * SB * TE * GH, "p (w k h) -> p w k h", w=2, h=GH)
        wl = batch_words(SB * TE * GH, "p (k h) -> p k h", h=GH)
        assert o <= AW - BO, o

        ts_row = sb("ts_row", [1, NSP], I32)
        ptick = sb("ptick", [1, 2])
        ej_row = sb("ej_row", [1, P], I32)
        QO = STK + XB * D
        pd0 = view(A, QO, NQC * P)
        pd1 = view(A, QO + 512, NQC * P)
        pdm = view(A, QO + 1024, NQC * P)
        pde = view(A, QO + 1536, MD)
        pdf = view(A, QO + 1600, 3 * MD)
        zrow = view(A, QO + 2048, XR)
        bres2 = view(C, 6200, D)
        rsd = view(G, 970, NT)
        ftc = [view(G, 1000 + g * 512, 512) for g in range(KD)]
        pn = [sb(f"pn{c}", [P, MD]) for c in range(NQC)]
        pn16 = sb("pn16", [P, MD])

        ps = ctx.enter_context(nc.psum_tensor("ps", [P, 8, 512], F32))
        psf = ps[:, :, :].rearrange("p b w -> p (b w)")
        psb = ps[:, 6, 0:256].bitcast(BF16)

        R_ROWS, R_SCAN = 9, 10
        RQ = NB * KD
        done_after = [[t for t in range(NT) if g == KD - 1 and b * BW < (t + 1) * P <= (b + 1) * BW]
                      for b in range(NB) for g in range(KD)]

        s_const = sem("constants_ready")
        s_x = [sem(f"x_loaded{c}") for c in range(XC)]
        s_w = sem("projection_weights_loaded")
        s_att = sem("att_zeroed")
        s_attd = sem("att_loaded")
        v_step, a_step, g_step, p_step = sem("vector_steps"), sem("scalar_steps"), sem("gpsimd_steps"), sem("tensor_steps")
        s_wa = sem("score_weights_product")
        s_wac = sem("score_weights_ready")
        s_var = sem("variances_ready")
        s_sd = sem("deviations_ready")
        s_xn = sem("normalized_tiles")
        s_xt = sem("xn_transposed")
        s_nsp = sem("node_scores_product")
        s_nas = sem("node_scores")
        s_xtc = sem("xn_transposed_in_sbuf")
        s_prj = sem("projected_tiles")
        s_prv = sem("qkv_psum_read")
        s_hst = [sem(f"h_stored{u}") for u in range(2)]
        s_hrow = sem("h_row_in_sbuf")
        s_sq = sem("queries_and_keys_squared")
        s_ss = sem("squared_norms")
        s_nrm = sem("norms")
        s_ast = sem("source_scores_stored")
        s_qn = sem("q_normalized")
        s_qt = sem("q_transposed")
        s_qtc = sem("q_transposed_in_sbuf")
        s_kx = sem("k_extended")
        s_kb = sem("k_and_v_copied")
        s_phi = sem("pair_features")
        s_kv = sem("pair_features_used")
        s_kvc = sem("kv_sums_in_sbuf")
        s_cft = sem("coefficients_transposed")
        s_cfc = sem("coefficients_in_sbuf")
        s_cf0 = sem("square_coefficients")
        s_cfd = sem("coefficients_done")
        s_pair = sem("pair_matrices")
        s_spl = [sem(f"split_part{g}") for g in range(KD)]
        s_stk = sem("stack_loaded")
        s_z = sem("pair_sums")
        s_zs = sem("pair_sums_squared")
        s_zc = sem("half_shift_sums_in_sbuf")
        s_b7 = sem("edge_products_read")
        s_zu = sem("squares_used")
        s_spa = sem("query_parts_by_scalar")
        s_rem = sem("query_remainders")
        s_t = sem("gram_products")
        s_tq = sem("gram_terms")
        s_y = sem("mix_numerators")
        s_yT = sem("mix_outputs")
        s_wpt = sem("output_weights_loaded")
        s_mo = sem("mix_projected")
        s_mor = sem("mix_added")
        s_esrc = sem("sources_loaded")
        s_edst_l = sem("destinations_loaded")
        s_epad = sem("source_padding_set")
        s_dpad = sem("destination_padding_set")
        s_sg = [sem(f"scores_gathered{u}") for u in range(4)]
        s_sh = sem("neighbour_values_moved")
        s_shr = sem("chunk_values_ready")
        s_tr = sem("small_transposes")
        s_mxd = sem("maxima_stored")
        s_edst = sem("padded_edges_stored")
        s_off = sem("tile_offsets_counted")
        s_offp = sem("tile_offsets_summed")
        s_slot = sem("slot_tables_ready")
        s_slg = sem("slot_rows_gathered")
        s_slf = sem("slot_rows_converted")
        s_slt = sem("slot_rows_transposed")
        s_slc = sem("slot_words_placed")
        s_dlst = sem("local_destinations_stored")
        s_accz = sem("accumulator_cleared")
        s_ix = sem("source_numbers")
        s_dl = [sem(f"destination_rows{u}") for u in range(NBUF)]
        s_tick = sem("batch_word_written")
        s_gg = [sem(f"rows_gathered{u}") for u in range(NBUF)]
        s_oht = sem("onehot_rows")
        s_dp = sem("destination_scores")
        s_dv = sem("destination_scores_read")
        s_wl = sem("log_weights")
        s_we = sem("weights")
        s_msg = sem("messages")
        s_agg = sem("messages_summed")
        s_accd = sem("sums_added")
        s_w1 = sem("expert_weights_loaded")
        s_w2 = sem("late_expert_weights_loaded")
        s_hl = [sem(f"h_reloaded{c}") for c in range(LC)]
        s_own = sem("own_messages")
        s_fin2 = sem("final_weights_normalized")
        s_att2 = sem("own_messages_added")
        s_fin = sem("final_exponents")
        s_fine = sem("final_weights")
        s_var2 = sem("variances2_ready")
        s_sd2 = sem("deviations2_ready")
        s_xn2 = sem("tokens_normalized")
        s_gt = sem("tokens_transposed")
        s_gtc = sem("tokens_transposed_in_sbuf")
        s_gs = sem("gate_scores")
        s_gw = sem("gate_weights_loaded")
        s_sel = sem("experts_chosen")
        s_pre = sem("ranks_summed")
        s_e2 = sem("second_gate_exp")
        s_ez = sem("second_gate_gap")
        s_pos = sem("token_positions")
        s_ejp = sem("expert_row_product")
        s_ej = sem("expert_row_ready")
        s_zero = sem("token_slots_cleared")
        s_sc = sem("tokens_scattered")
        s_fx = [sem(f"expert_tokens{u}") for u in range(JB)]
        s_ft = sem("expert_tokens_transposed")
        s_ftc = sem("expert_tokens_in_sbuf")
        s_w1c = sem("first_weights_copied")
        s_f1 = sem("hidden_products")
        s_fhc = sem("hidden_activated")
        s_f2 = sem("expert_products")
        s_f2c = sem("expert_results")
        s_tok = sem("token_rows_ready")
        s_fw = sem("expert_results_weighted")
        s_fy = sem("expert_results_added")
        s_jt = sem("expert_word_written")
        s_res = sem("residuals_stored")
        s_out = sem("outputs_stored")
        s_zrow = sem("zero_row_ready")
        s_zero_v = sem("zeros_ready")
        s_pairb = sem("pair_matrices_ready")
        s_pairT = sem("pair_matrices_transposed")
        s_z16 = sem("half_shift_sums")
        s_z16s = sem("half_shift_squares")
        s_dn = sem("denominators_summed")
        s_den = sem("denominators_read")

        o = 0

        def word(n, *shape, pat=None, **kw):
            nonlocal o
            v = view(S, o, n, pat, **kw)
            o += n
            return v

        cnt, offs, fo, co, nsl, stt, sex, dif, tile0 = (word(32) for _ in range(9))
        tint = word(32).bitcast(I32)
        ts_p, gs_p, sl_p, tsm, tsc = (word(2) for _ in range(5))
        gs_i = word(2).bitcast(I32)
        chv = word(12, pat="p (q h) -> p q h", h=GH)
        cin = word(12, pat="p (q h) -> p q h", h=GH)
        iota_e, cnt_e, ntl, endj, basej = (word(NE) for _ in range(5))
        nti = word(NE).bitcast(I32)
        ej, ejc = word(1), word(1)
        half32 = word(32)
        junk = word(GE // 2)
        rowval = word(1)
        wait_w = word(NT)
        mv2 = word(2 * NT, pat="p (t s) -> p t s", s=2)
        assert o <= 700, o

        o = 800

        def tail(n, pat=None, **kw):
            nonlocal o
            v = view(G, o, n, pat, **kw)
            o += n
            return v

        NH = NT * GH
        has, mlog, slog, mtop, den, f1, f2 = (tail(NH, "p (t h) -> p t h", h=GH) for _ in range(7))
        dlog = tail(2 * NH, "p (w t h) -> p w t h", w=2, h=GH)
        dexp = tail(2 * NH, "p (w t h) -> p w t h", w=2, h=GH)
        hall = view(H, 0, NT * D, "p (t c) -> p t c", t=NT)
        stats2 = view(G, 800, NT * 6, "p (t s) -> p t s", s=6)
        NX = NT * NE
        bgb = tail(NE)
        wg_s = tail(KD * NE, "p (k e) -> p k e", k=KD)
        gsc = tail(NX, "p (t e) -> p t e", e=NE)
        top = tail(NX, "p (t e) -> p t e", e=NE)
        topi = tail(NX, "p (t e) -> p t e", e=NE).bitcast(U32)
        ti = tail(NT * 2, "p (t e) -> p t e", e=2)
        msk = [tail(NX, "p (t e) -> p t e", e=NE) for _ in range(2)]
        msum = tail(NX, "p (t e) -> p t e", e=NE)
        cum = tail(NX, "p (t e) -> p t e", e=NE)
        pos = tail(NX, "p (t e) -> p t e", e=NE)
        mp = tail(NX, "p (t e) -> p t e", e=NE)
        zeros_e = tail(32)
        g2T = [view(tables, u * D, D, "p (k n) -> p k n", k=KD) for u in range(2)]
        assert o <= GW, o
        wait_s = sb("deviations2", [P, NT])[:, :]
        dif2 = sb("dif2", [P, NT, GH])[:, :, :]
        egap = sb("egap", [P, NT])
        eexp = sb("eexp", [P, NT])
        pr = [sb(f"prob{k}", [P, NT]) for k in range(2)]
        posf = [sb(f"posf{k}", [P, NT]) for k in range(2)]
        posi = [sb(f"posi{k}", [P, NT], I32) for k in range(2)]
        b1_s = sb("b1_s", [P, NE * HC])
        xrow = view(C, 0, NT * XR, "p (t c) -> p t c", t=NT)
        xn2 = xrow[:, :, 0:D]
        xfT = [view(C, u * D, D, "p (k n) -> p k n", k=KD) for u in range(2)]
        xf = [view(C, 512 + u * XR, XR) for u in range(JB)]
        HH = HID // 2
        EO = 512 + JB * XR
        w1c = [view(C, EO + u * KD * HH, KD * HH, "p (k n) -> p k n", k=KD) for u in range(2)]
        hT = [view(C, EO + 2048 + u * HID, HID, "p (c n) -> p c n", c=HC) for u in range(2)]
        ys = [view(C, EO + 4096 + u * D, D) for u in range(2)]
        b2_s = view(G, 1000, NE * D, "p (e c) -> p e c", e=NE)

        def bc(t, shape_pairs):
            return ap(t, 0, [list(t.ap[0])] + shape_pairs)

        def over(v, n):
            return ap(v, 0, [list(q) for q in v.ap] + [[0, n]])

        def under(v, n):
            q = [list(z) for z in v.ap]
            return ap(v, 0, [q[0], [0, n]] + q[1:])

        def back(v):
            (ps_, pn), (st, n) = v.ap
            return ap(v, st * (n - 1), [[ps_, pn], [-st, n]])

        def late(t, lag):
            return not isinstance(t, int) or t >= lag

        xt = x[0:(NT - 1) * P, :].rearrange("(t p) c -> p t c", p=P)
        ot = out[0:(NT - 1) * P, :].rearrange("(t p) c -> p t c", p=P)

        block = ctx.enter_context(nc.Block())

        @block.sync
        def _(sp):
            for c in range(XC - 1):
                a, b = c * XW, (c + 1) * XW
                sp.dma_start(res[:, a:b, :], xt[:, a:b, :]).then_inc(s_x[c], 16)
            sp.wait_ge(s_const, 1)
            sp.dma_start(res[0:TAIL, NT - 1, :], x[(NT - 1) * P:N, :]).then_inc(s_x[XC - 1], 16)
            full = E // EP

            def load_edges(t, v, done):
                sp.dma_start(v[0:full, :], t[0:full * EP].rearrange("(p e) -> p e", e=EP)).then_inc(done, 16)
                sp.dma_start(v[full:full + 1, 0:E - full * EP],
                             t[full * EP:E].rearrange("(a e) -> a e", a=1)).then_inc(done, 16)
            sp.wait_ge(s_epad, 1)
            load_edges(src, src_i, s_esrc)
            sp.wait_ge(s_dpad, 1)
            load_edges(dst, dsc_i, s_edst_l)
            sp.dma_start(wcat_s, wcat).then_inc(s_w, 16)
            sp.dma_start(bqk_s, rows(bqkv, P, 2 * D)).then_inc(s_w, 16)
            sp.dma_start(bv_s, rows(bqkv, P, D, 2 * D)).then_inc(s_w, 16)
            sp.dma_start(tempb, rows(temp, P, MH)).then_inc(s_w, 16)
            sp.wait_ge(s_nas, 1)
            sp.dma_start(as_d.rearrange("(t p) h -> p t h", p=P), nas[:, :, 0:GH]).then_inc(s_ast, 16)
            sp.wait_ge(s_esrc, 32)
            sp.dma_start(src_d.rearrange("g w -> (g w)").rearrange("(p e) -> p e", e=EP), src_i).then_inc(s_edst, 16)
            sp.wait_ge(s_edst_l, 32)
            sp.dma_start(dst_d.rearrange("g w -> (g w)").rearrange("(p e) -> p e", e=EP), dsc_i).then_inc(s_edst, 16)

            def store_h(t, u, i):
                sp.wait_ge(s_hrow, t + 1)
                sp.dma_start(h_d.rearrange("(t p) c -> t p c", p=P)[ds(t, 1)].rearrange("o p c -> (o p) c"),
                             hrow[u][:, 0:HROW]).then_inc(s_hst[u], 16)
            skewed(sp.Fori, NT, 2, [(store_h, 0)])
            for g in range(KD):
                sp.wait_ge(s_spl[g], NP // SPW)
                for h in range(QC):
                    for s in range(3):
                        sp.dma_start(stack[s * MD:(s + 1) * MD, g * QC + h, :],
                                     split[s][h * MD:(h + 1) * MD, g, :]).then_inc(s_stk, 16)

            sp.dma_start(wpt_s, wpt).then_inc(s_wpt, 16)
            sp.wait_ge(s_slf, 1)
            for u in range(2):
                sp.dma_start(dl_d[u * P:(u + 1) * P, :], fdlb[:, u, :]).then_inc(s_dlst, 16)
            sp.wait_ge(s_shr, 1)
            sp.dma_start(max_d.rearrange("g w -> (g w)").rearrange("(p e) -> p e", p=P),
                         mx5.rearrange("p e h -> p (e h)")).then_inc(s_mxd, 16)

            sp.wait_ge(s_mor, NT)
            sp.wait_ge(s_dlst, 32)

            def load_batch(b, u, i):
                if late(b, NBUF):
                    sp.wait_ge(s_oht, b - (NBUF - 1))
                d = dl_d[ds(b * SB, SB), :]
                sp.dma_start(dlb[u].rearrange("p (s e) -> p s e", s=SB),
                             bass.AP(d.tensor, d.offset, [[0, P], [GE, SB], [1, GE]])).then_inc(s_dl[u], 16)

            def load_weights(b, u, i):
                if u == 0 and not isinstance(b, int):
                    o = i * PIECE - PIECE
                    sp.dma_start(A[:, ds(o, PIECE)], w12[:, ds(o, PIECE)]).then_inc(s_w1, 16)
            skewed(sp.Fori, NBT, NBUF, [(load_batch, 0), (load_weights, 0)])
            sp.dma_start(A[:, PIECES * PIECE:BO], w12[:, PIECES * PIECE:BO]).then_inc(s_w1, 16)

            sp.wait_ge(s_accd, NS)
            for c in range(LC):
                sp.dma_start(hall[:, c * LW:(c + 1) * LW, :],
                             h_d.rearrange("(t p) c -> p t c", p=P)[:, c * LW:(c + 1) * LW, 0:D]).then_inc(s_hl[c], 16)
            sp.dma_start(bgb, rows(bg, P, NE)).then_inc(s_gw, 16)
            sp.dma_start(wg_s, wg).then_inc(s_gw, 16)
            sp.dma_start(b1_s[:, :], b1).then_inc(s_w2, 16)
            sp.wait_ge(s_att2, LC)
            sp.dma_start(sum_d[0:NP, :].rearrange("(t p) c -> p t c", p=P), res[:, :, :]).then_inc(s_res, 16)
            for e in range(EL):
                o = BO + e * HC * D
                sp.dma_start(arena[:, o:o + HC * D], w12[:, o:o + HC * D]).then_inc(s_w2, 16)
            sp.wait_ge(s_pos, 1)
            sp.dma_start(b2_s, ap(b2, 0, [[0, P], [D, NE], [1, D]])).then_inc(s_w2, 16)

            sp.wait_ge(s_sc, 16 * TOPK * NT)

            def load_tokens(j, u, i):
                if late(j, JB):
                    sp.wait_ge(s_fy, 16 * (j - JB + 1))
                sp.dma_start(xf[u], xs_d.rearrange("(t p) c -> t p c", p=P)[ds(j, 1)].rearrange("o p c -> (o p) c"))\
                  .then_inc(s_fx[u], 16)
            skewed(sp.Fori, NJ, JB, [(load_tokens, 0)])

            sp.wait_ge(s_fy, 16 * NJ)
            sp.dma_start(out, sum_d[0:N, :]).then_inc(s_out, 16)
            sp.wait_ge(s_out, 16)

        @block.gpsimd
        def _(pool):
            st = Steps(pool, g_step)
            pool.memset(res[:, NT - 1, :], 0.0).then_inc(s_const, 1)
            pool.memset(att_s, 0.0).then_inc(s_att, 1)
            pool.memset(identf[:, :], 0.0)
            st(pool.memset(onesf[:, :], 1.0))
            pool.affine_select(out=identf[:, :], in_=identf[:, :], compare_op=ALU.not_equal, fill=1.0,
                               base=0, pattern=[[-1, P]], channel_multiplier=1).then_inc(s_const, 1)
            pool.affine_select(out=lower[:, :], in_=onesf[:, :], compare_op=ALU.is_ge, fill=0.0,
                               base=-1, pattern=[[1, P]], channel_multiplier=-1).then_inc(s_const, 1)
            pool.iota(iota_f[:, :], pattern=[[1, P]], base=0, channel_multiplier=0,
                      allow_small_or_imprecise_dtypes=True).then_inc(s_const, 1)
            pool.iota(iota_p[:, :], pattern=[[0, 1]], base=0, channel_multiplier=1,
                      allow_small_or_imprecise_dtypes=True).then_inc(s_const, 1)
            pool.wait_ge(s_const, 5)
            for s in range(3):
                q = slice(s * MD, (s + 1) * MD)
                st(pool.iota(pd0[q].rearrange("p (c r i) -> p c r i", c=NQC, r=QC),
                             pattern=[[0, NQC], [0, QC], [1, MD]], base=0, channel_multiplier=-1,
                             allow_small_or_imprecise_dtypes=True))
                st(pool.iota(pd1[q].rearrange("p (c r i) -> p c r i", c=NQC, r=QC),
                             pattern=[[QC, NQC], [1, QC], [1, MD]], base=0, channel_multiplier=-1,
                             allow_small_or_imprecise_dtypes=True))
                pool.iota(pde[q], pattern=[[1, MD]], base=0, channel_multiplier=-1,
                          allow_small_or_imprecise_dtypes=True).then_inc(s_pair, 1)
                pool.wait_ge(s_pair, s + 1)

            pool.wait_ge(s_ast, 16)
            pool.wait_ge(s_esrc, 32)
            for j in range(EP):
                if j == EP - 64:
                    pool.wait_ge(s_slot, 1)
                    pool.wait_ge(s_edst, 32)
                    for u in range(2):
                        idx = bass.IndirectOffsetOnAxis(gs_i[:, u:u + 1], 0)
                        pool.indirect_dma_start(sl_src[:, u, :], None, src_d, idx).then_inc(s_slg, 16)
                        pool.indirect_dma_start(sl_dst[:, u, :], None, dst_d, idx).then_inc(s_slg, 16)
                pool.indirect_dma_start(sco[:, j, :], None, as_d, bass.IndirectOffsetOnAxis(src_i[:, j:j + 1], 0))\
                    .then_inc(s_sg[j % 4], 16)

            pool.wait_ge(s_mxd, 16)
            for u in range(2):
                pool.indirect_dma_start(sl_max[:, u].rearrange("p w c -> p (w c)"), None, max_d,
                                        bass.IndirectOffsetOnAxis(gs_i[:, u:u + 1], 0)).then_inc(s_slg, 16)

            for u in range(2):
                pool.wait_ge(s_hst[u], 16 * ((NT + 1 - u) // 2))

            st(pool.memset(ptick[:, :], 0.0))

            def gather(b, u, i):
                if late(b, 1):
                    pool.wait_ge(s_tick, b)
                if late(b, NBUF):
                    pool.wait_ge(s_agg, b * SB - SB * (NBUF - 1))
                pool.wait_ge(s_ix, b + 1)
                pool.tensor_tensor(ptick[:, 1:2], ptick[:, 0:1], ptick[:, 0:1], ALU.add).then_inc(s_tick, 1)
                for k in range(SB * TE):
                    pool.indirect_dma_start(gb[u][:, k, 0:HROW], None, h_d,
                                            bass.IndirectOffsetOnAxis(sidx[u][:, k:k + 1], 0))\
                        .then_inc(s_gg[u], 16)
            skewed(pool.Fori, NBT, NBUF, [(gather, 0)])

            pool.wait_ge(s_fin2, 1)
            for c in range(LC):
                pool.wait_ge(s_hl[c], 16)
                v = hall[:, c * LW:(c + 1) * LW, :].rearrange("p t (h c) -> p t h c", h=GH)
                st(pool.tensor_tensor(v, v, over(f2[:, c * LW:(c + 1) * LW, :], GD), ALU.mult))
                v = hall[:, c * LW:(c + 1) * LW, :]
                pool.tensor_tensor(v, v, res[:, c * LW:(c + 1) * LW, :], ALU.add).then_inc(s_own, 1)

            pool.wait_ge(s_zero, 32)
            pool.wait_ge(s_pos, 1)
            for k in range(TOPK):
                pool.wait_ge(s_tok, k + 1)
                for t in range(NT):
                    n = P if t < NT - 1 else TAIL
                    pool.indirect_dma_start(xs_d, bass.IndirectOffsetOnAxis(posi[k][0:n, t:t + 1], 0),
                                            xrow[0:n, t, :], None).then_inc(s_sc, 16)

            def add_results(j, u, i):
                if late(j, 1):
                    pool.wait_ge(s_jt, j)
                    pool.wait_ge(s_fy, 16 * j)
                pool.wait_ge(s_fw, j + 1)
                pool.tensor_tensor(ptick[:, 1:2], ptick[:, 0:1], ptick[:, 0:1], ALU.add).then_inc(s_jt, 1)
                pool.indirect_dma_start(sum_d, bass.IndirectOffsetOnAxis(xf[u][:, D:D + 1].bitcast(I32), 0),
                                        ys[u % 2], None, compute_op=ALU.add).then_inc(s_fy, 16)
            pool.wait_ge(s_res, 16)
            pool.wait_ge(s_tick, NBT)
            skewed(pool.Fori, NJ, JB, [(add_results, 0)])
            pool.wait_ge(s_fy, 16 * NJ)

        @block.scalar
        def _(act):
            A_ = nc.scalar
            it = [None]

            def turns(n, w, *parts):
                skewed(act.Fori, n, w, parts)

            act.dma_start(wgt_s, wgt).then_inc(s_attd, 16)
            act.wait_ge(s_att, 1)
            for h in range(GH):
                q = GD * (h % 2)
                for w, a in ((0, att_src), (GH, att_dst)):
                    act.dma_start(att_s[q:q + GD, h // 2, w + h:w + h + 1],
                                  a[h:h + 1, :].rearrange("a c -> c a")).then_inc(s_attd, 16)
            act.dma_start(bres_s, rows(gbias, P, D)).then_inc(s_w, 16)
            act.dma_start(bres2, rows(bproj, P, D)).then_inc(s_w, 16)
            act.wait_ge(s_zrow, 2)
            act.dma_start(xs_d.rearrange("(j p) c -> p j c", p=P), ap(zrow, 0, [list(zrow.ap[0]), [0, NJ], [1, XR]]))\
               .then_inc(s_zero, 16)
            act.dma_start(sum_d[NP:NP + P, :], zrow[:, 0:D]).then_inc(s_zero, 16)
            for c in range(XC):
                act.wait_ge(s_var, c + 1)
                A_.activation(rsd[:, XW * c:min(XW * c + XW, NT)], rstd[:, XW * c:min(XW * c + XW, NT)], ACT.Sqrt)\
                  .then_inc(s_sd, 1)

            act.wait_ge(s_wa, 1)
            act.copy(wacc_s, ps[:, 7, 0:KD * AH].rearrange("p (k n) -> p k n", k=KD)).then_inc(s_wac, 1)

            def keep_T(t, u, i):
                act.wait_ge(s_xt, t + 1)
                A_.copy(xT[:, :, ds(t * P, P)], ps[:, u, 0:D].rearrange("p (k n) -> p k n", k=KD)).then_inc(s_xtc, 1)
            turns(NT, XB, (keep_T, 0))
            act.wait_ge(s_nsp, 1)
            A_.copy(nas[:, :, :], ps[:, 5, 0:NT * AH].rearrange("p (t c) -> p t c", c=AH)).then_inc(s_nas, 1)
            act.wait_ge(s_nas, 1)

            def rows_out(t, u, i):
                act.wait_ge(s_prj, t + 1)
                if late(t, 2):
                    act.wait_ge(s_hst[u], 16 * i)
                A_.copy(hrow[u][:, D:HROW], nas[:, ds(t, 1), 0:GH].rearrange("p o c -> p (o c)"))
                A_.copy(hrow[u][:, 0:D], ps[:, 3 * u, 0:D]).then_inc(s_hrow, 1)

            def squares(t, u, i):
                act.wait_ge(s_prv, t + 1)
                if late(t, 2):
                    act.wait_ge(s_ss, t - 1)
                A_.activation(qksq[u], qk[u], ACT.Square).then_inc(s_sq, 1)

            def norms(t, u, i):
                act.wait_ge(s_ss, t + 1)
                if late(t, 2):
                    act.wait_ge(s_qn, t - 1)
                A_.activation(rn[u], ssq[u], ACT.Sqrt).then_inc(s_nrm, 1)

            turns(NT, 2, (rows_out, 0), (squares, 0), (norms, 1))

            def q_out(t, u, i):
                act.wait_ge(s_qt, t + 1)
                A_.copy(qT[:, :, ds(t * P, P)], ps[:, 6 + u, 0:D].rearrange("p (g n) -> p g n", g=KD))\
                  .then_inc(s_qtc, 1)
            turns(NT, 2, (q_out, 0))

            def extend(t, u, i):
                if late(t, 2):
                    act.wait_ge(s_phi, t - 1)
                    act.wait_ge(s_kb, t - 1)
                v = kx[u].rearrange("p (h c) -> p h c", h=MH)
                k = kh[:, ds(t, 1), :].rearrange("p o (h c) -> p (o h) c", c=MD)
                A_.copy(v[:, :, 0:MD], k)
                A_.copy(v[:, :, MD:MD + SQ], k[:, :, 0:SQ]).then_inc(s_kx, 1)

            def beside(t, u, i):
                if late(t, 2):
                    act.wait_ge(s_kv, t - 1)
                act.wait_ge(s_kx, t + 1)
                k = kx[u].rearrange("p (h c) -> p h c", h=MH)[:, :, 0:MD]
                A_.activation(phi[u][:, :, 0:MD], k, ACT.Square)
                A_.copy(kb[u].rearrange("p (h c) -> p h c", c=MD), k)
                A_.copy(vb[u], vv[:, ds(t, 1), :].rearrange("p o c -> p (o c)")).then_inc(s_kb, 1)
            act.wait_ge(s_qn, NT)
            act.wait_ge(s_prv, NT)
            act.wait_ge(s_qt, NT)
            act.wait_ge(s_zero, 32)
            turns(NT, 2, (extend, 0), (beside, 1))

            act.wait_ge(s_kv, NT)
            for n in range(NSP_ + 1):
                for part in range(2):
                    m = n - part
                    if 0 <= m < NSP_:
                        g, col = m // SPC, slice(m % SPC * SPW, (m % SPC + 1) * SPW)
                        if part:
                            act.wait_ge(s_rem, m + 1)
                        A_.copy(split[part][:, g, col], rem[m % 2] if part else qT[:, g, col]).then_inc(s_spa, 1)

            act.wait_ge(s_stk, 16 * 3 * MH)
            act.wait_ge(s_cfd, 1)
            for n in range(RQ * NQC):
                for half in range(2):
                    act.wait_ge(s_z, 2 * n + half + 1)
                    if n >= 2 and not half:
                        act.wait_ge(s_zu, n - 1)
                    A_.activation(zsq[n % 2].rearrange("p (h n) -> p h n", h=QC)[:, 2 * half:2 * half + 2, :],
                                  ps[:, 2 * half:2 * half + 2, 0:BW], ACT.Square).then_inc(s_zs, 1)

            def sources(b, u, i):
                if late(b, NBUF):
                    act.wait_ge(s_gg[u], 16 * SB * TE * i)
                A_.copy(sidx[u], tsrc_f[:, ds(b * (SB * TE), SB * TE)]).then_inc(s_ix, 1)

            def weigh(b, u, i):
                act.wait_ge(s_wl, b + 1)
                A_.activation(gb[u][:, :, D:D + GH], wl[u % 2], ACT.Exp).then_inc(s_we, 1)
            act.wait_ge(s_slc, 2)
            act.wait_ge(s_mo, NT)
            turns(NBT, NBUF, (sources, 0), (weigh, 3))

            act.wait_ge(s_fin, 1)
            A_.activation(dexp, dlog, ACT.Exp).then_inc(s_fine, 1)
            def tokens_T(t, u, i):
                act.wait_ge(s_gt, t + 1)
                if late(t, 2):
                    act.wait_ge(s_gs, t - 1)
                A_.copy(g2T[u], ps[:, 5 + u, 0:D].rearrange("p (k n) -> p k n", k=KD)).then_inc(s_gtc, 1)
            for c in range(LC + 1):
                if c < LC:
                    act.wait_ge(s_var2, c + 1)
                    A_.activation(wait_s[:, c * LW:(c + 1) * LW], wait_w[:, c * LW:(c + 1) * LW], ACT.Sqrt).then_inc(s_sd2, 1)
                if c:
                    for t in range((c - 1) * LW, c * LW):
                        tokens_T(t, t % 2, t // 2)
            act.wait_ge(s_ez, 1)
            A_.activation(eexp[:, :], egap[:, :], ACT.Exp).then_inc(s_e2, 1)

            act.wait_ge(s_w2, 16 * (EL + 2))

            def tokens_T2(j, u, i):
                act.wait_ge(s_ft, j + 1)
                if late(j, 2):
                    act.wait_ge(s_f1, 2 * j - 2)
                A_.copy(xfT[u], ps[:, 7 * u, 0:D].rearrange("p (k n) -> p k n", k=KD)).then_inc(s_ftc, 1)

            def hidden(j, u, i):
                ej = act.value_load(ej_row[0:1, ds(j, 1)], min_val=0, max_val=NE - 1)
                if late(j, 2):
                    act.wait_ge(s_f2, j - 1)
                for n_ in range(2):
                    act.wait_ge(s_f1, 2 * j + (1 + n_))
                    for c in range(n_ * HC // 2, (n_ + 1) * HC // 2):
                        last = A_.activation(hT[u][:, c, :], ps[:, 1 + 2 * u + n_, (c % 4) * P:(c % 4 + 1) * P], ACT.Relu,
                                             bias=b1_s[:, ds(ej * HC + c, 1)])
                last.then_inc(s_fhc, 1)

            act.wait_ge(s_ej, 1)
            turns(NJ, 2, (tokens_T2, 0), (hidden, 1))

        @block.tensor
        def _(pe):
            MM, TR = nc.tensor.matmul, nc.tensor.transpose

            def turns(n, w, *parts):
                skewed(pe.Fori, n, w, parts)

            pe.wait_ge(s_attd, 16 * (1 + AH))
            pe.wait_ge(s_const, 5)
            for k in range(KD):
                for c in range(KD):
                    last = MM(ps[:, 7, k * AH:(k + 1) * AH], wgt_s[:, c, k * P:(k + 1) * P], att_s[:, c, :],
                              start=(c == 0), stop=(c == KD - 1))
            last.then_inc(s_wa, 1)

            def transpose_x(t, u, i):
                pe.wait_ge(s_xn, t + 1)
                if late(t, XB):
                    pe.wait_ge(s_xtc, t - (XB - 1))
                for k in range(KD):
                    last = TR(ps[:, u, k * P:(k + 1) * P], xn[u][:, k * P:(k + 1) * P], identf[:, :])
                last.then_inc(s_xt, 1)

            def node_scores(t):
                pe.wait_ge(s_xtc, t + 1)
                for k in range(KD):
                    last = MM(ps[:, 5, t * AH:(t + 1) * AH], xT[:, k, t * P:(t + 1) * P], wacc_s[:, k, :],
                              start=(k == 0), stop=(k == KD - 1))
                return last
            for t in range(NT + 2):
                if t < NT:
                    transpose_x(t, t % XB, t // XB)
                if t == 2:
                    pe.wait_ge(s_wac, 1)
                if t >= 2:
                    last = node_scores(t - 2)
            last.then_inc(s_nsp, 1)
            pe.wait_ge(s_pairb, 1)
            for c in range(NQC):
                last = TR(psb[:, c * MD:(c + 1) * MD], pairb[0:MD, c, :], identb[0:MD, 0:MD])
            last.then_inc(s_pairT, 1)
            pe.wait_ge(s_w, 16 * 6)
            pe.wait_ge(s_nas, 1)

            def project(t, u, i):
                if late(t, 2):
                    pe.wait_ge(s_hrow, t - 1)
                    pe.wait_ge(s_prv, t - 1)
                for o_, s in ((ps[:, 3 * u, 0:D], slice(0, D)), (ps[:, 3 * u + 1, :], slice(D, 3 * D)),
                              (ps[:, 3 * u + 2, 0:D], slice(3 * D, 4 * D))):
                    for k in range(KD):
                        last = MM(o_, xT[:, k, t * P:(t + 1) * P], wcat_s[:, k, s], start=(k == 0), stop=(k == KD - 1))
                last.then_inc(s_prj, 1)
            for t in range(NT):
                project(t, t % 2, t // 2)

            def q_T(t, u):
                pe.wait_ge(s_qn, t + 1)
                if late(t, 2):
                    pe.wait_ge(s_qtc, t - 1)
                for g in range(KD):
                    last = TR(ps[:, 6 + u, g * P:(g + 1) * P],
                              qn[:, t, g * P:(g + 1) * P], identf[:, :])
                last.then_inc(s_qt, 1)
            pe.wait_ge(s_off, 1)
            MM(ps[:, 5, 256:288], onesf[:, :], cnt, start=True, stop=True).then_inc(s_offp, 1)
            for t in range(NT):
                q_T(t, t % 2)
            pe.wait_ge(s_off, 2)
            for u in range(2):
                last = MM(ps[0:1, 5, u * P:(u + 1) * P], tsc[:, u:u + 1], identf[:, :], start=True, stop=True)
            last.then_inc(s_offp, 1)

            pe.wait_ge(s_prv, NT)
            pe.wait_ge(s_hrow, NT)
            pe.wait_ge(s_zero_v, 1)
            for g in range(4):
                MM(ps[:, g, :], zz[:, 0:P], zz, start=True, stop=False, skip_group_check=True)

            def sums(t, u, n=P, final=False):
                pe.wait_ge(s_phi, t + 1)
                pe.wait_ge(s_kb, t + 1)
                for g in range(KD):
                    k_ = kb[u][0:n, g * P:(g + 1) * P]
                    v_ = vb[u][0:n, g * P:(g + 1) * P]
                    f_ = f16[u][0:n, g * P:(g + 1) * P]
                    for h in range(QC):
                        MM(ps[h * MD:(h + 1) * MD, g, :],
                           v_[:, h * MD:(h + 1) * MD],
                           phi[u][0:n, g * QC + h, :], start=False, stop=final, skip_group_check=True)
                    b = ps[:, 2 + g, :]
                    kw = dict(start=False, stop=final, skip_group_check=True)
                    MM(b[:, 0:P], k_, v_, **kw)
                    MM(b[:, P:2 * P], k_, k_, **kw)
                    MM(b[:, 2 * P:3 * P], f_, v_, **kw)
                    MM(b[:, 3 * P:3 * P + 1], k_, onesf[0:n, 0:1], **kw)
                    last = MM(b[:, 3 * P + 1:3 * P + 2], v_, onesf[0:n, 0:1], **kw)
                last.then_inc(s_kv, 1)
            sums(0, 0)
            sums(1, 1)
            with pe.Fori(1, NT // 2) as i:
                sums(2 * i, 0)
                sums(2 * i + 1, 1)
            sums(NT - 1, 0, TAIL, True)

            pe.wait_ge(s_kvc, 1)
            for c in range(NQC):
                for g in range(KD):
                    last = TR(ps[:, 4 + g, c * P:(c + 1) * P], ftc[g][:, c * P:(c + 1) * P], identf[:, :])
            last.then_inc(s_cft, 1)
            pe.wait_ge(s_cfc, 1)
            for g in range(KD):
                for c in range(NQC):
                    MM(ps[0:MD, 6, g * P:(g + 1) * P], pn[c][:, :], coef[c][g], start=(c == 0), stop=False)
                last = MM(ps[0:MD, 6, g * P:(g + 1) * P], pn16[:, :], cf16[g], start=False, stop=True)
            last.then_inc(s_cf0, 1)

            pe.wait_ge(s_cfd, 1)
            pe.wait_ge(s_stk, 16 * 3 * MH)
            pe.wait_ge(s_wpt, 16)

            def edge_stage(r):
                if r == R_ROWS:
                    pe.wait_ge(s_slf, 1)
                    for u in range(2):
                        if u:
                            pe.wait_ge(s_slc, u)
                        for m in range(2 * TE):
                            k = m % TE
                            last = TR(ps[:, 7, m * P:(m + 1) * P], (fsrc, fdl)[m // TE][:, u, k * P:(k + 1) * P], identf[:, :])
                        last.then_inc(s_slt, 1)
                    pe.wait_ge(s_slc, 2)
                if r in (R_SCAN, R_SCAN + 1):
                    d = r - R_SCAN
                    pe.wait_ge(s_sh, 2 * d + 1)
                    for q in range(3):
                        last = TR(ps[0:GH, 7, q * P:(q + 1) * P], chv[:, q, :], identf[:, :])
                    last.then_inc(s_tr, 1)
                    pe.wait_ge(s_sh, 2 * d + 2)
                    for q in range(2):
                        last = TR(ps[:, 7, 3 * P + q * GH:3 * P + (q + 1) * GH], rowv[0:GH, 6 + q, :], identf[0:GH, 0:GH])
                    last.then_inc(s_tr, 1)
                    pe.wait_ge(s_b7, 1 + d)

            def mix_out(m):
                if m >= 2:
                    pe.wait_ge(s_mor, m - 1)
                for g in range(KD):
                    last = MM(ps[:, 6 + m % 2, 0:D], yT[:, g, m * P:(m + 1) * P], wpt_s[:, g, :],
                              start=(g == 0), stop=(g == KD - 1))
                last.then_inc(s_mo, 1)

            def use(n):
                r, c = n // NQC, n % NQC
                g = r % KD
                pe.wait_ge(s_zs, 2 * n + 2)
                if c == 0 and r >= KD:
                    pe.wait_ge(s_yT, r - KD + 1)
                for h in range(QC):
                    last = MM(ps[h * MD:(h + 1) * MD, 4 + g, 0:BW], coef[c][g][:, h * MD:(h + 1) * MD],
                              zsq[n % 2][:, h * BW:(h + 1) * BW], start=(c == 0), stop=False, skip_group_check=True)
                last.then_inc(s_zu, 1)
                if c < NQC - 1:
                    return
                col = slice(r // KD * BW, (r // KD + 1) * BW)
                MM(ps[:, 4 + g, 0:BW], lin[g], qT[:, g, col], start=False, stop=False, skip_group_check=True)
                pe.wait_ge(s_z16s, r + 1)
                MM(ps[:, 4 + g, 0:BW], cf16[g], z16, start=False, stop=True, skip_group_check=True).then_inc(s_y, 1)

            for n in range(RQ * NQC + 1):
                if n < RQ * NQC:
                    r, c = n // NQC, n % NQC
                    b, g = r // KD, r % KD
                    col = slice(b * BW, (b + 1) * BW)
                    if c == 2:
                        if r:
                            pe.wait_ge(s_den, r)
                        MM(ps[:, 6, 0:BW], gram[g], qT[:, g, col], start=True, stop=True).then_inc(s_t, 1)
                        for h in range(QC):
                            last = MM(ps[h * MD:(h + 1) * MD, 7, 0:BW], pair16[:, :], stack[0:3 * MD, g * QC + h, col],
                                      start=True, stop=True)
                        last.then_inc(s_z16, 1)
                    if c == 3:
                        pe.wait_ge(s_tq, r + 1)
                        MM(ps[:, 6, 0:BW], blocks[:, :], tq[r % 2], start=True, stop=True).then_inc(s_dn, 1)
                    for half in range(2):
                        if n:
                            pe.wait_ge(s_zs, 2 * n - 1 + half)
                        for h in (2 * half, 2 * half + 1):
                            last = MM(ps[:, h, 0:BW], pairb[:, c, :], stack[0:3 * MD, g * QC + h, col],
                                      start=True, stop=True)
                        last.then_inc(s_z, 1)
                if n:
                    use(n - 1)
                if n < RQ * NQC and n % NQC == 1 and n // NQC:
                    r = n // NQC - 1
                    if done_after[r]:
                        pe.wait_ge(s_yT, r + 1)
                    for t in done_after[r]:
                        mix_out(t)
                    if done_after[r]:
                        pe.wait_ge(s_mor, done_after[r][-1] + 1)
                    edge_stage(r)
            pe.wait_ge(s_yT, RQ)
            for t in done_after[RQ - 1]:
                mix_out(t)
            pe.wait_ge(s_mor, NT)
            edge_stage(RQ - 1)

            pe.wait_ge(s_slg, 16 * 6)
            for u in range(2):
                for m in range(TE * (GH + 1)):
                    w, k = m // TE, m % TE
                    last = TR(ps[:, 2 + 3 * u + m // 4, (m % 4) * P:(m % 4 + 1) * P],
                              sl_max[:, u, k * P:(k + 1) * P, w], identf[:, :])
                last.then_inc(s_slt, 1)

            pe.wait_ge(s_accz, 1)

            def scores(b, u, i):
                pe.wait_ge(s_oht, b + 1)
                if late(b, 2):
                    pe.wait_ge(s_dv, b - 1)
                for s in range(SB):
                    t = pe.value_load(ts_row[0:1, ds(b * SB + s, 1)], min_val=0, max_val=NT - 1)
                    for k in range(TE):
                        m = s * TE + k
                        last = MM(ps[:, u % 2, m * 12:(m + 1) * 12], oht[u % 2][:, m * P:(m + 1) * P],
                                  d3[:, ds(t * 12, 12)], start=True, stop=True)
                last.then_inc(s_dp, 1)

            def aggregate(b, u, i):
                pe.wait_ge(s_msg, b + 1)
                if late(b, 2):
                    pe.wait_ge(s_accd, b * SB - SB)
                for s in range(SB):
                    for k in range(TE):
                        m = s * TE + k
                        last = MM(ps[:, 2 + u % 2 * SB + s, 0:ACOL], oh[u % 2][:, m, :], gb[u][:, m, :],
                                  start=(k == 0), stop=(k == TE - 1))
                    last.then_inc(s_agg, 1)

            turns(NBT, NBUF, (scores, 0), (aggregate, 2))

            pe.wait_ge(s_gw, 32)

            def tokens_T(t, u, i):
                pe.wait_ge(s_xn2, t + 1)
                if late(t, 2):
                    pe.wait_ge(s_gtc, t - 1)
                for k in range(KD):
                    last = TR(ps[:, 5 + u, k * P:(k + 1) * P], xn2[:, t, k * P:(k + 1) * P], identf[:, :])
                last.then_inc(s_gt, 1)

            def gate(t, u, i):
                pe.wait_ge(s_gtc, t + 1)
                for k in range(KD):
                    last = MM(ps[:, 7, t * NE:(t + 1) * NE], g2T[u][:, k, :], wg_s[:, k, :], start=(k == 0), stop=(k == KD - 1))
                last.then_inc(s_gs, 1)
            for t in range(NT + 1):
                if t < NT:
                    tokens_T(t, t % 2, t // 2)
                if t:
                    gate(t - 1, (t - 1) % 2, 0)
            pe.wait_ge(s_sel, 1)
            MM(ps[:, 0, 0:NX], lower[:, :], msum.rearrange("p t e -> p (t e)"), start=True, stop=True)
            MM(ps[:, 1, 0:NX], onesf[:, :], msum.rearrange("p t e -> p (t e)"), start=True, stop=True).then_inc(s_pre, 1)
            pe.wait_ge(s_sel, 2)
            MM(ps[0:1, 2, 0:P], ejc, identf[:, :], start=True, stop=True).then_inc(s_ejp, 1)

            pe.wait_ge(s_ej, 1)
            pe.wait_ge(s_w1, 16 * (PIECES + 1))
            pe.wait_ge(s_w2, 16 * (EL + 2))

            def tokens_T2(j, u, i):
                pe.wait_ge(s_fx[u], 16 * i + 16)
                if late(j, 2):
                    pe.wait_ge(s_ftc, j - 1)
                for k in range(KD):
                    last = TR(ps[:, 7 * (u % 2), k * P:(k + 1) * P], xf[u][:, k * P:(k + 1) * P], identf[:, :])
                last.then_inc(s_ft, 1)

            def hidden(j, u, i):
                pe.wait_ge(s_ftc, j + 1)
                if late(j, 2):
                    pe.wait_ge(s_fhc, j - 1)
                for n_ in range(2):
                    pe.wait_ge(s_w1c, 2 * j + (1 + n_))
                    for c in range(HC // 2):
                        for k in range(KD):
                            last = MM(ps[:, 1 + 2 * (u % 2) + n_, c * P:(c + 1) * P], w1c[n_][:, k, c * P:(c + 1) * P],
                                      xfT[u % 2][:, k, :], start=(k == 0), stop=(k == KD - 1))
                    last.then_inc(s_f1, 1)

            def results(j, u, i):
                e = pe.value_load(ej_row[0:1, ds(j, 1)], min_val=0, max_val=NE - 1)
                pe.wait_ge(s_fhc, j + 1)
                if late(j, 2):
                    pe.wait_ge(s_f2c, j - 1)
                for c in range(HC):
                    last = MM(ps[:, 5 + u % 2, 0:D], hT[u % 2][:, c, :],
                              w2_s[:, ds(e, 1), c, :].rearrange("p o n -> p (o n)"), start=(c == 0), stop=(c == HC - 1))
                last.then_inc(s_f2, 1)
            turns(NJ, JB, (tokens_T2, 0), (hidden, 1), (results, 2))

        @block.vector
        def _(dve):
            V = nc.vector
            st = Steps(dve, v_step)

            def turns(n, w, per, *parts):
                skewed(lambda first, end: st.loop(first, end, per), n, w, parts)

            V.memset(src_i, 0).then_inc(s_epad, 1)
            V.memset(dsc_i, PAD_DST).then_inc(s_dpad, 1)
            dve.wait_ge(s_const, 5)
            V.memset(zrow, 0.0).then_inc(s_zrow, 1)
            dve.wait_ge(s_zrow, 1)
            V.tensor_scalar(zrow[:, D:D + 1].bitcast(I32), iota_p[:, :], float(NP), None, ALU.add).then_inc(s_zrow, 1)
            V.memset(ssmin[:, 0:MH], (EPS_N / QSCALE) ** 2)
            V.memset(ssmin[:, MH:2 * MH], EPS_N ** 2)
            st(V.memset(blocks[:, :], 0.0))
            for h in range(QC):
                V.memset(blocks[h * MD:(h + 1) * MD, h * MD:(h + 1) * MD], 1.0)
            for c in range(XC):
                a, b = XW * c, min(XW * c + XW, NT)
                dve.wait_ge(s_x[c], 16)
                for t in range(a, b):
                    ins = V.bn_stats(stats[:, t, :], res[:, t, :])
                st(ins)
                for t in range(a, b):
                    ins = V.bn_aggr(mv[:, t, :], stats[:, t, :])
                st(ins)
                V.tensor_scalar(rstd[:, a:b], mv[:, a:b, 1], EPS_LN, None, ALU.add).then_inc(s_var, 1)
            dve.wait_ge(s_sd, XC)
            st(V.reciprocal(rstd, rsd))

            def normalize(t, u, i):
                if late(t, XB):
                    dve.wait_ge(s_xt, t - (XB - 1))
                tt = ds(t, 1)
                V.tensor_scalar(xn[u], res[:, tt, :].rearrange("p o c -> p (o c)"),
                                mv[:, tt, 0], rstd[:, tt], ALU.subtract, ALU.mult).then_inc(s_xn, 1)

            turns(NT, XB, 0, (normalize, 0))
            dve.wait_ge(s_const, 5)
            V.tensor_copy(identb[:, :], identf[:, :])
            dve.wait_ge(s_pair, 3)
            q = slice(0, 3 * MD)
            V.tensor_scalar(pdm[q], pd1[q], 0.0, None, ALU.is_equal)
            st(V.tensor_scalar(pd0[q], pd0[q], 0.0, None, ALU.is_equal))
            st(V.tensor_tensor(pd0[q], pd0[q], pdm[q], ALU.max))
            st(V.tensor_scalar(pdm[q], pd1[q], float(MD), None, ALU.is_equal))
            V.tensor_tensor(pairb[:, :, :].rearrange("p c f -> p (c f)"), pd0[0:3 * MD], pdm[0:3 * MD], ALU.max)\
                .then_inc(s_pairb, 1)
            dve.wait_ge(s_pairb, 1)
            V.tensor_scalar(pdf[q, 0:MD], pde[q, 0:MD], 0.0, None, ALU.is_equal)
            V.tensor_scalar(pdf[q, MD:2 * MD], pde[q, 0:MD], float(SQ), None, ALU.is_equal)
            st(V.tensor_scalar(pdf[q, 2 * MD:3 * MD], pde[q, 0:MD], float(-SQ), None, ALU.is_equal))
            st(V.tensor_tensor(pdf[q, 0:MD], pdf[q, 0:MD], pdf[q, MD:2 * MD], ALU.max))
            st(V.tensor_tensor(pair16[:, :], pdf[q, 0:MD], pdf[q, 2 * MD:3 * MD], ALU.max))
            for h in range(QC):
                V.tensor_scalar(pn16[h * MD:(h + 1) * MD, :], pair16[0:MD, :], -1.0, None, ALU.mult)
            dve.wait_ge(s_pairT, 1)
            for c in range(NQC):
                ins = V.tensor_scalar(pn[c][:, :], psb[:, c * MD:(c + 1) * MD], -1.0, None, ALU.mult)
            st(ins)
            st(V.tensor_copy(pn[0][0:MD, :], identf[0:MD, 0:MD]))

            dve.wait_ge(s_w, 16 * 6)
            dve.wait_ge(s_xn, NT)
            st(V.tensor_tensor(bres_s, bres_s, bres2, ALU.add))
            st(V.tensor_tensor(res[:, :, :], res[:, :, :], under(bres_s, NT), ALU.add))

            def heads(t, u, i):
                dve.wait_ge(s_prj, t + 1)
                V.tensor_tensor(vv[:, ds(t, 1), :].rearrange("p o c -> p (o c)"), ps[:, 3 * u + 2, 0:D], bv_s, ALU.add)
                if late(t, 2):
                    dve.wait_ge(s_qn, t - 1)
                V.tensor_tensor(qk[u].rearrange("p h c -> p (h c)"), ps[:, 3 * u + 1, :], bqk_s, ALU.add).then_inc(s_prv, 1)

            marks = {}

            def norms_a(t, u, i):
                dve.wait_ge(s_nrm, t + 1)
                marks["reciprocals"] = st.mark(V.reciprocal(rn[u], rn[u]))

            def squares_a(t, u, i):
                dve.wait_ge(s_sq, t + 1)
                marks["sums"] = st.mark(V.tensor_reduce(ssq[u], qksq[u], X, ALU.add))

            def norms_b(t, u, i):
                dve.wait_ge(v_step, marks["reciprocals"])
                marks["factors"] = st.mark(V.tensor_tensor(rn[u][:, 0:MH], rn[u][:, 0:MH], tempb, ALU.mult))

            def squares_b(t, u, i):
                dve.wait_ge(v_step, marks["sums"])
                V.tensor_tensor(ssq[u], ssq[u], ssmin, ALU.max).then_inc(s_ss, 1)

            def unit(t, u, i):
                V.tensor_tensor(kh[:, ds(t, 1), :].rearrange("p o (h c) -> p (o h) c", c=MD), qk[u][:, MH:2 * MH, :],
                                over(rn[u][:, MH:2 * MH], MD), ALU.mult)
                dve.wait_ge(v_step, marks["factors"])
                V.tensor_tensor(qn[:, ds(t, 1), :].rearrange("p o (h c) -> p (o h) c", c=MD), qk[u][:, 0:MH, :],
                                over(rn[u][:, 0:MH], MD), ALU.mult).then_inc(s_qn, 1)

            a, z = slice(0, NT), slice(1, NT + 1)

            def count(t, u, i):
                st(V.tensor_scalar(below, dsc, tile0[:, ds(t, 1)], None, ALU.is_lt, ALU.add, accum_out=cnt[:, ds(t, 1)]))
            V.memset(cnt, 0.0)
            dve.wait_ge(s_edst_l, 32)
            st(V.tensor_copy(dsc, dsc_i))
            st(V.tensor_scalar(tile0, iota_f[:, 0:32], float(P), None, ALU.mult))
            turns(NT, 2, 8, (norms_a, 2), (squares_a, 1), (norms_b, 2), (squares_b, 1), (unit, 2),
                  (heads, 0), (count, 0))
            V.memset(offs, 0.0).then_inc(s_off, 1)
            dve.wait_ge(s_off, 1)
            dve.wait_ge(s_offp, 1)
            st(V.tensor_copy(offs, ps[:, 5, 256:288]))
            st(V.memset(offs[:, NT:NT + 1], float(E)))
            st(V.tensor_copy(tint, offs))
            st(V.tensor_scalar(tint, tint, GE.bit_length() - 1, None, ALU.logical_shift_right))
            st(V.tensor_copy(fo, tint))
            st(V.tensor_scalar(tint, offs, float(GE - 1), None, ALU.add))
            st(V.tensor_scalar(tint, tint, GE.bit_length() - 1, None, ALU.logical_shift_right))
            st(V.tensor_copy(co, tint))
            V.tensor_tensor(nsl[:, a], co[:, z], fo[:, a], ALU.subtract)
            st(V.tensor_tensor(half32[:, a], offs[:, z], offs[:, a], ALU.is_gt))
            st(V.tensor_tensor(nsl[:, a], nsl[:, a], half32[:, a], ALU.mult))
            st(V.memset(half32, 0.0))
            st(V.tensor_tensor_scan(stt[:, a], nsl[:, a], half32[:, a], 0.0, ALU.add, ALU.add))
            st(V.tensor_tensor(sex[:, a], stt[:, a], nsl[:, a], ALU.subtract))
            st(V.tensor_tensor(dif[:, a], fo[:, a], sex[:, a], ALU.subtract))
            V.tensor_copy(sl_p[:, 0:1], iota_p[:, :])
            st(V.tensor_scalar(sl_p[:, 1:2], iota_p[:, :], float(P), None, ALU.add))
            for u in range(2):
                st(V.tensor_scalar(half32[:, a], stt[:, a], sl_p[:, u:u + 1], None, ALU.is_le, ALU.add,
                                   accum_out=ts_p[:, u:u + 1]))
            for u in range(2):
                st(V.scalar_tensor_tensor(half32[:, a], iota_f[:, a], ts_p[:, u:u + 1], dif[:, a],
                                          ALU.is_equal, ALU.mult, accum_out=gs_p[:, u:u + 1]))
            V.tensor_scalar(tsm, ts_p, float(P), None, ALU.mult)
            V.tensor_scalar(tsc, ts_p, float(NT - 1), None, ALU.min).then_inc(s_off, 1)
            st(V.tensor_tensor(gs_p, gs_p, sl_p, ALU.add))
            st(V.tensor_scalar(gs_p, gs_p, float(NG - 1), None, ALU.min))
            V.tensor_copy(gs_i, gs_p).then_inc(s_slot, 1)
            dve.wait_ge(s_offp, 2)
            st(V.tensor_copy(ts_row[:, :], ps[0:1, 5, 0:NSP]))

            dve.wait_ge(s_prj, NT)
            dve.wait_ge(s_nrm, NT)
            dve.wait_ge(s_qn, NT)
            dve.wait_ge(s_hst[0], 16 * ((NT + 1) // 2))
            dve.wait_ge(s_hst[1], 16 * (NT // 2))
            V.memset(zz, 0.0).then_inc(s_zero_v, 1)
            V.memset(fadd[:, 0:1], 0.0)
            V.memset(badd[:, EP - 1:EP], 0.0)
            V.tensor_copy(chv[:, 1, :], ap(dsc, EP - 1, [list(dsc.ap[0]), [0, GH]]))
            V.tensor_copy(chv[:, 2, :], ap(dsc, 0, [list(dsc.ap[0]), [0, GH]]))
            st(V.tensor_tensor(fadd[:, 1:EP], dsc[:, 1:EP], dsc[:, 0:EP - 1], ALU.is_equal))
            st(V.tensor_scalar(fadd[:, 1:EP], fadd[:, 1:EP], -1.0, BIG, ALU.add, ALU.mult))
            st(V.tensor_copy(badd[:, 0:EP - 1], fadd[:, 1:EP]))


            def pairs(t, u, i):
                dve.wait_ge(s_kx, t + 1)
                if late(t, 2):
                    dve.wait_ge(s_kv, t - 1)
                k0 = ap(kx[u], 0, [list(kx[u].ap[0]), [48, MH], [0, SQ - 1], [1, MD]])
                k1 = ap(kx[u], 1, [list(kx[u].ap[0]), [48, MH], [1, SQ - 1], [1, MD]])
                kk = kx[u].rearrange("p (h c) -> p h c", h=MH)
                V.tensor_tensor(f16[u].rearrange("p (h c) -> p h c", h=MH), kk[:, :, 0:MD], kk[:, :, SQ:SQ + MD], ALU.mult)
                V.tensor_tensor(phi[u].rearrange("p h (r i) -> p h r i", i=MD)[:, :, 1:SQ], k0, k1, ALU.mult).then_inc(s_phi, 1)
            turns(NT, 2, 0, (pairs, 0))

            dve.wait_ge(s_kv, NT)
            for g in range(KD):
                b = ps[:, 2 + g, :]
                V.tensor_scalar(ftc[g], ps[:, g, :], 0.5, None, ALU.mult)
                V.tensor_tensor(lin[g], b[:, 0:P], blocks[:, :], ALU.mult)
                V.scalar_tensor_tensor(gram[g], b[:, P:2 * P], 0.5, blocks[:, :], ALU.mult, ALU.mult)
                V.scalar_tensor_tensor(cf16[g], b[:, 2 * P:3 * P], 0.25, blocks[:, :], ALU.mult, ALU.mult)
                V.tensor_copy(sk[g][:, :], b[:, 3 * P:3 * P + 1])
                ins = V.tensor_copy(sv[g][:, :], b[:, 3 * P + 1:3 * P + 2])
            ins.then_inc(s_kvc, 1)

            for m in range(NSP_ + 1):
                if m < NSP_:
                    g, col = m // SPC, slice(m % SPC * SPW, (m % SPC + 1) * SPW)
                    dve.wait_ge(s_spa, max(2 * m, 1))
                    if m >= 2:
                        dve.wait_ge(s_spl[(m - 2) // SPC], (m - 2) % SPC + 1)
                    V.tensor_tensor(rem[m % 2], qT[:, g, col], split[0][:, g, col], ALU.subtract).then_inc(s_rem, 1)
                if m:
                    l = m - 1
                    g, col = l // SPC, slice(l % SPC * SPW, (l % SPC + 1) * SPW)
                    dve.wait_ge(s_spa, min(2 * l + 3, 2 * NSP_))
                    V.tensor_tensor(split[2][:, g, col], rem[l % 2], split[1][:, g, col], ALU.subtract)\
                        .then_inc(s_spl[g], 1)
            dve.wait_ge(s_spl[KD - 1], SPC)

            dve.wait_ge(s_cft, 1)
            for g in range(KD):
                for c in range(NQC):
                    ins = V.tensor_copy(coef[c][g], ps[:, 4 + g, c * P:(c + 1) * P])
            ins.then_inc(s_cfc, 1)
            dve.wait_ge(s_cf0, 1)
            for g in range(KD):
                ins = V.tensor_copy(coef[0][g][0:MD, :], ps[0:MD, 6, g * P:(g + 1) * P])
            ins.then_inc(s_cfd, 1)

            rv = rowv[0:GH]
            R0, R1, R2, R3, R4, R5, R6, R7 = (rv[:, q, :] for q in range(8))
            n1 = P - 1

            def edge_stage(r):
                if r == R_ROWS:
                    dve.wait_ge(s_slg, 16 * 4)
                    V.tensor_copy(fsrc, sl_src)
                    for u in range(2):
                        ins = V.tensor_scalar(fdl[:, u, :], sl_dst[:, u, :], tsm[:, u:u + 1], None, ALU.subtract)
                    st(ins)
                    V.tensor_copy(fdlb, fdl).then_inc(s_slf, 1)
                    for u in range(2):
                        n = min(P, NS - u * P)
                        dve.wait_ge(s_slt, u + 1)
                        v = ps[:, 7, :].rearrange("p (w k s) -> p w k s", w=2, k=TE)
                        V.tensor_copy(tsrc[:, u * P:u * P + n].rearrange("p s k -> p k s"), v[:, 0, :, 0:n])
                        V.tensor_copy(tdl[:, u * P:u * P + n].rearrange("p s k -> p k s"), v[:, 1, :, 0:n]).then_inc(s_slc, 1)
                if r == R_SCAN:
                    for j in range(4):
                        dve.wait_ge(s_sg[j], 16 * (EP // 4))
                    for h in range(GH):
                        ins = V.tensor_tensor_scan(fwd[:, :, h], fadd, sco[:, :, h], -BIG, ALU.add, ALU.max)
                    st(ins)
                    V.tensor_copy(chv[:, 0, :], fwd[:, EP - 1, :]).then_inc(s_sh, 1)
                    dve.wait_ge(s_tr, 1)
                    st(V.tensor_copy(rv[:, 0:3, :], ps[0:GH, 7, 0:3 * P].rearrange("p (q n) -> p q n", q=3)))
                    V.memset(R3[:, 0:1], -BIG)
                    V.memset(R6[:, 0:1], -BIG)
                    V.memset(R7, 0.0)
                    V.tensor_tensor(R3[:, 1:P], R1[:, 1:P], R1[:, 0:n1], ALU.is_equal)
                    st(V.tensor_tensor(R5[:, 1:P], R2[:, 1:P], R1[:, 0:n1], ALU.is_equal))
                    V.tensor_scalar(R5[:, 1:P], R5[:, 1:P], -1.0, BIG, ALU.add, ALU.mult)
                    st(V.tensor_scalar(R3[:, 1:P], R3[:, 1:P], -1.0, BIG, ALU.add, ALU.mult))
                    st(V.tensor_tensor_scan(R4, R3, R0, -BIG, ALU.add, ALU.max))
                    V.tensor_tensor(R6[:, 1:P], R5[:, 1:P], R4[:, 0:n1], ALU.add).then_inc(s_sh, 1)
                    dve.wait_ge(s_tr, 2)
                    V.tensor_copy(cin[:, 0:2, :], ps[:, 7, 3 * P:3 * P + 2 * GH].rearrange("p (q h) -> p q h", q=2))\
                        .then_inc(s_b7, 1)
                    dve.wait_ge(s_b7, 1)
                if r == R_SCAN + 1:
                    for h in range(GH):
                        ins = V.tensor_tensor_scan(fwd[:, :, h], fadd, sco[:, :, h], cin[:, 0, h:h + 1], ALU.add, ALU.max)
                    st(ins)
                    for h in range(GH):
                        ins = V.tensor_tensor_scan(back(mx5[:, :, h]), back(badd), back(fwd[:, :, h]), -BIG, ALU.add, ALU.max)
                    st(ins)
                    V.tensor_copy(chv[:, 0, :], mx5[:, 0, 0:GH]).then_inc(s_sh, 1)
                    dve.wait_ge(s_tr, 3)
                    st(V.tensor_copy(R0, ps[0:GH, 7, 0:P]))
                    V.memset(R3[:, n1:P], -BIG)
                    V.memset(R6[:, n1:P], -BIG)
                    V.tensor_tensor(R3[:, 0:n1], R2[:, 0:n1], R2[:, 1:P], ALU.is_equal)
                    st(V.tensor_tensor(R7[:, 0:n1], R1[:, 0:n1], R2[:, 1:P], ALU.is_equal))
                    V.tensor_scalar(R5[:, 0:n1], R7[:, 0:n1], -1.0, BIG, ALU.add, ALU.mult)
                    st(V.tensor_scalar(R3[:, 0:n1], R3[:, 0:n1], -1.0, BIG, ALU.add, ALU.mult))
                    st(V.tensor_tensor_scan(back(R4), back(R3), back(R0), -BIG, ALU.add, ALU.max))
                    V.tensor_tensor(R6[:, 0:n1], R5[:, 0:n1], R4[:, 1:P], ALU.add).then_inc(s_sh, 1)
                    dve.wait_ge(s_tr, 4)
                    V.tensor_copy(cin[:, 0:2, :], ps[:, 7, 3 * P:3 * P + 2 * GH].rearrange("p (q h) -> p q h", q=2))\
                        .then_inc(s_b7, 1)
                    dve.wait_ge(s_b7, 2)
                    for h in range(GH):
                        V.tensor_tensor_scan(back(mx5[:, :, h]), back(badd), back(fwd[:, :, h]), cin[:, 0, h:h + 1],
                                             ALU.add, ALU.max)
                    V.tensor_scalar(mx5[:, 0:EP - 1, GH], badd[:, 0:EP - 1], -1.0, None, ALU.is_lt)
                    V.tensor_scalar(mx5[:, EP - 1, GH:GH + 1], cin[:, 1, 0:1], -1.0, 1.0, ALU.mult, ALU.add).then_inc(s_shr, 1)

            dve.wait_ge(s_stk, 16 * 3 * MH)
            for b in range(NB):
                col = slice(b * BW, (b + 1) * BW)
                for g in range(KD):
                    r = b * KD + g
                    dve.wait_ge(s_z16, r + 1)
                    V.tensor_copy(zc, ps[:, 7, 0:BW]).then_inc(s_zc, 1)
                    dve.wait_ge(s_zc, r + 1)
                    V.tensor_tensor(z16, zc, zc, ALU.mult).then_inc(s_z16s, 1)
                    dve.wait_ge(s_t, r + 1)
                    if r >= 2:
                        dve.wait_ge(s_dn, r - 1)
                    V.scalar_tensor_tensor(tq[r % 2], ps[:, 6, 0:BW], sk[g][:, 0:1], qT[:, g, col], ALU.add, ALU.mult)\
                        .then_inc(s_tq, 1)
                    dve.wait_ge(s_dn, r + 1)
                    V.tensor_scalar(rden[r % 2], ps[:, 6, 0:BW], float(N), None, ALU.add).then_inc(s_den, 1)
                    dve.wait_ge(s_den, r + 1)
                    st(V.reciprocal(rden[r % 2], rden[r % 2]))
                    dve.wait_ge(s_y, r + 1)
                    V.scalar_tensor_tensor(yT[:, g, col], ps[:, 4 + g, 0:BW], sv[g][:, 0:1], rden[r % 2],
                                           ALU.add, ALU.mult).then_inc(s_yT, 1)
                    for t in done_after[r]:
                        dve.wait_ge(s_mo, t + 1)
                        V.tensor_tensor(res[:, t, :], res[:, t, :], ps[:, 6 + t % 2, 0:D], ALU.add).then_inc(s_mor, 1)
                    edge_stage(r)

            for u in range(2):
                n = min(P, NS - u * P)
                dve.wait_ge(s_slt, u + 3)
                V.tensor_copy(tmax[:, u * P:u * P + n].rearrange("p s k c -> p c k s"),
                              ap(psf, (2 + 3 * u) * 512, [list(psf.ap[0]), [TE * P, GH + 1], [P, TE], [1, n]])).then_inc(s_slc, 1)
            d3v = d3[:, :].rearrange("p (t h q) -> p t h q", h=GH, q=3)
            a_d = nas[:, :, GH:AH]
            r1 = dif2
            st(V.tensor_copy(d3v[:, :, :, 0], a_d))
            st(V.tensor_tensor(r1, a_d, d3v[:, :, :, 0], ALU.subtract))
            st(V.tensor_copy(d3v[:, :, :, 1], r1))
            st(V.tensor_tensor(r1, r1, d3v[:, :, :, 1], ALU.subtract))
            st(V.tensor_copy(d3v[:, :, :, 2], r1))
            dve.wait_ge(s_dlst, 32)
            V.memset(acc[:, :], 0.0).then_inc(s_accz, 1)
            dve.wait_ge(s_accz, 1)

            def onehots(b, u, i):
                v = u % 2
                dve.wait_ge(s_dl[u], 16 * i + 16)
                if late(b, 2):
                    dve.wait_ge(s_dp, b - 1)
                V.tensor_scalar(oht[v], dlb[u], iota_p[:, 0:1], None, ALU.is_equal).then_inc(s_oht, 1)

            def masks(b, u, i):
                if late(b, 2):
                    dve.wait_ge(s_agg, b * SB - SB)
                V.tensor_tensor(oh[u % 2], under(iota_f[:, :], SB * TE), over(tdl_f[:, ds(b * (SB * TE), SB * TE)], P),
                                ALU.is_equal)

            def weights(b, u, i):
                v = u % 2
                dve.wait_ge(s_dp, b + 1)
                tm_ = tmax_f[:, ds(b * (SB * TE), SB * TE), :]
                st(V.tensor_reduce(dv[v].rearrange("p k h -> p (k h)"),
                                   ps[:, v, 0:SB * TE * 12].rearrange("p (k q) -> p k q", q=3), X, ALU.add))
                V.tensor_tensor(a2[v][:, 1], dv[v], tm_[:, :, 0:GH], ALU.add).then_inc(s_dv, 1)
                dve.wait_ge(s_gg[u], 16 * SB * TE * i + 16 * SB * TE)
                st(V.tensor_tensor(a2[v][:, 0], dv[v], gb[u][:, :, D:D + GH], ALU.add))
                leaky = V.scalar_tensor_tensor(lk[v].rearrange("p w k h -> p (w k h)"),
                                               a2[v].rearrange("p w k h -> p (w k h)"), 0.2,
                                               a2[v].rearrange("p w k h -> p (w k h)"), ALU.mult, ALU.max)
                lky = st.mark(leaky)
                V.tensor_tensor(gb[u][:, :, D + GH:ACOL], tm_[:, :, 0:GH], over(tm_[:, :, GH], GH), ALU.mult)
                dve.wait_ge(v_step, lky)
                if late(b, 2):
                    dve.wait_ge(s_we, b - 1)
                V.tensor_tensor(wl[v], lk[v][:, 0], lk[v][:, 1], ALU.subtract).then_inc(s_wl, 1)

            def messages(b, u, i):
                dve.wait_ge(s_we, b + 1)
                m = gb[u][:, :, 0:D].rearrange("p k (h c) -> p k h c", c=GD)
                V.tensor_tensor(m, m, over(gb[u][:, :, D:D + GH], GD), ALU.mult).then_inc(s_msg, 1)

            def accumulate(b, u, i):
                for s in range(SB):
                    t = dve.value_load(ts_row[0:1, ds(b * SB + s, 1)], min_val=0, max_val=NT - 1)
                    dve.wait_ge(s_agg, b * SB + (s + 1))
                    if s or late(b, 1):
                        dve.wait_ge(s_accd, b * SB + s)
                    a = acc[:, ds(t * ACOL, ACOL)]
                    V.tensor_tensor(a, a, ps[:, 2 + u % 2 * SB + s, 0:ACOL], ALU.add).then_inc(s_accd, 1)
            turns(NBT, NBUF, 3 * NBUF, (onehots, 0), (weights, 1), (masks, 2), (messages, 2), (accumulate, 3))

            dve.wait_ge(s_accd, NS)
            dve.wait_ge(s_agg, NS)
            accv = acc[:, :].rearrange("p (t c) -> p t c", c=ACOL)
            eden, emax = accv[:, :, D:D + GH], accv[:, :, D + GH:ACOL]
            a_s = nas[:, :, 0:GH]
            V.tensor_scalar(has, eden, 0.0, None, ALU.is_gt)
            V.tensor_tensor(mlog, emax, a_d, ALU.add)
            st(V.tensor_tensor(slog, a_s, a_d, ALU.add))
            V.scalar_tensor_tensor(f1, mlog, 0.2, mlog, ALU.mult, ALU.max)
            V.scalar_tensor_tensor(f2, slog, 0.2, slog, ALU.mult, ALU.max)
            st(V.tensor_scalar(has, has, -1.0, BIG, ALU.add, ALU.mult))
            st(V.tensor_tensor(f1, f1, has, ALU.add))
            st(V.tensor_tensor(mtop, f1, f2, ALU.max))
            V.tensor_tensor(dlog[:, 0], f1, mtop, ALU.subtract)
            V.tensor_tensor(dlog[:, 1], f2, mtop, ALU.subtract).then_inc(s_fin, 1)
            dve.wait_ge(s_fine, 1)
            st(V.tensor_tensor(den, eden, dexp[:, 0], ALU.mult))
            st(V.tensor_tensor(den, den, dexp[:, 1], ALU.add))
            st(V.reciprocal(den, den))
            V.tensor_tensor(f1, dexp[:, 0], den, ALU.mult)
            V.tensor_tensor(f2, dexp[:, 1], den, ALU.mult).then_inc(s_fin2, 1)
            dve.wait_ge(s_fin2, 1)

            for c in range(LC + 1):
                if c < LC:
                    q = slice(c * LW, (c + 1) * LW)
                    v = accv[:, q, 0:D].rearrange("p t (h c) -> p t h c", h=GH)
                    st(V.tensor_tensor(v, v, over(f1[:, q, :], GD), ALU.mult))
                    dve.wait_ge(s_own, c + 1)
                    V.tensor_tensor(res[:, q, :], accv[:, q, 0:D], hall[:, q, :], ALU.add).then_inc(s_att2, 1)
                    dve.wait_ge(s_att2, c + 1)
                    for t in range(c * LW, (c + 1) * LW):
                        ins = V.bn_stats(stats2[:, t, :], res[:, t, :])
                    st(ins)
                    for t in range(c * LW, (c + 1) * LW):
                        ins = V.bn_aggr(mv2[:, t, :], stats2[:, t, :])
                    st(ins)
                    V.tensor_scalar(wait_w[:, q], mv2[:, q, 1], EPS_LN, None, ALU.add).then_inc(s_var2, 1)
                if c:
                    q = slice((c - 1) * LW, c * LW)
                    dve.wait_ge(s_sd2, c)
                    st(V.reciprocal(wait_w[:, q], wait_s[:, q]))
                    for t in range((c - 1) * LW, c * LW):
                        V.tensor_scalar(xn2[:, t, :], res[:, t, :], mv2[:, t, 0:1], wait_w[:, t:t + 1],
                                        ALU.subtract, ALU.mult).then_inc(s_xn2, 1)

            V.tensor_copy(iota_e, iota_f[:, 0:NE])
            st(V.memset(zeros_e, 0.0))
            V.tensor_scalar(rowval, iota_p[:, :], float(TAIL), None, ALU.is_lt)
            dve.wait_ge(s_gs, NT)
            dve.wait_ge(s_gw, 32)
            st(V.tensor_tensor(gsc, ps[:, 7, 0:NX].rearrange("p (t e) -> p t e", e=NE), under(bgb, NT), ALU.add))
            for t in range(NT):
                ins = V.max(top[:, t, :], gsc[:, t, :])
            st(ins)
            for t in range(NT):
                ins = V.max_index(topi[:, t, :], top[:, t, :], gsc[:, t, :])
            st(ins)
            V.tensor_tensor(egap[:, :], top[:, :, 1], top[:, :, 0], ALU.subtract).then_inc(s_ez, 1)
            st(V.tensor_copy(ti, topi[:, :, 0:2]))
            for k in range(TOPK):
                ins = V.tensor_tensor(msk[k], under(iota_e, NT), over(ti[:, :, k], NE), ALU.is_equal)
            st(ins)
            for k in range(TOPK):
                ins = V.tensor_scalar(msk[k][:, NT - 1, :], msk[k][:, NT - 1, :], rowval[:, 0:1], None, ALU.mult)
            st(ins)
            V.tensor_tensor(msum, msk[0], msk[1], ALU.add).then_inc(s_sel, 1)
            dve.wait_ge(s_e2, 1)
            st(V.tensor_scalar(pr[0][:, :], eexp[:, :], 1.0, None, ALU.add))
            st(V.reciprocal(pr[0][:, :], pr[0][:, :]))
            st(V.tensor_tensor(pr[1][:, :], eexp[:, :], pr[0][:, :], ALU.mult))
            V.tensor_scalar(xrow[:, :, D].bitcast(I32), tile0[:, 0:NT], iota_p[:, 0:1], None, ALU.add)
            V.tensor_copy(xrow[:, :, D + 1], pr[0][:, :]).then_inc(s_tok, 1)
            dve.wait_ge(s_pre, 1)
            tot = ps[:, 1, 0:NX].rearrange("p (t e) -> p t e", e=NE)
            for e in range(NE):
                ins = V.tensor_tensor_scan(cum[:, :, e], tot[:, :, e], zeros_e[:, 0:NT], 0.0, ALU.add, ALU.add)
            st(ins)
            st(V.tensor_tensor(pos, cum, tot, ALU.subtract))
            st(V.tensor_tensor(pos, pos, ps[:, 0, 0:NX].rearrange("p (t e) -> p t e", e=NE), ALU.add))
            st(V.tensor_scalar(nti, cum[:, NT - 1, :], float(P - 1), None, ALU.add))
            st(V.tensor_scalar(nti, nti, P.bit_length() - 1, None, ALU.logical_shift_right))
            st(V.tensor_copy(ntl, nti))
            st(V.tensor_tensor_scan(endj, ntl, zeros_e[:, 0:NE], 0.0, ALU.add, ALU.add))
            st(V.tensor_tensor(basej, endj, ntl, ALU.subtract))
            st(V.tensor_scalar(basej, basej, float(P), None, ALU.mult))
            st(V.tensor_tensor(pos, pos, under(basej, NT), ALU.add))
            st(V.tensor_scalar(cnt_e, endj, iota_p[:, 0:1], None, ALU.is_le, ALU.add, accum_out=ej))
            V.tensor_scalar(ejc, ej, float(NE - 1), None, ALU.min).then_inc(s_sel, 1)
            for k in range(TOPK):
                st(V.tensor_tensor(mp, msk[k], pos, ALU.mult))
                st(V.tensor_reduce(posf[k][:, :], mp, X, ALU.add))
                ins = V.tensor_copy(posi[k][:, :], posf[k][:, :])
            ins.then_inc(s_pos, 1)
            dve.wait_ge(s_ejp, 1)
            V.tensor_copy(ej_row[:, :], ps[0:1, 2, 0:P]).then_inc(s_ej, 1)
            dve.wait_ge(s_sc, 16 * NT)
            V.tensor_copy(xrow[:, :, D + 1], pr[1][:, :]).then_inc(s_tok, 1)

            dve.wait_ge(s_w2, 16 * (EL + 2))
            dve.wait_ge(s_sc, 16 * TOPK * NT)

            def first_weights(j, u, i):
                e = dve.value_load(ej_row[0:1, ds(j, 1)], min_val=0, max_val=NE - 1)
                for n_ in range(2):
                    if late(j, 1):
                        dve.wait_ge(s_f1, 2 * j - (1 - n_))
                    V.tensor_copy(w1c[n_], w1_s[:, ds(e, 1), :, n_ * HH:(n_ + 1) * HH].rearrange("p o k n -> p (o k) n"))\
                        .then_inc(s_w1c, 1)

            def results(j, u, i):
                v = u % 2
                e = dve.value_load(ej_row[0:1, ds(j, 1)], min_val=0, max_val=NE - 1)
                dve.wait_ge(s_f2, j + 1)
                if late(j, 2):
                    dve.wait_ge(s_fy, 16 * (j - 1))
                V.tensor_tensor(ys[v], ps[:, 5 + v, 0:D], b2_s[:, ds(e, 1), :].rearrange("p o c -> p (o c)"), ALU.add)\
                    .then_inc(s_f2c, 1)
                dve.wait_ge(s_f2c, j + 1)
                dve.wait_ge(s_fx[u], 16 * i + 16)
                V.tensor_scalar(ys[v], ys[v], xf[u][:, D + 1:D + 2], None, ALU.mult).then_inc(s_fw, 1)
            dve.wait_ge(s_ej, 1)
            dve.wait_ge(s_w1, 16 * (PIECES + 1))
            turns(NJ, JB, 0, (first_weights, 0), (results, 2))


def kernel(**inputs):
    import numpy as np
    import concourse.bacc as bacc
    from concourse.bass_utils import run_bass_kernel_spmd

    get = {k: np.asarray(v) for k, v in inputs.items()}

    def chunks(w):
        return w.reshape(-1, 128, w.shape[-1]).transpose(1, 0, 2)

    w1 = get["L0_ffn_W1"].transpose(0, 2, 1).reshape(NE, KD, P, HID).transpose(2, 0, 1, 3)
    w2 = get["L0_ffn_W2"].transpose(0, 2, 1).reshape(NE, HC, P, D).transpose(2, 0, 1, 3)
    arrays = {
        "x": get["x"], "src": get["src"], "dst": get["dst"],
        "wcat": chunks(np.concatenate([get["L0_gnn_W"], get["L0_mix_Wqkv"].T], axis=1)),
        "wgt": chunks(get["L0_gnn_W"].T),
        "att_src": get["L0_gnn_att_src"], "att_dst": get["L0_gnn_att_dst"], "gbias": get["L0_gnn_bias"],
        "bqkv": get["L0_mix_bqkv"], "wpt": chunks(get["L0_mix_Wproj"].T), "bproj": get["L0_mix_bproj"],
        "temp": get["L0_mix_temperature"].reshape(MH),
        "wg": chunks(get["L0_ffn_Wg"].T), "bg": get["L0_ffn_bg"],
        "w12": np.concatenate([w1.reshape(P, -1), w2.reshape(P, -1)], axis=1), "b1": get["L0_ffn_b1"].reshape(NE, HC, P).transpose(2, 0, 1).reshape(P, NE * HC),
        "b2": get["L0_ffn_b2"],
    }
    nc = bacc.Bacc("TRN2", target_bir_lowering=False, num_devices=1)
    args, feed = [], {}
    for name, a in arrays.items():
        a = np.ascontiguousarray(a)
        feed[f"in_{name}"] = a
        args.append(nc.dram_tensor(f"in_{name}", a.shape, mybir.dt.from_np(a.dtype), kind="ExternalInput").ap())
    out = nc.dram_tensor("out", (N, D), F32, kind="ExternalOutput").ap()
    gps_layer(nc, *args, out)
    r = run_bass_kernel_spmd(nc, [feed], core_ids=[0])
    return r.results[0]["out"]
```
